# Optimizing a Trainium2 kernel written in Bass

```python
import numpy as np
import jax
import jax.numpy as jnp

def _softmax(x, axis=-1):
    return jax.nn.softmax(x, axis=axis)

def _gelu(x):
    return jax.nn.gelu(x, approximate=True)

def _silu(x):
    return jax.nn.silu(x)

def _sigmoid(x):
    return jax.nn.sigmoid(x)

def _layernorm(x, axis=-1, eps=1e-05):
    m = jnp.mean(x, axis=axis, keepdims=True)
    v = jnp.var(x, axis=axis, keepdims=True)
    return (x - m) / jnp.sqrt(v + eps)

def _scatter_add(tgt, idx, src, axis=0):
    return tgt.at[idx].add(src)

def _segment_sum(src, seg, n):
    return jax.ops.segment_sum(src, seg, n)
kernel_name = 'mk_perceiver_d2_seqx_r4_e1a62c'

def setup_inputs(seed: int=0):
    np.random.seed(seed)
    _w = jnp.asarray

    def _rec_inputs():
        import jax
        import jax.numpy as jnp
        _rk = jax.random.key(seed)
        x = -0.0002928 + 1 * jax.random.normal(jax.random.fold_in(_rk, 1), (32, 32, 512), jnp.float32)
        _lenS = 32 - jax.random.randint(jax.random.fold_in(_rk, 7), (32,), 0, max(1, 32 // 4) + 1, jnp.int32)
        _lenS2 = 257 - jax.random.randint(jax.random.fold_in(_rk, 8), (32,), 0, max(1, 257 // 4) + 1, jnp.int32)
        _ctx_512P = jax.random.normal(jax.random.fold_in(_rk, 11), (32, 16, 128), jnp.float32)
        _ctx_512c = jax.random.dirichlet(jax.random.fold_in(_rk, 511), 0.3 * jnp.ones((16,), jnp.float32), (32, 257))
        _ctx_512t = jnp.einsum('bsk,bkd->bsd', _ctx_512c, _ctx_512P)
        _ctx_512t = _ctx_512t * jax.lax.rsqrt(jnp.mean(jnp.square(_ctx_512t)) + 1e-12) * 0.953939
        ctx_512 = 0.000227908 + 0.99994 * (_ctx_512t + 0.3 * jax.random.normal(jax.random.fold_in(_rk, 611), (32, 257, 128), jnp.float32))
        return (x, ctx_512)
    x, ctx_512 = _rec_inputs()

    def _L0_xattn_setup():
        import jax, jax.numpy as jnp
        import numpy as np
        B, S, L = (2, 256, 256)
        DIM_Q, H, K, D_C, D_CQ, R = (512, 16, 128, 128, 384, 64)

        def _rope_tables(seq_len, dim, dtype):
            inv_freq = 1.0 / 10000.0 ** (jnp.arange(0, dim, 2, dtype=dtype) / dim)
            t = jnp.arange(seq_len, dtype=dtype)
            freqs = t[:, None] * inv_freq[None, :]
            sin = jnp.repeat(jnp.sin(freqs), 2, axis=-1)
            cos = jnp.repeat(jnp.cos(freqs), 2, axis=-1)
            return (sin, cos)

        def _rotate_half(x):
            h = x.shape[-1] // 2
            return jnp.concatenate([-x[..., h:], x[..., :h]], axis=-1)
        key = jax.random.key(seed)
        ks = jax.random.split(key, 8)
        s_in = 1.0 / np.sqrt(DIM_Q)
        s_k = 1.0 / np.sqrt(K)
        s_cq = 1.0 / np.sqrt(D_CQ)
        s_c = 1.0 / np.sqrt(D_C)
        return {'hidden_q': jax.random.normal(ks[0], (B, S, DIM_Q), jnp.float32), 'kv_c': jax.random.normal(ks[1], (B, L, D_C), jnp.float32), 'Wq': jax.random.normal(ks[2], (H * K, DIM_Q), jnp.float32) * s_in, 'w_kc_q': jax.random.normal(ks[3], (H, K, D_CQ), jnp.float32) * s_k, 'w_kc_kv': jax.random.normal(ks[4], (H, K, D_C), jnp.float32) * s_k, 'W_qr': jax.random.normal(ks[5], (H, D_CQ, R), jnp.float32) * s_cq / np.sqrt(R), 'W_kr': jax.random.normal(ks[6], (H, D_C, R), jnp.float32) * s_c, 'Wo': jax.random.normal(ks[7], (DIM_Q, H * K), jnp.float32) * s_k}
    _L0_xattn_all = _L0_xattn_setup()
    _L0_xattn_in = {k: v for k, v in _L0_xattn_all.items() if k in ('Wq', 'w_kc_q', 'w_kc_kv', 'W_qr', 'W_kr', 'Wo')}
    del _L0_xattn_all

    def _L0_attn_setup():
        import jax, jax.numpy as jnp
        import numpy as np
        D_MODEL = 512
        N_HEADS = 16
        N_KV_HEADS = 2
        D_HEAD = D_MODEL // N_HEADS
        N_GROUPS = N_HEADS // N_KV_HEADS
        B, T = (2, 512)
        key = jax.random.key(seed)
        ks = jax.random.split(key, 9)
        s = 0.02
        return {'x': jax.random.normal(ks[0], (B, T, D_MODEL), jnp.float32), 'Wq': jax.random.normal(ks[1], (D_MODEL, N_HEADS * D_HEAD), jnp.float32) * s, 'bq': jnp.zeros((N_HEADS * D_HEAD,), jnp.float32), 'Wk': jax.random.normal(ks[2], (D_MODEL, N_KV_HEADS * D_HEAD), jnp.float32) * s, 'bk': jnp.zeros((N_KV_HEADS * D_HEAD,), jnp.float32), 'Wv': jax.random.normal(ks[3], (D_MODEL, N_KV_HEADS * D_HEAD), jnp.float32) * s, 'bv': jnp.zeros((N_KV_HEADS * D_HEAD,), jnp.float32), 'Wo': jax.random.normal(ks[4], (D_MODEL, D_MODEL), jnp.float32) * s, 'bo': jnp.zeros((D_MODEL,), jnp.float32)}
    _L0_attn_all = _L0_attn_setup()
    _L0_attn_in = {k: v for k, v in _L0_attn_all.items() if k in ('Wq', 'bq', 'Wk', 'bk', 'Wv', 'bv', 'Wo', 'bo')}
    del _L0_attn_all

    def _L0_ffn_setup():
        import jax, jax.numpy as jnp
        import numpy as np
        HIDDEN = 512
        INTER = 2048
        SCALE = 64.0

        def fwht(x):
            orig_shape = x.shape
            n = orig_shape[-1]
            x = x.reshape(-1, n)
            h = 1
            while h < n:
                x = x.reshape(-1, n // (2 * h), 2, h)
                a, b = (x[:, :, 0, :], x[:, :, 1, :])
                x = jnp.stack([a + b, a - b], axis=2).reshape(-1, n)
                h *= 2
            return (x / jnp.sqrt(jnp.asarray(n, x.dtype))).reshape(orig_shape)
        key = jax.random.key(seed)
        ks = jax.random.split(key, 8)
        inp = jax.random.normal(ks[0], (4, 512, HIDDEN), dtype=jnp.float32)
        SU_ug = jnp.where(jax.random.bernoulli(ks[1], 0.5, (HIDDEN,)), 1.0, -1.0).astype(jnp.float32)
        SU_dp = jnp.where(jax.random.bernoulli(ks[2], 0.5, (INTER,)), 1.0, -1.0).astype(jnp.float32)
        Wscale_ug = jax.random.uniform(ks[3], (2 * INTER,), jnp.float32, 0.5, 1.5)
        Wscale_dp = jax.random.uniform(ks[4], (HIDDEN,), jnp.float32, 0.5, 1.5)
        W_up = jax.random.normal(ks[5], (INTER, HIDDEN), dtype=jnp.float32) * 0.02
        W_gate = jax.random.normal(ks[6], (INTER, HIDDEN), dtype=jnp.float32) * 0.02
        W_down = jax.random.normal(ks[7], (HIDDEN, INTER), dtype=jnp.float32) * 0.02
        return {'input': inp, 'SU_ug': SU_ug, 'SU_dp': SU_dp, 'Wscale_ug': Wscale_ug, 'Wscale_dp': Wscale_dp, 'W_up': W_up, 'W_gate': W_gate, 'W_down': W_down}
    _L0_ffn_all = _L0_ffn_setup()
    _L0_ffn_in = {k: v for k, v in _L0_ffn_all.items() if k in ('SU_ug', 'SU_dp', 'Wscale_ug', 'Wscale_dp', 'W_up', 'W_gate', 'W_down')}
    del _L0_ffn_all

    def _L1_xattn_setup():
        import jax, jax.numpy as jnp
        import numpy as np
        B, S, L = (2, 256, 256)
        DIM_Q, H, K, D_C, D_CQ, R = (512, 16, 128, 128, 384, 64)

        def _rope_tables(length, dim):
            inv = 1.0 / 10000.0 ** (jnp.arange(0, dim, 2, dtype=jnp.float32) / dim)
            f = jnp.arange(length, dtype=jnp.float32)[:, None] * inv[None, :]
            sin = jnp.repeat(jnp.sin(f), 2, axis=-1)
            cos = jnp.repeat(jnp.cos(f), 2, axis=-1)
            return (sin, cos)

        def _rotate_half(x):
            half = x.shape[-1] // 2
            return jnp.concatenate([-x[..., half:], x[..., :half]], axis=-1)

        def _apply_rope(x, sin, cos):
            return x * cos + _rotate_half(x) * sin
        key = jax.random.key(seed)
        ks = jax.random.split(key, 8)
        return {'hidden_q': jax.random.normal(ks[0], (B, S, DIM_Q), jnp.float32), 'kv_c': jax.random.normal(ks[1], (B, L, D_C), jnp.float32), 'Wq': jax.random.normal(ks[2], (H * K, DIM_Q), jnp.float32) / np.sqrt(DIM_Q).astype(np.float32), 'w_kc_q': jax.random.normal(ks[3], (H, K, D_CQ), jnp.float32) / np.sqrt(K).astype(np.float32), 'w_kc_kv': jax.random.normal(ks[4], (H, K, D_C), jnp.float32) / np.sqrt(K).astype(np.float32), 'W_qr': jax.random.normal(ks[5], (H, D_CQ, R), jnp.float32) / np.float32(np.sqrt(D_CQ) * np.sqrt(R)), 'W_kr': jax.random.normal(ks[6], (H, D_C, R), jnp.float32) / np.sqrt(D_C).astype(np.float32), 'Wo': jax.random.normal(ks[7], (DIM_Q, H * K), jnp.float32) / np.sqrt(H * K).astype(np.float32)}
    _L1_xattn_all = _L1_xattn_setup()
    _L1_xattn_in = {k: v for k, v in _L1_xattn_all.items() if k in ('Wq', 'w_kc_q', 'w_kc_kv', 'W_qr', 'W_kr', 'Wo')}
    del _L1_xattn_all

    def _L1_attn_setup():
        import jax, jax.numpy as jnp
        import numpy as np
        B, N, H = (1, 1024, 512)
        NH, HD = (16, H // 16)
        WINDOW = 1024
        EPS = 1e-06
        THETA = 10000.0
        NEG = -1e+30

        def rmsnorm(x, w):
            var = jnp.mean(jnp.square(x.astype(jnp.float32)), axis=-1, keepdims=True)
            return (x * jax.lax.rsqrt(var + EPS)).astype(w.dtype) * w

        def rotate_half(x):
            x1, x2 = (x[..., :x.shape[-1] // 2], x[..., x.shape[-1] // 2:])
            return jnp.concatenate((-x2, x1), axis=-1)
        key = jax.random.key(seed)
        k1, k2, k3 = jax.random.split(key, 3)
        x = jax.random.normal(k1, (B, N, H), dtype=jnp.float32)
        w_qkv = jax.random.normal(k2, (H, 3 * H), dtype=jnp.float32) * (1.0 / np.sqrt(H))
        w_out = jax.random.normal(k3, (H, H), dtype=jnp.float32) * (1.0 / np.sqrt(H))
        q_gamma = jnp.ones((HD,), dtype=jnp.float32)
        k_gamma = jnp.ones((HD,), dtype=jnp.float32)
        return {'x': x, 'w_qkv': w_qkv, 'w_out': w_out, 'q_gamma': q_gamma, 'k_gamma': k_gamma}
    _L1_attn_all = _L1_attn_setup()
    _L1_attn_in = {k: v for k, v in _L1_attn_all.items() if k in ('w_qkv', 'w_out', 'q_gamma', 'k_gamma')}
    del _L1_attn_all

    def _L1_ffn_setup():
        import jax
        import jax.numpy as jnp
        import numpy as np
        NUM_EXPERTS = 32
        HIDDEN = 512
        INTER = 192
        TOP_K = 8
        TAU = 0.05
        BATCH, SEQ = (2, 256)
        key = jax.random.key(seed)
        k1, k2, k3, k4 = jax.random.split(key, 4)
        return {'hidden_states': jax.random.normal(k1, (BATCH, SEQ, HIDDEN), dtype=jnp.float32), 'gate_weight': jax.random.normal(k2, (NUM_EXPERTS, HIDDEN), dtype=jnp.float32) * 0.02, 'gate_up_proj': jax.random.normal(k3, (NUM_EXPERTS, 2 * INTER, HIDDEN), dtype=jnp.float32) * 0.02, 'down_proj': jax.random.normal(k4, (NUM_EXPERTS, HIDDEN, INTER), dtype=jnp.float32) * 0.02, 'layer_alpha': jnp.array(1.0, dtype=jnp.float32)}
    _L1_ffn_all = _L1_ffn_setup()
    _L1_ffn_in = {k: v for k, v in _L1_ffn_all.items() if k in ('gate_weight', 'gate_up_proj', 'down_proj', 'layer_alpha')}
    del _L1_ffn_all
    return {'x': x, 'ctx_512': ctx_512, 'L0_xattn_Wq': _L0_xattn_in['Wq'], 'L0_xattn_w_kc_q': _L0_xattn_in['w_kc_q'], 'L0_xattn_w_kc_kv': _L0_xattn_in['w_kc_kv'], 'L0_xattn_W_qr': _L0_xattn_in['W_qr'], 'L0_xattn_W_kr': _L0_xattn_in['W_kr'], 'L0_xattn_Wo': _L0_xattn_in['Wo'], 'L0_attn_Wq': _L0_attn_in['Wq'], 'L0_attn_bq': _L0_attn_in['bq'], 'L0_attn_Wk': _L0_attn_in['Wk'], 'L0_attn_bk': _L0_attn_in['bk'], 'L0_attn_Wv': _L0_attn_in['Wv'], 'L0_attn_bv': _L0_attn_in['bv'], 'L0_attn_Wo': _L0_attn_in['Wo'], 'L0_attn_bo': _L0_attn_in['bo'], 'L0_ffn_SU_ug': _L0_ffn_in['SU_ug'], 'L0_ffn_SU_dp': _L0_ffn_in['SU_dp'], 'L0_ffn_Wscale_ug': _L0_ffn_in['Wscale_ug'], 'L0_ffn_Wscale_dp': _L0_ffn_in['Wscale_dp'], 'L0_ffn_W_up': _L0_ffn_in['W_up'], 'L0_ffn_W_gate': _L0_ffn_in['W_gate'], 'L0_ffn_W_down': _L0_ffn_in['W_down'], 'L1_xattn_Wq': _L1_xattn_in['Wq'], 'L1_xattn_w_kc_q': _L1_xattn_in['w_kc_q'], 'L1_xattn_w_kc_kv': _L1_xattn_in['w_kc_kv'], 'L1_xattn_W_qr': _L1_xattn_in['W_qr'], 'L1_xattn_W_kr': _L1_xattn_in['W_kr'], 'L1_xattn_Wo': _L1_xattn_in['Wo'], 'L1_attn_w_qkv': _L1_attn_in['w_qkv'], 'L1_attn_w_out': _L1_attn_in['w_out'], 'L1_attn_q_gamma': _L1_attn_in['q_gamma'], 'L1_attn_k_gamma': _L1_attn_in['k_gamma'], 'L1_ffn_gate_weight': _L1_ffn_in['gate_weight'], 'L1_ffn_gate_up_proj': _L1_ffn_in['gate_up_proj'], 'L1_ffn_down_proj': _L1_ffn_in['down_proj'], 'L1_ffn_layer_alpha': _L1_ffn_in['layer_alpha']}

def reference(x, ctx_512, L0_xattn_Wq, L0_xattn_w_kc_q, L0_xattn_w_kc_kv, L0_xattn_W_qr, L0_xattn_W_kr, L0_xattn_Wo, L0_attn_Wq, L0_attn_bq, L0_attn_Wk, L0_attn_bk, L0_attn_Wv, L0_attn_bv, L0_attn_Wo, L0_attn_bo, L0_ffn_SU_ug, L0_ffn_SU_dp, L0_ffn_Wscale_ug, L0_ffn_Wscale_dp, L0_ffn_W_up, L0_ffn_W_gate, L0_ffn_W_down, L1_xattn_Wq, L1_xattn_w_kc_q, L1_xattn_w_kc_kv, L1_xattn_W_qr, L1_xattn_W_kr, L1_xattn_Wo, L1_attn_w_qkv, L1_attn_w_out, L1_attn_q_gamma, L1_attn_k_gamma, L1_ffn_gate_weight, L1_ffn_gate_up_proj, L1_ffn_down_proj, L1_ffn_layer_alpha):
    import jax
    import jax.numpy as jnp

    def _L0_xattn_ref(hidden_q, kv_c, Wq, w_kc_q, w_kc_kv, W_qr, W_kr, Wo):
        import jax, jax.numpy as jnp
        import numpy as np
        B, S, L = (2, 256, 256)
        DIM_Q, H, K, D_C, D_CQ, R = (512, 16, 128, 128, 384, 64)

        def _rope_tables(seq_len, dim, dtype):
            inv_freq = 1.0 / 10000.0 ** (jnp.arange(0, dim, 2, dtype=dtype) / dim)
            t = jnp.arange(seq_len, dtype=dtype)
            freqs = t[:, None] * inv_freq[None, :]
            sin = jnp.repeat(jnp.sin(freqs), 2, axis=-1)
            cos = jnp.repeat(jnp.cos(freqs), 2, axis=-1)
            return (sin, cos)

        def _rotate_half(x):
            h = x.shape[-1] // 2
            return jnp.concatenate([-x[..., h:], x[..., :h]], axis=-1)
        b, s, _ = hidden_q.shape
        l = kv_c.shape[1]
        q_hk = (hidden_q @ Wq.T).reshape(b, s, H, K)
        q_big = jnp.einsum('bshk,hkq->bshq', q_hk, w_kc_q)
        sin, cos = _rope_tables(l, D_C, kv_c.dtype)
        kv_rope = kv_c * cos[None] + _rotate_half(kv_c) * sin[None]
        q_r = jnp.einsum('bshq,hqr->bhsr', q_big, W_qr)
        k_r = jnp.einsum('bld,hdr->bhlr', kv_rope, W_kr)
        scores = jnp.einsum('bhsr,bhlr->bhsl', q_r, k_r)
        attn = jax.nn.softmax(scores, axis=-1)
        ctx_c = jnp.einsum('bhsl,bld->bhsd', attn, kv_rope)
        ctx_lat = jnp.einsum('bhsd,hkd->bshk', ctx_c, w_kc_kv)
        out = ctx_lat.reshape(b, s, H * K) @ Wo.T
        return out

    def _L0_attn_ref(x, Wq, bq, Wk, bk, Wv, bv, Wo, bo):
        import jax, jax.numpy as jnp
        import numpy as np
        D_MODEL = 512
        N_HEADS = 16
        N_KV_HEADS = 2
        D_HEAD = D_MODEL // N_HEADS
        N_GROUPS = N_HEADS // N_KV_HEADS
        B, T = (2, 512)
        Bx, Tx, C = x.shape
        Q = (x @ Wq + bq).reshape(Bx, Tx, N_HEADS, D_HEAD)
        K = (x @ Wk + bk).reshape(Bx, Tx, N_KV_HEADS, D_HEAD)
        V = (x @ Wv + bv).reshape(Bx, Tx, N_KV_HEADS, D_HEAD)
        Qg = Q.reshape(Bx, Tx, N_KV_HEADS, N_GROUPS, D_HEAD)
        scale = jnp.sqrt(jnp.float32(D_HEAD))
        scores = jnp.einsum('bqkgd,bskd->bkgqs', Qg, K) / scale
        causal = jnp.triu(jnp.ones((Tx, Tx), bool), k=1)
        scores = jnp.where(causal, -jnp.inf, scores)
        attn = jax.nn.softmax(scores, axis=-1)
        out = jnp.einsum('bkgqs,bskd->bqkgd', attn, V).reshape(Bx, Tx, C)
        return out @ Wo + bo

    def _L0_ffn_ref(input, SU_ug, SU_dp, Wscale_ug, Wscale_dp, W_up, W_gate, W_down):
        import jax, jax.numpy as jnp
        import numpy as np
        HIDDEN = 512
        INTER = 2048
        SCALE = 64.0

        def fwht(x):
            orig_shape = x.shape
            n = orig_shape[-1]
            x = x.reshape(-1, n)
            h = 1
            while h < n:
                x = x.reshape(-1, n // (2 * h), 2, h)
                a, b = (x[:, :, 0, :], x[:, :, 1, :])
                x = jnp.stack([a + b, a - b], axis=2).reshape(-1, n)
                h *= 2
            return (x / jnp.sqrt(jnp.asarray(n, x.dtype))).reshape(orig_shape)
        n = SU_ug.shape[0]
        x = input.reshape(-1, n)
        x = fwht(x * SU_ug) / SCALE
        x_up = x @ W_up.T * (Wscale_ug[:INTER] * SCALE)
        x_gate = x @ W_gate.T * (Wscale_ug[INTER:] * SCALE)
        x = jax.nn.silu(x_gate) * x_up
        x = fwht(x * SU_dp) / SCALE
        x = x @ W_down.T * (Wscale_dp * SCALE)
        return x.reshape(input.shape)

    def _L1_xattn_ref(hidden_q, kv_c, Wq, w_kc_q, w_kc_kv, W_qr, W_kr, Wo):
        import jax, jax.numpy as jnp
        import numpy as np
        B, S, L = (2, 256, 256)
        DIM_Q, H, K, D_C, D_CQ, R = (512, 16, 128, 128, 384, 64)

        def _rope_tables(length, dim):
            inv = 1.0 / 10000.0 ** (jnp.arange(0, dim, 2, dtype=jnp.float32) / dim)
            f = jnp.arange(length, dtype=jnp.float32)[:, None] * inv[None, :]
            sin = jnp.repeat(jnp.sin(f), 2, axis=-1)
            cos = jnp.repeat(jnp.cos(f), 2, axis=-1)
            return (sin, cos)

        def _rotate_half(x):
            half = x.shape[-1] // 2
            return jnp.concatenate([-x[..., half:], x[..., :half]], axis=-1)

        def _apply_rope(x, sin, cos):
            return x * cos + _rotate_half(x) * sin
        Bv, Sv, _ = hidden_q.shape
        _, Lv, _ = kv_c.shape
        q_hk = (hidden_q @ Wq.T).reshape(Bv, Sv, H, K)
        q_big = jnp.einsum('bshk,hkq->bshq', q_hk, w_kc_q)
        sin_q, cos_q = _rope_tables(Sv, D_CQ)
        q_big = _apply_rope(q_big, sin_q[None, :, None, :], cos_q[None, :, None, :])
        sin_k, cos_k = _rope_tables(Lv, D_C)
        kv_r = _apply_rope(kv_c, sin_k[None], cos_k[None])
        q_r = jnp.einsum('bshq,hqr->bhsr', q_big, W_qr)
        k_r = jnp.einsum('bld,hdr->bhlr', kv_r, W_kr)
        scores = jnp.einsum('bhsr,bhlr->bhsl', q_r, k_r)
        attn = jax.nn.softmax(scores, axis=-1)
        ctx_c = jnp.einsum('bhsl,bld->bhsd', attn, kv_r)
        ctx_lat = jnp.einsum('bhsd,hkd->bhsk', ctx_c, w_kc_kv)
        ctx = ctx_lat.transpose(0, 2, 1, 3).reshape(Bv, Sv, H * K)
        return ctx @ Wo.T

    def _L1_attn_ref(x, w_qkv, w_out, q_gamma, k_gamma):
        import jax, jax.numpy as jnp
        import numpy as np
        B, N, H = (1, 1024, 512)
        NH, HD = (16, H // 16)
        WINDOW = 1024
        EPS = 1e-06
        THETA = 10000.0
        NEG = -1e+30

        def rmsnorm(x, w):
            var = jnp.mean(jnp.square(x.astype(jnp.float32)), axis=-1, keepdims=True)
            return (x * jax.lax.rsqrt(var + EPS)).astype(w.dtype) * w

        def rotate_half(x):
            x1, x2 = (x[..., :x.shape[-1] // 2], x[..., x.shape[-1] // 2:])
            return jnp.concatenate((-x2, x1), axis=-1)
        b, n, _ = x.shape
        qkv = jnp.einsum('bnh,hm->bnm', x, w_qkv)
        q, k, v = jnp.split(qkv, 3, axis=-1)
        q = q.reshape(b, n, NH, HD).transpose(0, 2, 1, 3)
        k = k.reshape(b, n, NH, HD).transpose(0, 2, 1, 3)
        v = v.reshape(b, n, NH, HD).transpose(0, 2, 1, 3)
        q = rmsnorm(q, q_gamma)
        k = rmsnorm(k, k_gamma)
        inv_freq = 1.0 / THETA ** (jnp.arange(0, HD, 2, dtype=jnp.float32) / HD)
        t = jnp.arange(n, dtype=jnp.float32)
        freqs = t[:, None] * inv_freq[None, :]
        emb = jnp.concatenate((freqs, freqs), axis=-1)
        cos = jnp.cos(emb)[None, None, :, :]
        sin = jnp.sin(emb)[None, None, :, :]
        q = q * cos + rotate_half(q) * sin
        k = k * cos + rotate_half(k) * sin
        kv_len = k.shape[-2]
        q_idx = jnp.arange(n)[:, None] + (kv_len - n)
        k_idx = jnp.arange(kv_len)[None, :]
        mask = (q_idx >= k_idx) & (q_idx - k_idx <= WINDOW)
        scores = jnp.einsum('bhqd,bhkd->bhqk', q, k) / np.sqrt(HD)
        scores = jnp.where(mask[None, None, :, :], scores, NEG)
        attn = jax.nn.softmax(scores, axis=-1)
        out = jnp.einsum('bhqk,bhkd->bhqd', attn, v)
        out = out.transpose(0, 2, 1, 3).reshape(b, n, H)
        return jnp.einsum('bnh,hm->bnm', out, w_out)

    def _L1_ffn_ref(hidden_states, gate_weight, gate_up_proj, down_proj, layer_alpha):
        import jax
        import jax.numpy as jnp
        import numpy as np
        NUM_EXPERTS = 32
        HIDDEN = 512
        INTER = 192
        TOP_K = 8
        TAU = 0.05
        BATCH, SEQ = (2, 256)
        B, S, H = hidden_states.shape
        x = hidden_states.reshape(-1, H)
        T = x.shape[0]
        logits = x @ gate_weight.T
        probs = jax.nn.softmax(logits.astype(jnp.float32), axis=-1).astype(logits.dtype)
        topv, topi = jax.lax.top_k(probs, TOP_K)
        topv = topv / jnp.clip(topv.sum(axis=-1, keepdims=True), 1e-12)
        scaled = topv * layer_alpha.astype(topv.dtype)
        active = scaled >= TAU
        empty = ~jnp.any(active, axis=-1)
        fallback = jnp.arange(TOP_K)[None, :] == jnp.argmax(scaled, axis=-1)[:, None]
        active = active | empty[:, None] & fallback
        routing_weights = topv * active.astype(topv.dtype)
        routing_weights = routing_weights / jnp.clip(routing_weights.sum(axis=-1, keepdims=True), 1e-12)
        combine = jnp.zeros((T, NUM_EXPERTS), dtype=x.dtype)
        combine = combine.at[jnp.arange(T)[:, None], topi].add(routing_weights)

        def expert_step(acc, xs):
            w_gu, w_d, c_e = xs
            gu = x @ w_gu.T
            g, u = jnp.split(gu, 2, axis=-1)
            h = jax.nn.silu(g) * u
            acc = acc + h @ w_d.T * c_e[:, None]
            return (acc, None)
        out, _ = jax.lax.scan(expert_step, jnp.zeros_like(x), (gate_up_proj, down_proj, combine.T))
        return out.reshape(B, S, H)
    x = x + _L0_xattn_ref(_layernorm(x, axis=-1), ctx_512, L0_xattn_Wq, L0_xattn_w_kc_q, L0_xattn_w_kc_kv, L0_xattn_W_qr, L0_xattn_W_kr, L0_xattn_Wo)
    x = x + _L0_attn_ref(_layernorm(x, axis=-1), L0_attn_Wq, L0_attn_bq, L0_attn_Wk, L0_attn_bk, L0_attn_Wv, L0_attn_bv, L0_attn_Wo, L0_attn_bo)
    x = x + _L0_ffn_ref(_layernorm(x, axis=-1), L0_ffn_SU_ug, L0_ffn_SU_dp, L0_ffn_Wscale_ug, L0_ffn_Wscale_dp, L0_ffn_W_up, L0_ffn_W_gate, L0_ffn_W_down)
    x = x + _L1_xattn_ref(_layernorm(x, axis=-1), ctx_512, L1_xattn_Wq, L1_xattn_w_kc_q, L1_xattn_w_kc_kv, L1_xattn_W_qr, L1_xattn_W_kr, L1_xattn_Wo)
    x = x + _L1_attn_ref(_layernorm(x, axis=-1), L1_attn_w_qkv, L1_attn_w_out, L1_attn_q_gamma, L1_attn_k_gamma)
    x = x + _L1_ffn_ref(_layernorm(x, axis=-1), L1_ffn_gate_weight, L1_ffn_gate_up_proj, L1_ffn_down_proj, L1_ffn_layer_alpha)
    return x

_drawn_inputs = setup_inputs


def setup_inputs(seed=0):
    import zlib

    import numpy as np

    out = dict(_drawn_inputs(seed))
    spreads = {'L0_attn_bq': (0.0, 0.8),
     'L0_attn_bk': (0.0, 0.8),
     'L0_attn_bv': (0.0, 0.371),
     'L0_attn_bo': (0.0, 0.1),
     'L1_attn_q_gamma': (1.0, 0.6),
     'L1_attn_k_gamma': (1.0, 0.6)}
    factors = {'L0_attn_Wq': 8.0,
     'L0_attn_Wk': 8.0,
     'L0_ffn_Wscale_ug': 2.779,
     'L0_ffn_Wscale_dp': 4.097,
     'L1_ffn_gate_weight': 8.0,
     'L1_ffn_gate_up_proj': 8.0,
     'L1_ffn_down_proj': 8.0}
    for name, (base, spread) in spreads.items():
        noise = np.random.default_rng([zlib.crc32(name.encode()), seed]).standard_normal(out[name].shape)
        drawn = base * np.exp(spread * noise) if base else spread * noise
        out[name] = jnp.asarray(drawn.astype(out[name].dtype))
    for name, factor in factors.items():
        out[name] = (out[name] * factor).astype(out[name].dtype)
    return out
```

```python
from contextlib import ExitStack

import numpy as np

import concourse.bass as bass
from concourse import mybir

ALU = mybir.AluOpType
ACT = mybir.ActivationFunctionType
F32 = mybir.dt.float32
U32 = mybir.dt.uint32
AX_X = mybir.AxisListType.X

P = 128
BANK = 512
B, S, D = 32, 32, 512
TOK = B * S
NT = TOK // P
BPT = P // S
KD = D // P
L, DC = 257, 128
LC = (L - 1) // P
XH, XK, DCQ, RR = 16, 128, 384, 64
QC = DCQ // P
AH, DH = 16, 32
HPT = P // DH
AT = AH // HPT
KVH = 2
INTER = 2048
FC = INTER // P
NE, EI, TOPK, TAU = 32, 192, 8, 0.05
E2 = EI - P
NEG = -1e30

L0_PACK = {"wq": D, "kcq": QC * XK, "qr": QC * RR, "kr": DC, "kckv": DC, "wo": D}
L1_PACK = {"wq": KD * XK, "kcq": DCQ, "qr": DCQ + DCQ // 2, "kr": DC, "kckv": DC, "wo": D}
SLOT = 2560
NSLOT = 4


def columns(pack):
    at, out = 0, {}
    for name, n in pack.items():
        out[name] = (at, at + n)
        at += n
    return out, at


class Engine:

    def __init__(self, sem):
        self.sem, self.count, self.steps = sem, 0, []

    def __call__(self, step, *after):
        self.count += 1
        self.steps.append((step, after, True))
        return (self.sem, self.count)

    def quiet(self, step, *after):
        self.steps.append((step, after, False))

    def now(self):
        return (self.sem, self.count)

    def emit(self, eng):
        reached = {}

        def wait(mark):
            if mark is None:
                return
            if isinstance(mark, list):
                for m in mark:
                    wait(m)
                return
            sem, value = mark
            if reached.get(id(sem), 0) < value:
                eng.wait_ge(sem, value)
                reached[id(sem)] = value

        for step, after, counted in self.steps:
            for mark in after:
                wait(mark)
            ins = step(eng) if step else None
            if counted:
                ins.then_inc(self.sem, 1)


class Slot:

    def __init__(self, ap, sem=None):
        self.ap, self.sem, self.landed = ap, sem, 0
        self.marks, self.taken = [], False

    @property
    def free(self):
        return self.marks

    @free.setter
    def free(self, marks):
        self.marks, self.taken = marks, False


class Ring:
    def __init__(self, slots):
        self.slots, self.n = slots, 0

    def take(self):
        slot = self.slots[self.n % len(self.slots)]
        self.n += 1
        assert not slot.taken, "taken again before its readers are known"
        slot.taken = True
        return slot


def build_kernel(nc, d, out, last_phase=6):
    with ExitStack() as ctx:
        def sem(name):
            return ctx.enter_context(nc.semaphore(name))

        def keep(name, shape, dt=F32):
            return ctx.enter_context(nc.sbuf_tensor(name, shape, dt))

        pe, act, dve, pool, sp = (Engine(sem(f"s_{n}")) for n in ("pe", "act", "dve", "pool", "sp"))
        compute = (pe, act, dve, pool)

        def dma(slot, dst, src, *after):
            slot.landed += 16
            sp.quiet(lambda e: e.dma_start(dst, src).then_inc(slot.sem, 16), *after)
            return (slot.sem, slot.landed)

        def barrier():
            marks = [q.now() for q in compute]
            for q in compute:
                q.quiet(None, marks)
            return marks

        banks = ctx.enter_context(nc.psum_tensor("banks", [P, 8, BANK], F32))

        def psum(first, n=1):
            return banks[:, first:first + n, :].rearrange("p a n -> p (a n)")

        x = keep("x", [P, NT, D])
        hT = keep("hT", [P, KD, TOK])
        xn = Ring([Slot(keep(f"xn{i}", [P, D])) for i in range(2)])
        stats = keep("stats", [P, NT, 6])
        moments = keep("moments", [P, NT, 2])
        rstd = keep("rstd", [P, NT])
        wring = Ring([Slot(keep(f"w{i}", [P, SLOT]), sem(f"s_w{i}")) for i in range(NSLOT)])
        ident = keep("ident", [P, P])
        kcos = keep("kcos", [P, 3, DC])
        ksin = keep("ksin", [P, 3, DC])

        power = keep("power", [P, AH])
        power_set = pool(lambda e: e.memset(power[:], -0.5))
        const = Slot(None, sem("s_const"))
        xin = [Slot(None, sem(f"s_x{i}")) for i in range(NT)]
        x_ready = []
        for i in range(NT):
            x_ready.append([dma(xin[i], x[:, i, :], d["x"][i * P:(i + 1) * P, :])])
            if i == 0:
                dma(const, ident[:], d["ident"])
        dma(const, kcos[:].rearrange("p a n -> p (a n)"), d["kcos"])
        const_ready = dma(const, ksin[:].rearrange("p a n -> p (a n)"), d["ksin"])

        def load_weights(src, n):
            slot = wring.take()
            ready = dma(slot, slot.ap[:, 0:n], src, list(slot.free))
            return slot, ready

        def layernorm_tile(i, scale=None, batch_major=False):
            m1 = dve(lambda e: e.bn_stats(stats[:, i, :], x[:, i, :]), x_ready[i])
            m2 = dve(lambda e: e.bn_aggr(moments[:, i, :], stats[:, i, :]), m1)
            m3 = dve(lambda e: e.tensor_scalar(rstd[:, i:i + 1], moments[:, i, 1:2], 1e-5, None, ALU.add), m2)
            m3 = pool(lambda e: e.tensor_tensor(rstd[:, i:i + 1], rstd[:, i:i + 1], power[:, 0:1], ALU.pow), m3, power_set)
            buf = xn.take()
            m4 = dve(lambda e: e.tensor_scalar(buf.ap[:], x[:, i, :], moments[:, i, 0:1], rstd[:, i:i + 1],
                                               ALU.subtract, ALU.mult), m3, list(buf.free))
            bank = ln_banks.take()
            for k in range(KD):
                step = lambda e, k=k: e.transpose(bank.ap[:, k * P:(k + 1) * P], buf.ap[:, k * P:(k + 1) * P], ident[:])
                if k < KD - 1:
                    pe.quiet(step, m4, const_ready, list(bank.free))
                else:
                    turned = pe(step)
            buf.free = [turned]
            dst = hT[:, :, i * P:(i + 1) * P]
            src = bank.ap.rearrange("p (k n) -> p k n", k=KD)
            if batch_major:
                dst = dst.rearrange("p k (b s) -> p k b s", s=S)
                src = src.rearrange("p k (s b) -> p k b s", s=S)
                done = act(lambda e: [e.copy(dst[:, k, :, :], src[:, k, :, :]) for k in range(KD)][-1], turned)
            elif scale is None:
                done = act(lambda e: e.copy(dst, src), turned)
            else:
                done = dve(lambda e: e.tensor_tensor(dst, src, scale, ALU.mult), turned, const_ready)
            bank.free = [done]
            return done

        def layernorm(**kind):
            return [layernorm_tile(i, **kind) for i in range(NT)]

        def mm_group(out_ap, pairs, after=()):
            for n, (w, m) in enumerate(pairs):
                step = lambda e, n=n, w=w, m=m: e.matmul(out_ap, w, m, start=n == 0, stop=n == len(pairs) - 1)
                if n < len(pairs) - 1:
                    pe.quiet(step, *(after if n == 0 else ()))
                else:
                    return pe(step, *(after if n == 0 else ()))

        def cross_attention(name, rope_q):
            nonlocal ln_banks
            barrier()
            cols, width = columns(L1_PACK if rope_q else L0_PACK)
            with ExitStack() as arena:
                def sb(n, shape, dt=F32):
                    return arena.enter_context(nc.sbuf_tensor(f"{name}_{n}", shape, dt))

                qT = sb("qT", [P, NT, XH, P])
                wn = sb("wn", [P, XH, D])
                q_done = [[None, None] for _ in range(XH)]
                wn_done = [None] * XH

                ln_banks = Ring([Slot(psum(6)), Slot(psum(7))])
                h_ready = layernorm()
                small = Ring([Slot(psum(4)), Slot(psum(5))])
                wide = Ring([Slot(psum(i)) for i in range(4)])
                with ExitStack() as part:
                    def sbp(n, shape):
                        return part.enter_context(nc.sbuf_tensor(f"{name}_{n}", shape, F32))

                    def half(ap, t):
                        return ap[:, t * BANK:(t + 1) * BANK]

                    def q_cols(h, t):
                        return qT[:, t * (NT // 2):(t + 1) * (NT // 2), h, :]

                    def tiles(ap):
                        return ap.rearrange("p (i n) -> p i n", n=P)

                    weights = {}

                    def fetch(h):
                        weights[h] = load_weights(d[f"{name}_heads"][h], width)

                    def w(h, key, rows=P):
                        a, b = cols[key]
                        return weights[h][0].ap[0:rows, a:b]

                    def fold_out(h):
                        bank = small.take()
                        m = mm_group(bank.ap, [(w(h, "kckv"), w(h, "wo"))], (list(bank.free), weights[h][1]))
                        wn_done[h] = act(lambda e: e.copy(wn[:, h, :], bank.ap), m)
                        bank.free = [wn_done[h]]

                    if not rope_q:
                        t1 = Ring([Slot(sbp(f"t1_{i}", [RR, XK])) for i in range(2)])
                        t2 = Ring([Slot(sbp(f"t2_{i}", [P, DC])) for i in range(2)])
                        mq = Ring([Slot(sbp(f"mq_{i}", [P, KD, DC])) for i in range(2)])
                        T1, T2, MQ = {}, {}, {}

                        def fold_1(h):
                            bank, dst = small.take(), t1.take()
                            kcq = w(h, "kcq").rearrange("p (c k) -> p c k", c=QC)
                            qr = w(h, "qr").rearrange("p (c r) -> p c r", c=QC)
                            m = mm_group(bank.ap[0:RR, 0:XK], [(qr[:, c, :], kcq[:, c, :]) for c in range(QC)],
                                         (list(bank.free), weights[h][1]))
                            T1[h] = (dst, act(lambda e: e.copy(dst.ap[:], bank.ap[0:RR, 0:XK]), m, list(dst.free)))
                            bank.free = [T1[h][1]]

                        def fold_2(h):
                            bank, dst = small.take(), t2.take()
                            src, ready = T1[h]
                            m = mm_group(bank.ap[:, 0:DC], [(src.ap[:], w(h, "kr", RR))], (list(bank.free), ready))
                            src.free = [m]
                            T2[h] = (dst, dve(lambda e: e.tensor_copy(dst.ap[:], bank.ap[:, 0:DC]), m, list(dst.free)))
                            bank.free = [T2[h][1]]

                        def fold_3(h):
                            bank, dst = small.take(), mq.take()
                            src, ready = T2[h]
                            for k in range(KD):
                                m = mm_group(bank.ap[:, k * P:(k + 1) * P], [(w(h, "wq")[:, k * P:(k + 1) * P], src.ap[:])],
                                             (list(bank.free), ready))
                            src.free = [m]
                            MQ[h] = (dst, dve(lambda e: e.tensor_copy(dst.ap[:].rearrange("p k n -> p (k n)"), bank.ap), m,
                                              list(dst.free)))
                            bank.free = [MQ[h][1]]

                        def project(h):
                            src, ready = MQ[h]
                            for t in range(TOK // BANK):
                                bank = wide.take()
                                m = mm_group(bank.ap, [(src.ap[:, k, :], half(hT[:, k, :], t)) for k in range(KD)],
                                             (list(bank.free), ready, h_ready))
                                q = (act if t else dve)
                                copy = (lambda e, t=t, bank=bank: e.copy(q_cols(h, t), tiles(bank.ap))) if t else \
                                    (lambda e, t=t, bank=bank: e.tensor_copy(q_cols(h, t), tiles(bank.ap)))
                                q_done[h][t] = q(copy, m)
                                bank.free = [q_done[h][t]]
                            src.free = [m]

                        for h in range(XH + 3):
                            if h < XH:
                                fetch(h)
                                fold_1(h)
                            if 0 <= h - 1 < XH:
                                fold_2(h - 1)
                            if 0 <= h - 2 < XH:
                                fold_3(h - 2)
                                fold_out(h - 2)
                                weights[h - 2][0].free = [pe.now()]
                            if 0 <= h - 3 < XH:
                                project(h - 3)
                    else:
                        cosq = sbp("cosq", [P, QC, S])
                        sinq = sbp("sinq", [P, QC, S])
                        tabs = Slot(None, sem(f"s_{name}_tabs"))
                        start = [q.now() for q in compute]
                        dma(tabs, cosq[:].rearrange("p a n -> p (a n)"), d["cosq"], prior)
                        tabs_ready = dma(tabs, sinq[:].rearrange("p a n -> p (a n)"), d["sinq"], prior)
                        ubuf = Ring([Slot(sbp(f"u_{i}", [P, 2, QC, DC])) for i in range(2)])
                        qh = Ring([Slot(sbp(f"qh_{i}", [P, BANK])) for i in range(2)])
                        ybuf = Ring([Slot(sbp(f"y_{i}", [P, 2, BANK])) for i in range(4)])
                        U, QH, Y = {}, {}, {}

                        def fold_u(h):
                            dst = ubuf.take()
                            marks = []
                            for v in range(2):
                                bank = small.take()
                                for c in range(QC):
                                    at = c * P + v * (DCQ // 2)
                                    m = mm_group(bank.ap[:, c * P:(c + 1) * P],
                                                 [(w(h, "qr", RR)[:, at:at + P], w(h, "kr", RR))],
                                                 (list(bank.free), weights[h][1]))
                                marks.append(act(lambda e, v=v, bank=bank: e.copy(
                                    dst.ap[:, v, :, :].rearrange("p c n -> p (c n)"), bank.ap[:, 0:QC * P]), m, list(dst.free)))
                                bank.free = [marks[-1]]
                            U[h] = (dst, marks)

                        def query(h, t):
                            bank, dst = wide.take(), qh.take()
                            wq = w(h, "wq").rearrange("p (k n) -> p k n", k=KD)
                            m = mm_group(bank.ap, [(wq[:, k, :], half(hT[:, k, :], t)) for k in range(KD)],
                                         (list(bank.free), weights[h][1], h_ready))
                            QH[h, t] = (dst, act(lambda e: e.copy(dst.ap[:], bank.ap), m, list(dst.free)))
                            bank.free = [QH[h, t][1]]

                        def widen(h, t, c):
                            bank, dst = wide.take(), ybuf.take()
                            src, ready = QH[h, t]
                            m = mm_group(bank.ap, [(w(h, "kcq")[:, c * P:(c + 1) * P], src.ap[:])], (list(bank.free), ready))
                            src.free = [m]
                            marks = []
                            for v, tab in enumerate((cosq, sinq)):
                                table = tab[:, c, :].rearrange("p (i s b) -> p i s b", i=1, b=1).to_broadcast([P, BANK // P, S, BPT])
                                marks.append(dve(lambda e, v=v, table=table: e.tensor_tensor(
                                    dst.ap[:, v, :].rearrange("p (i s b) -> p i s b", s=S, b=BPT),
                                    bank.ap.rearrange("p (i s b) -> p i s b", s=S, b=BPT), table, ALU.mult),
                                    m, tabs_ready, list(dst.free)))
                            bank.free = marks
                            Y[h, t, c] = (dst, marks)

                        acc = {}

                        def narrow(h, t, c):
                            if c == 0:
                                acc[h, t] = wide2.take()
                            bank = acc[h, t]
                            src, ready = Y[h, t, c]
                            for v in range(2):
                                step = lambda e, v=v: e.matmul(bank.ap, U[h][0].ap[:, v, c, :], src.ap[:, v, :],
                                                               start=c == 0 and v == 0, stop=c == QC - 1 and v == 1)
                                if v == 0:
                                    pe.quiet(step, ready, U[h][1], list(bank.free) if c == 0 else None)
                                else:
                                    m = pe(step)
                            src.free = [m]
                            if c == QC - 1:
                                q_done[h][t] = act(lambda e: e.copy(q_cols(h, t), tiles(bank.ap)), m)
                                bank.free = [q_done[h][t]]
                                if t == 1:
                                    U[h][0].free = [m]
                                    weights[h][0].free = [m]

                        wide = Ring([Slot(psum(i)) for i in range(4)])
                        wide2 = Ring([Slot(psum(6)), Slot(psum(7))])
                        for s_, slot in zip(wide2.slots, ln_banks.slots):
                            s_.free = list(slot.free)
                        items = [(h, t, c) for h in range(XH) for t in range(2) for c in range(QC)]
                        LAG = 2
                        fetch(0)
                        query(0, 0)
                        for n in range(len(items) + LAG):
                            if n < len(items):
                                h, t, c = items[n]
                                if c == 0 and t == 0:
                                    fold_u(h)
                                    fold_out(h)
                                    if h + 1 < XH:
                                        fetch(h + 1)
                                if c == 1:
                                    nxt = (h, 1) if t == 0 else (h + 1, 0)
                                    if nxt[0] < XH:
                                        query(*nxt)
                                widen(h, t, c)
                            if n >= LAG:
                                narrow(*items[n - LAG])
                last = barrier()

                craw = Ring([Slot(sb(f"craw{i}", [P, 3, DC]), sem(f"s_{name}_c{i}")) for i in range(2)])
                rot = sb("rot", [P, 3, DC])
                kv = Ring([Slot(sb(f"kv{i}", [P, 3, DC])) for i in range(4)])
                kvT = Ring([Slot(sb(f"kvT{i}", [P, LC * P + S])) for i in range(3)])
                prob = Ring([Slot(sb(f"prob{i}", [P, 4, LC * P])) for i in range(2)])
                pT = Ring([Slot(sb(f"pT{i}", [P, LC, BANK])) for i in range(2)])
                small4 = Ring([Slot(sb(f"small4_{i}", [P, 5, 4])) for i in range(4)])
                s_banks = Ring([Slot(psum(0, 2)), Slot(psum(2, 2))])
                t_banks = Ring([Slot(psum(4, 2))])
                c_bank = Slot(psum(6))
                k_bank = Slot(psum(7))
                o_bank = k_bank
                KV, KT, PR, PT = {}, {}, {}, {}

                def of_batch(b, head=0, n=XH):
                    cols = qT[:, b // BPT, :, :].rearrange("p h n -> p (h n)")
                    return cols[:, head * P + b % BPT:(head + n) * P:BPT]
                rot_free = [None]

                def keys(b):
                    raw, dst = craw.take(), kv.take()
                    for c in range(LC):
                        dma(raw, raw.ap[:, c, :], d["ctx"][b, c * P:(c + 1) * P, :], list(raw.free), last)
                    ready = dma(raw, raw.ap[:, LC, :], d["ctx"][b, L - 1:L, :].to_broadcast([P, DC]))
                    hw = DC // 2
                    m1 = pool(lambda e: e.tensor_tensor(dst.ap[:], raw.ap[:], kcos[:], ALU.mult), ready, list(dst.free), const_ready)
                    m2 = pool(lambda e: e.tensor_tensor(rot[:, :, 0:hw], raw.ap[:, :, hw:DC], ksin[:, :, 0:hw], ALU.mult), rot_free[0])
                    m3 = pool(lambda e: e.tensor_tensor(rot[:, :, hw:DC], raw.ap[:, :, 0:hw], ksin[:, :, hw:DC], ALU.mult))
                    m4 = pool(lambda e: e.tensor_tensor(dst.ap[:], dst.ap[:], rot[:], ALU.add), m1, m2, m3)
                    raw.free = [m3]
                    rot_free[0] = m4
                    m5 = pool(lambda e: e.tensor_tensor(dst.ap[:, 0:LC, :], dst.ap[:, 0:LC, :],
                                                        dst.ap[:, LC:LC + 1, :].to_broadcast([P, LC, DC]), ALU.subtract), m4)
                    KV[b] = (dst, m5)

                def keys_T(b):
                    src, ready = KV[b]
                    dst = kvT.take()
                    for c in range(LC):
                        pe.quiet(lambda e, c=c: e.transpose(k_bank.ap[:, c * P:(c + 1) * P], src.ap[:, c, :], ident[:]),
                                 ready, list(k_bank.free))
                    m = pe(lambda e: e.transpose(k_bank.ap[:, LC * P:LC * P + S], src.ap[0:S, LC, :], ident[0:S, 0:S]))
                    done = act(lambda e: e.copy(dst.ap[:], k_bank.ap[:, 0:LC * P + S]), m, list(dst.free))
                    k_bank.free = [done]
                    KT[b] = (dst, done)

                def scores(b):
                    kt, ready = KT[b]
                    bank = s_banks.take()
                    for r in range(4):
                        m = mm_group(bank.ap[:, r * 256:(r + 1) * 256],
                                     [(of_batch(b, 4 * r, 4), kt.ap[:, 0:LC * P])],
                                     (list(bank.free), ready))
                    dst = prob.take()
                    small = small4.take()
                    mx, neg, sums, tail, rec = (small.ap[:, n, :] for n in range(5))
                    sc = bank.ap.rearrange("p (r n) -> p r n", r=4)
                    m1 = dve(lambda e: e.tensor_reduce(mx, sc, AX_X, ALU.max), m, list(small.free))
                    m2 = dve(lambda e: e.tensor_scalar(neg, mx, -1.0, 0.0, ALU.mult, ALU.min), m1)
                    for r in range(4):
                        m3 = act(lambda e, r=r: e.activation(dst.ap[:, r, :], sc[:, r, :], ACT.Exp, bias=neg[:, r:r + 1],
                                                             accum_out=sums[:, r:r + 1]), m2, list(dst.free))
                    bank.free = [m3]
                    m4 = act(lambda e: e.activation(tail, neg, ACT.Exp))
                    m5 = dve(lambda e: e.tensor_tensor(sums, sums, tail, ALU.add), m4)
                    m6 = dve(lambda e: e.reciprocal(rec, sums), m5)
                    m7 = pool(lambda e: e.tensor_tensor(dst.ap[:], dst.ap[:],
                                                        rec.rearrange("p (r n) -> p r n", n=1).to_broadcast([P, 4, LC * P]),
                                                        ALU.mult), m6)
                    small.free = [m7]
                    PR[b] = (dst, m7)

                def turn(b):
                    src, ready = PR[b]
                    bank, dst = t_banks.take(), pT.take()
                    for c in range(LC):
                        for r in range(4):
                            step = lambda e, c=c, r=r: e.transpose(bank.ap[:, c * BANK + r * P:c * BANK + (r + 1) * P],
                                                                   src.ap[:, r, c * P:(c + 1) * P], ident[:])
                            if r < 3:
                                pe.quiet(step, ready, list(bank.free))
                            else:
                                m = pe(step)
                        if c == 0:
                            d0 = act(lambda e: e.copy(dst.ap[:, 0, :], bank.ap[:, 0:BANK]), m, list(dst.free))
                        else:
                            d1 = dve(lambda e: e.tensor_copy(dst.ap[:, 1, :], bank.ap[:, BANK:2 * BANK]), m, list(dst.free))
                    src.free = [m]
                    bank.free = [d0, d1]
                    PT[b] = (dst, [d0, d1])

                ctx_done = {}

                def values(b):
                    src, ready = PT[b]
                    v, _ = KV[b]
                    kt, _ = KT[b]
                    m = mm_group(c_bank.ap, [(v.ap[:, c, :], src.ap[:, c, :]) for c in range(LC)], (list(c_bank.free), ready))
                    src.free = [m]
                    v.free = [m]
                    ctx_done[b] = dve(lambda e: e.tensor_scalar(
                        of_batch(b), c_bank.ap,
                        kt.ap[:, LC * P:LC * P + 1], None, ALU.add), m)
                    c_bank.free = [ctx_done[b]]
                    kt.free = [ctx_done[b]]

                def output(i):
                    m = mm_group(o_bank.ap, [(qT[:, i, h, :], wn[:, h, :]) for h in range(XH)],
                                 (list(o_bank.free), ctx_done[i * BPT + BPT - 1]))
                    done = dve(lambda e: e.tensor_tensor(x[:, i, :], x[:, i, :], o_bank.ap, ALU.add), m)
                    o_bank.free = [done]
                    x_ready[i] = [done]

                keys(0)
                keys(1)
                keys_T(0)
                for b in range(B + 3):
                    if b < B:
                        scores(b)
                    if 0 <= b - 2 < B:
                        values(b - 2)
                    if b + 2 < B:
                        keys(b + 2)
                    if b + 1 < B:
                        keys_T(b + 1)
                    if 0 <= b - 1 < B:
                        turn(b - 1)
                    if b >= 3 and (b - 3) % BPT == BPT - 1:
                        output((b - 3) // BPT)

        def self_attention(name, groups, normed):
            nonlocal ln_banks
            start = barrier()
            tpg = AT // groups
            kw = groups * P
            vw = groups * P if normed else groups * DH
            with ExitStack() as arena:
                def sb(n, shape, dt=F32):
                    return arena.enter_context(nc.sbuf_tensor(f"{name}_{n}", shape, dt))

                mask = sb("mask", [P, S])
                tabs = Slot(None, sem(f"s_{name}_tabs"))
                dma(tabs, mask[:], d["mask"], prior)
                if normed:
                    cosg, sing = sb("cosg", [P, 2, DH]), sb("sing", [P, 2, DH])
                    gam = sb("gam", [P, 4, DH])
                    for n, g in enumerate(("gq", "gq_roll", "gk", "gk_roll")):
                        dma(tabs, gam[:, n, :], d[g].to_broadcast([P, DH]), prior)
                    for n in range(2):
                        dma(tabs, cosg[:, n, :], d["acos"], prior)
                        tabs_ready = dma(tabs, sing[:, n, :], d["asin"], prior)
                    g1 = dve(lambda e: e.tensor_tensor(cosg[:], cosg[:], gam[:, 0::2, :], ALU.mult), tabs_ready)
                    g2 = dve(lambda e: e.tensor_tensor(sing[:], sing[:], gam[:, 1::2, :], ALU.mult), tabs_ready)
                    table_done = [g1, g2]
                else:
                    bias = {}
                    for key, n in (("bq", D), ("bk", kw), ("bv", vw), ("bo", D)):
                        bias[key] = sb(key, [P, n])
                        tabs_ready = dma(tabs, bias[key][:], d[f"{name}_{key}"].to_broadcast([P, n]), prior)
                    table_done = [tabs_ready]

                wq, wq_ready = load_weights(d[f"{name}_wq"], KD * D)
                wk, wk_ready = load_weights(d[f"{name}_wk"], KD * kw)
                wv, wv_ready = load_weights(d[f"{name}_wv"], KD * vw)
                wo, wo_ready = load_weights(d[f"{name}_wo"], KD * D)
                w_q = wq.ap[:, 0:KD * D].rearrange("p (k n) -> p k n", k=KD)
                w_k = wk.ap[:, 0:KD * kw].rearrange("p (k n) -> p k n", k=KD)
                w_v = wv.ap[:, 0:KD * vw].rearrange("p (k n) -> p k n", k=KD)
                w_o = wo.ap[:, 0:KD * D].rearrange("p (k n) -> p k n", k=KD)

                ln_banks = Ring([Slot(psum(6)), Slot(psum(7))])
                h_ready = layernorm(batch_major=True)

                kbd = Ring([Slot(sb(f"kbd{i}", [P, groups, BPT, P])) for i in range(2)])
                vbd = Ring([Slot(sb(f"vbd{i}", [P, BPT, groups, P])) for i in range(3)])
                for r in (kbd, vbd):
                    for s_ in r.slots:
                        s_.free = [pool(lambda e, s_=s_: e.memset(s_.ap[:], 0.0))]
                qn = Ring([Slot(sb(f"qn{i}", [P, D])) for i in range(2)])
                kn = Ring([Slot(sb(f"kn{i}", [P, kw])) for i in range(2)])
                vn = Ring([Slot(sb(f"vn{i}", [P, vw])) for i in range(2)])
                qTb = Ring([Slot(sb(f"qTb{i}", [P, AT, P])) for i in range(2)])
                pr = Ring([Slot(sb(f"pr{i}", [P, AH, S])) for i in range(2)])
                pTb = Ring([Slot(sb(f"pTb{i}", [P, AT, P])) for i in range(2)])
                oTb = Ring([Slot(sb(f"oTb{i}", [P, AT, P])) for i in range(2)])
                sq = sb("sq", [P, D])
                part_c = sb("part_c", [P, AH, DH])
                part_s = sb("part_s", [P, AH, DH])
                tiny = sb("tiny", [P, NT, 8, AH])
                banks_qkv = Ring([Slot(psum(i)) for i in range(3)])
                banks_t = Ring([Slot(psum(3)), Slot(psum(4))])
                banks_a = Ring([Slot(psum(5)), Slot(psum(6))])
                banks_o = Ring([Slot(psum(7))])
                banks_a.slots[1].free = list(ln_banks.slots[0].free)
                banks_o.slots[0].free = list(ln_banks.slots[1].free)
                Q, K, V, QT, KB, VB, PB, OB = ({} for _ in range(8))

                def normalise(i, src, dst, which, m):
                    ss, rs = tiny[:, i, 2 * which, :], tiny[:, i, 2 * which + 1, :]
                    heads = lambda ap: ap.rearrange("p (h d) -> p h d", d=DH)
                    hd = DH // 2
                    a1 = act(lambda e: e.activation(sq[:], src, ACT.Square), m, sq_free[0])
                    a2 = dve(lambda e: e.tensor_reduce(ss, heads(sq[:]), AX_X, ALU.add), a1)
                    sq_free[0] = a2
                    a3 = dve(lambda e: e.tensor_scalar(ss, ss, 1.0 / DH, 1e-6, ALU.mult, ALU.add), a2)
                    a4 = pool(lambda e: e.tensor_tensor(rs, ss, power[:], ALU.pow), a3)
                    bc = lambda ap, n=AH: ap.rearrange("p (o d) -> p o d", o=1).to_broadcast([P, n, ap.shape[-1]])
                    a5 = dve(lambda e: e.tensor_tensor(heads(dst.ap[:]), heads(src),
                                                       rs.rearrange("p (h o) -> p h o", o=1).to_broadcast([P, AH, DH]), ALU.mult),
                             a4, list(dst.free))
                    a6 = dve(lambda e: e.tensor_tensor(part_c[:], heads(dst.ap[:]), bc(cosg[:, which, :]), ALU.mult), a5, table_done, part_free[0])
                    a7 = pool(lambda e: e.tensor_tensor(part_s[:, :, 0:hd], heads(dst.ap[:])[:, :, hd:DH], bc(sing[:, which, 0:hd]), ALU.mult), a5, table_done, part_free[0])
                    a8 = pool(lambda e: e.tensor_tensor(part_s[:, :, hd:DH], heads(dst.ap[:])[:, :, 0:hd], bc(sing[:, which, hd:DH]), ALU.mult))
                    a9 = dve(lambda e: e.tensor_tensor(heads(dst.ap[:]), part_c[:], part_s[:], ALU.add), a6, a8)
                    part_free[0] = a9
                    return a5, a9

                sq_free, part_free = [None], [None]

                def project(i):
                    tok = slice(i * P, (i + 1) * P)
                    for which, (w_, n, ring, store, ready) in enumerate(
                            ((w_q, D, qn, Q, wq_ready), (w_k, kw, kn, K, wk_ready), (w_v, vw, vn, V, wv_ready))):
                        bank, dst = banks_qkv.take(), ring.take()
                        m = mm_group(bank.ap[:, 0:n], [(hT[:, k, tok], w_[:, k, :]) for k in range(KD)],
                                     (list(bank.free), ready, h_ready))
                        if normed and which < 2:
                            read, done = normalise(i, bank.ap[:, 0:n], dst, which, m)
                        elif normed:
                            read = done = act(lambda e, bank=bank, dst=dst: e.copy(dst.ap[:], bank.ap), m, list(dst.free))
                        else:
                            bv = bias[("bq", "bk", "bv")[which]]
                            read = done = dve(lambda e, bank=bank, dst=dst, n=n, bv=bv: e.tensor_tensor(
                                dst.ap[:], bank.ap[:, 0:n], bv[:], ALU.add), m, list(dst.free), table_done)
                        bank.free = [read]
                        store[i] = (dst, done)

                def spread(i):
                    qsrc, ready = Q[i]
                    bank, dst = banks_t.take(), qTb.take()
                    for t in range(AT):
                        step = lambda e, t=t: e.transpose(bank.ap[:, t * P:(t + 1) * P], qsrc.ap[:, t * P:(t + 1) * P], ident[:])
                        m = pe(step, ready, list(bank.free))
                    qsrc.free = [m]
                    done = act(lambda e: e.copy(dst.ap[:].rearrange("p t n -> p (t n)"), bank.ap), m, list(dst.free))
                    bank.free = [done]
                    QT[i] = (dst, done)
                    ksrc, ready = K[i]
                    kbank, kdst = banks_t.take(), kbd.take()
                    for t in range(groups):
                        step = lambda e, t=t: e.transpose(kbank.ap[:, t * P:(t + 1) * P], ksrc.ap[:, t * P:(t + 1) * P], ident[:])
                        m = pe(step, ready, list(kbank.free))
                    ksrc.free = [m]
                    marks = []
                    for j in range(HPT):
                        rows = slice(j * DH, (j + 1) * DH)
                        o = kdst.ap[rows, :, :, j * S:(j + 1) * S]
                        s_ = kbank.ap[rows, 0:groups * P].rearrange("p (t b s) -> p t b s", t=groups, s=S)
                        if j % 2:
                            marks.append(act(lambda e, o=o, s_=s_: e.copy(o, s_), m, list(kdst.free)))
                        else:
                            marks.append(dve(lambda e, o=o, s_=s_: e.tensor_copy(o, s_), m, list(kdst.free)))
                    kbank.free = marks
                    KB[i] = (kdst, marks)
                    vsrc, ready = V[i]
                    vdst = vbd.take()
                    marks = []
                    for b in range(BPT):
                        for j in range(HPT):
                            o = vdst.ap[j * S:(j + 1) * S, b, :, j * DH:(j + 1) * DH]
                            s_ = vsrc.ap[b * S:(b + 1) * S, :].rearrange("p (t j d) -> p t j d", t=groups, d=DH)
                            s_ = s_[:, :, j if normed else 0, :]
                            if j % 2:
                                marks.append(act(lambda e, o=o, s_=s_: e.copy(o, s_), ready, list(vdst.free)))
                            else:
                                marks.append(dve(lambda e, o=o, s_=s_: e.tensor_copy(o, s_), ready, list(vdst.free)))
                    vsrc.free = marks
                    VB[i] = (vdst, marks)

                def attend(i):
                    qt, q_ready = QT[i]
                    kb, k_ready = KB[i]
                    bank, dst = banks_a.take(), pr.take()
                    for b in range(BPT):
                        for t in range(AT):
                            m = mm_group(bank.ap[b * S:(b + 1) * S, t * P:(t + 1) * P],
                                         [(qt.ap[:, t, b * S:(b + 1) * S], kb.ap[:, t // tpg, b, :])],
                                         (list(bank.free), q_ready, k_ready))
                    qt.free = [m]
                    kb.free = [m]
                    mx, sm, rc = tiny[:, i, 4, :], tiny[:, i, 5, :], tiny[:, i, 6, :]
                    bc = lambda ap: ap.rearrange("p (h o) -> p h o", o=1).to_broadcast([P, AH, S])
                    sc = bank.ap.rearrange("p (h s) -> p h s", s=S)
                    c1 = dve(lambda e: e.tensor_tensor(dst.ap[:], sc, mask[:].rearrange("p (o s) -> p o s", o=1).to_broadcast([P, AH, S]),
                                                       ALU.add), m, table_done, list(dst.free))
                    bank.free = [c1]
                    c2 = dve(lambda e: e.tensor_reduce(mx, dst.ap[:], AX_X, ALU.max), c1)
                    c3 = pool(lambda e: e.tensor_tensor(dst.ap[:], dst.ap[:], bc(mx), ALU.subtract), c2)
                    c4 = act(lambda e: e.activation(dst.ap[:], dst.ap[:], ACT.Exp, scale=float(DH) ** -0.5), c3)
                    c5 = dve(lambda e: e.tensor_reduce(sm, dst.ap[:], AX_X, ALU.add), c4)
                    c6 = dve(lambda e: e.reciprocal(rc, sm), c5)
                    c7 = pool(lambda e: e.tensor_tensor(dst.ap[:], dst.ap[:], bc(rc), ALU.mult), c6)
                    PB[i] = (dst, c7)

                def mix(i):
                    src, ready = PB[i]
                    bank, dst = banks_t.take(), pTb.take()
                    for t in range(AT):
                        m = pe(lambda e, t=t: e.transpose(bank.ap[:, t * P:(t + 1) * P],
                                                          src.ap[:, t * HPT:(t + 1) * HPT, :], ident[:]),
                               ready, list(bank.free))
                    src.free = [m]
                    done = act(lambda e: e.copy(dst.ap[:].rearrange("p t n -> p (t n)"), bank.ap), m, list(dst.free))
                    bank.free = [done]
                    vb, v_ready = VB[i]
                    obank, odst = banks_a.take(), oTb.take()
                    for t in range(AT):
                        for b in range(BPT):
                            at = t * P + b * S
                            m = mm_group(obank.ap[:, at:at + S], [(vb.ap[:, b, t // tpg, :], dst.ap[:, t, b * S:(b + 1) * S])],
                                         (list(obank.free), v_ready, done))
                    vb.free = [m]
                    dst.free = [m]
                    odone = dve(lambda e: e.tensor_copy(
                        odst.ap[:].rearrange("p t (s b) -> p t b s", s=S),
                        obank.ap.rearrange("p (t b s) -> p t b s", t=AT, s=S)), m, list(odst.free))
                    obank.free = [odone]
                    OB[i] = (odst, odone)

                def output(i):
                    src, ready = OB[i]
                    bank = banks_o.take()
                    m = mm_group(bank.ap, [(src.ap[:, t, :], w_o[:, t, :]) for t in range(AT)],
                                 (list(bank.free), ready, wo_ready))
                    src.free = [m]
                    done = dve(lambda e: e.tensor_tensor(x[:, i, :], x[:, i, :], bank.ap, ALU.add), m)
                    bank.free = [done]
                    if not normed:
                        done = pool(lambda e: e.tensor_tensor(x[:, i, :], x[:, i, :], bias["bo"][:], ALU.add), done)
                    x_ready[i] = [done]

                for i in range(NT + 4):
                    if i < NT:
                        project(i)
                    if 0 <= i - 1 < NT:
                        spread(i - 1)
                    if 0 <= i - 2 < NT:
                        attend(i - 2)
                    if 0 <= i - 3 < NT:
                        mix(i - 3)
                    if 0 <= i - 4 < NT:
                        output(i - 4)
                for w_ in (wq, wk, wv, wo):
                    w_.free = [pe.now()]

        def hadamard_ffn(name):
            nonlocal ln_banks
            barrier()
            with ExitStack() as arena:
                def sb(n, shape, dt=F32):
                    return arena.enter_context(nc.sbuf_tensor(f"{name}_{n}", shape, dt))

                down = sb("down", [P, FC, D])
                z = sb("z", [P, FC, TOK])
                other = z[:, FC // 2:FC, :].rearrange("p a n -> p (a n)").rearrange("p (a n) -> p a n", a=FC)
                had = sb("had", [P, 2, P])
                su_ug = sb("su_ug", [P, KD])
                su_dp = sb("su_dp", [P, FC])
                ws_up = sb("ws_up", [P, FC])
                ws_gate = sb("ws_gate", [P, FC])
                ws_down = sb("ws_down", [P, D])
                su = sb("su", [P, FC])
                sg = Ring([Slot(sb(f"sg{i}", [P, TOK])) for i in range(2)])
                tabs = Slot(None, sem(f"s_{name}_tabs"))
                for dst, key in ((su_ug[:], "su_ug"), (had[:].rearrange("p a n -> p (a n)"), "had"), (su_dp[:], "su_dp"),
                                 (ws_up[:], "ws_up"), (ws_gate[:], "ws_gate")):
                    dma(tabs, dst, d[key], prior)
                tabs_ready = dma(tabs, ws_down[:], d["ws_down"].to_broadcast([P, D]), prior)
                scaled = dve(lambda e: e.tensor_tensor(su[:], ws_up[:], su_dp[:], ALU.mult), tabs_ready)

                ln_banks = Ring([Slot(psum(6)), Slot(psum(7))])
                h_ready = layernorm(scale=su_ug[:].rearrange("p (k o) -> p k o", o=1).to_broadcast([P, KD, P]))

                def butterfly(eng, src, dst, stride, after):
                    n = src.shape[1]
                    v = lambda ap: ap.rearrange("p (g two s) n -> p g two s n", two=2, s=stride)
                    marks = []
                    for g in range(n // (2 * stride)):
                        for o, op in ((0, ALU.add), (1, ALU.subtract)):
                            marks.append(eng(lambda e, g=g, o=o, op=op: e.tensor_tensor(
                                v(dst)[:, g, o, :, :], v(src)[:, g, 0, :, :], v(src)[:, g, 1, :, :], op), after))
                    return marks

                tmp = z[:, 0:2, :].rearrange("p a n -> p (a n)").rearrange("p (k n) -> p k n", k=KD)
                tmp2 = z[:, 2:4, :].rearrange("p a n -> p (a n)").rearrange("p (k n) -> p k n", k=KD)
                hx_ready = []
                banks_h = Ring([Slot(psum(i)) for i in range(4)])
                free = None
                for t in range(TOK // BANK):
                    cols_ = slice(t * BANK, (t + 1) * BANK)
                    got = []
                    for k in range(KD):
                        bank = banks_h.take()
                        m = mm_group(bank.ap, [(had[:, 0, :], hT[:, k, cols_])], (list(bank.free), h_ready, tabs_ready))
                        got.append(act(lambda e, k=k, bank=bank: e.copy(tmp[:, k, :], bank.ap), m, free))
                        bank.free = [got[-1]]
                    one = butterfly(dve, tmp, tmp2, 1, [got, free])
                    two = butterfly(dve, tmp2, hT[:, :, cols_], 2, [one, m])
                    free = [one, two]
                    hx_ready += two
                got = []
                banks_d = Ring([Slot(psum(4)), Slot(psum(5))])
                for q in range(FC // 4):
                    slot, ready = load_weights(d["wdT"][q], 4 * D)
                    for a in range(4):
                        bank = banks_d.take()
                        m = mm_group(bank.ap, [(had[:, 1, :], slot.ap[:, a * D:(a + 1) * D])], (list(bank.free), ready, tabs_ready))
                        got.append(act(lambda e, n=4 * q + a, bank=bank: e.copy(down[:, n, :], bank.ap), m))
                        bank.free = [got[-1]]
                    slot.free = [m]
                s1 = butterfly(pool, down[:], other, 1, got)
                s2 = butterfly(pool, other, down[:], 2, s1)
                s3 = butterfly(pool, down[:], other, 4, s2)
                s4 = butterfly(pool, other, down[:], 8, s3)

                pairs = Ring([Slot(psum(2 * i, 2)) for i in range(4)])
                for n, s_ in enumerate(pairs.slots):
                    s_.free = [[banks_h, banks_h, banks_d, ln_banks][n].slots[j + (2 if n == 1 else 0)].free for j in range(2)]
                    s_.free = [m for f in s_.free for m in f]
                z_ready = []
                for a in range(FC):
                    if a % 2 == 0:
                        slot, ready = load_weights(d["wug"][a // 2], 2 * 2 * KD * P)
                    wv_ = slot.ap[:, 0:4 * KD * P].rearrange("p (a u k n) -> p a u k n", a=2, u=2, k=KD)
                    gate, up = pairs.take(), pairs.take()
                    for u, unit in ((1, gate), (0, up)):
                        for t in range(2):
                            m = mm_group(unit.ap[:, t * BANK:(t + 1) * BANK],
                                         [(wv_[:, a % 2, u, k, :], hT[:, k, t * BANK:(t + 1) * BANK]) for k in range(KD)],
                                         (list(unit.free), ready, hx_ready))
                        if u == 1:
                            sgb = sg.take()
                            g1 = act(lambda e, a=a, sgb=sgb, unit=unit: e.activation(sgb.ap[:], unit.ap, ACT.Silu,
                                                                                     scale=ws_gate[:, a:a + 1]),
                                     m, list(sgb.free), tabs_ready)
                            unit.free = [g1]
                    z1 = dve(lambda e, a=a, sgb=sgb, up=up: e.scalar_tensor_tensor(
                        out=z[:, a, :], in0=up.ap, scalar=su[:, a:a + 1], in1=sgb.ap[:], op0=ALU.mult, op1=ALU.mult),
                        m, g1, scaled, s4 if a >= FC // 2 else [two])
                    up.free = [z1]
                    sgb.free = [z1]
                    z_ready.append(z1)
                    slot.free = [m]

                tail_banks = Ring([Slot(psum(i)) for i in range(8)])
                for n, s_ in enumerate(tail_banks.slots):
                    s_.free = list(pairs.slots[n // 2].free)
                for i in range(NT):
                    bank = tail_banks.take()
                    m = mm_group(bank.ap, [(z[:, a, i * P:(i + 1) * P], down[:, a, :]) for a in range(FC)],
                                 (list(bank.free), z_ready, s4))
                    buf = xn.take()
                    f1 = dve(lambda e, bank=bank, buf=buf: e.tensor_tensor(buf.ap[:], bank.ap, ws_down[:], ALU.mult), m, list(buf.free))
                    f2 = dve(lambda e, i=i, buf=buf: e.tensor_tensor(x[:, i, :], x[:, i, :], buf.ap[:], ALU.add), f1)
                    bank.free = [f1]
                    buf.free = [f2]
                    x_ready[i] = [f2]

        def experts(name):
            nonlocal ln_banks
            barrier()
            with ExitStack() as arena:
                def sb(n, shape, dt=F32):
                    return arena.enter_context(nc.sbuf_tensor(f"{name}_{n}", shape, dt))

                gate = sb("gate", [P, KD, NE])
                alpha = sb("alpha", [P, 1])
                iota = sb("iota", [P, NE])
                order = sb("order", [P, TOPK])
                tabs = Slot(None, sem(f"s_{name}_tabs"))
                dma(tabs, gate[:].rearrange("p k n -> p (k n)"), d["gate"], prior)
                dma(tabs, iota[:], d["iota"], prior)
                dma(tabs, order[:], d["order"], prior)
                tabs_ready = dma(tabs, alpha[:], d["alpha"].to_broadcast([P, 1]), prior)
                ln_banks = Ring([Slot(psum(6)), Slot(psum(7))])
                h_ready = layernorm()

                combine = sb("combine", [P, NT, NE])
                pb = sb("pb", [P, NT, NE])
                top = sb("top", [P, NT, TOPK])
                at = sb("at", [P, NT, TOPK], U32)
                atf = sb("atf", [P, NT, TOPK])
                rw = sb("rw", [P, NT, TOPK])
                act_ = sb("act_", [P, NT, TOPK])
                fb = sb("fb", [P, NT, TOPK])
                one = sb("one", [P, 10, NT])
                pick = sb("pick", [P, 2, NE])

                def chain(step, *after):
                    return dve(step, dve.now(), *after)

                def per_tile(ap, n):
                    return ap.rearrange("p (i o) -> p i o", o=1).to_broadcast([P, NT, n])

                bank = Slot(psum(0))
                for i in range(NT):
                    m = mm_group(bank.ap[:, i * NE:(i + 1) * NE],
                                 [(hT[:, k, i * P:(i + 1) * P], gate[:, k, :]) for k in range(KD)], (h_ready, tabs_ready))
                lg = bank.ap[:, 0:NT * NE].rearrange("p (i n) -> p i n", i=NT)
                chain(lambda e: e.tensor_reduce(one[:, 0, :], lg, AX_X, ALU.max), m)
                c1 = chain(lambda e: e.tensor_tensor(pb[:], lg, per_tile(one[:, 0, :], NE), ALU.subtract))
                c2 = act(lambda e: e.activation(pb[:], pb[:], ACT.Exp), c1)
                chain(lambda e: e.tensor_reduce(one[:, 1, :], pb[:], AX_X, ALU.add), c2)
                chain(lambda e: e.reciprocal(one[:, 2, :], one[:, 1, :]))
                chain(lambda e: e.tensor_tensor(pb[:], pb[:], per_tile(one[:, 2, :], NE), ALU.mult))
                for i in range(NT):
                    chain(lambda e, i=i: e.max(top[:, i, :], pb[:, i, :]))
                    chain(lambda e, i=i: e.max_index(at[:, i, :], top[:, i, :], pb[:, i, :]))
                chain(lambda e: e.tensor_copy(atf[:], at[:]))
                chain(lambda e: e.tensor_reduce(one[:, 3, :], top[:], AX_X, ALU.add))
                chain(lambda e: e.tensor_scalar(one[:, 3, :], one[:, 3, :], 1e-12, None, ALU.max))
                chain(lambda e: e.reciprocal(one[:, 3, :], one[:, 3, :]))
                chain(lambda e: e.tensor_tensor(rw[:], top[:], per_tile(one[:, 3, :], TOPK), ALU.mult))
                chain(lambda e: e.tensor_scalar(top[:], rw[:], alpha[:, 0:1], None, ALU.mult))
                chain(lambda e: e.tensor_scalar(act_[:], top[:], TAU, None, ALU.is_ge))
                chain(lambda e: e.tensor_reduce(one[:, 4, :], act_[:], AX_X, ALU.max))
                chain(lambda e: e.tensor_scalar(one[:, 4, :], one[:, 4, :], -1.0, 1.0, ALU.mult, ALU.add))
                chain(lambda e: e.tensor_reduce(one[:, 5, :], top[:], AX_X, ALU.max))
                chain(lambda e: e.tensor_tensor(fb[:], top[:], per_tile(one[:, 5, :], TOPK), ALU.is_equal))
                orders = order[:].rearrange("p (o n) -> p o n", o=1).to_broadcast([P, NT, TOPK])
                chain(lambda e: e.tensor_tensor(fb[:], fb[:], orders, ALU.mult))
                chain(lambda e: e.tensor_reduce(one[:, 6, :], fb[:], AX_X, ALU.max))
                chain(lambda e: e.tensor_tensor(fb[:], orders, per_tile(one[:, 6, :], TOPK), ALU.is_equal))
                chain(lambda e: e.tensor_tensor(fb[:], fb[:], per_tile(one[:, 4, :], TOPK), ALU.mult))
                chain(lambda e: e.tensor_tensor(act_[:], act_[:], fb[:], ALU.max))
                chain(lambda e: e.tensor_tensor(rw[:], rw[:], act_[:], ALU.mult))
                chain(lambda e: e.tensor_reduce(one[:, 7, :], rw[:], AX_X, ALU.add))
                chain(lambda e: e.tensor_scalar(one[:, 7, :], one[:, 7, :], 1e-12, None, ALU.max))
                chain(lambda e: e.reciprocal(one[:, 7, :], one[:, 7, :]))
                chain(lambda e: e.tensor_tensor(rw[:], rw[:], per_tile(one[:, 7, :], TOPK), ALU.mult))
                for i in range(NT):
                    for k in range(TOPK):
                        dst = combine[:, i, :] if k == 0 else pick[:, k % 2, :]
                        chain(lambda e, i=i, k=k, dst=dst: e.tensor_scalar(dst, iota[:], atf[:, i, k:k + 1], rw[:, i, k:k + 1],
                                                                           ALU.is_equal, ALU.mult))
                        if k:
                            chain(lambda e, i=i, k=k: e.tensor_tensor(combine[:, i, :], combine[:, i, :], pick[:, k % 2, :],
                                                                      ALU.add))
                routed = dve.now()

                z1b = Ring([Slot(sb(f"z1_{i}", [P, TOK])) for i in range(2)])
                z2b = Ring([Slot(sb(f"z2_{i}", [P, TOK])) for i in range(2)])
                sgb = Ring([Slot(sb(f"sg_{i}", [P, TOK])) for i in range(2)])
                units = Ring([Slot(psum(0, 2)), Slot(psum(2, 2)), Slot(psum(4, 2))])
                units.slots[0].free = [c1]
                outs = Ring([Slot(psum(6)), Slot(psum(7))])
                for s_, o in zip(outs.slots, ln_banks.slots):
                    s_.free = list(o.free)
                W, Z = {}, {}

                def hidden(e_):
                    slot, ready = W[e_]
                    wgu = slot.ap[:, 0:KD * 2 * EI].rearrange("p (k n) -> p k n", k=KD)

                    def product(col):
                        unit = units.take()
                        for t in range(2):
                            m = mm_group(unit.ap[:, t * BANK:(t + 1) * BANK],
                                         [(wgu[:, k, col:col + P], hT[:, k, t * BANK:(t + 1) * BANK]) for k in range(KD)],
                                         (list(unit.free), ready, h_ready))
                        return unit, m

                    g, m = product(0)
                    sg1 = sgb.take()
                    s1 = act(lambda e: e.activation(sg1.ap[:], g.ap, ACT.Silu), m, list(sg1.free))
                    g.free = [s1]
                    u, m = product(2 * P)
                    z1 = z1b.take()
                    s2 = dve(lambda e: e.tensor_tensor(z1.ap[:], u.ap, sg1.ap[:], ALU.mult), m, s1, list(z1.free))
                    u.free = [s2]
                    sg1.free = [s2]
                    gu, m = product(P)
                    sg2, z2 = sgb.take(), z2b.take()
                    s3 = act(lambda e: e.activation(sg2.ap[E2:P, :], gu.ap[0:E2, :], ACT.Silu), m, list(sg2.free))
                    s4 = dve(lambda e: e.tensor_tensor(z2.ap[E2:P, :], gu.ap[E2:P, :], sg2.ap[E2:P, :], ALU.mult), s3, list(z2.free))
                    gu.free = [s4]
                    sg2.free = [s4]
                    Z[e_] = (z1, z2, [s2, s4])

                def contribute(e_):
                    slot, ready = W[e_]
                    z1, z2, z_ready = Z[e_]
                    wd1 = slot.ap[:, KD * 2 * EI:KD * 2 * EI + D]
                    wd2 = slot.ap[E2:P, KD * 2 * EI + D:KD * 2 * EI + 2 * D]
                    for i in range(NT):
                        bank = outs.take()
                        m = mm_group(bank.ap, [(z1.ap[:, i * P:(i + 1) * P], wd1), (z2.ap[E2:P, i * P:(i + 1) * P], wd2)],
                                     (list(bank.free), z_ready))
                        done = dve(lambda e, i=i, bank=bank: e.scalar_tensor_tensor(
                            out=x[:, i, :], in0=bank.ap, scalar=combine[:, i, e_:e_ + 1], in1=x[:, i, :],
                            op0=ALU.mult, op1=ALU.add), m, routed, x_ready[i])
                        bank.free = [done]
                        x_ready[i] = [done]
                    slot.free = [m]
                    z1.free = [m]
                    z2.free = [m]

                W[0] = load_weights(d["experts"][0], SLOT)
                for e_ in range(NE + 1):
                    if e_ + 1 < NE:
                        W[e_ + 1] = load_weights(d["experts"][e_ + 1], SLOT)
                    if e_ < NE:
                        hidden(e_)
                    if e_ >= 1:
                        contribute(e_ - 1)

        ln_banks = None
        phases = [lambda: cross_attention("L0x", False), lambda: self_attention("L0a", KVH, False),
                  lambda: hadamard_ffn("L0f"), lambda: cross_attention("L1x", True),
                  lambda: self_attention("L1a", AT, True), lambda: experts("L1f")]
        for phase in phases[:last_phase]:
            prior = [q.now() for q in compute]
            phase()

        stored = Slot(None, sem("s_stored"))
        for i in range(NT):
            end = dma(stored, out[i * P:(i + 1) * P, :], x[:, i, :], x_ready[i])
        sp.quiet(None, end)

        with nc.Block() as block:
            @block.sync
            def _(eng):
                sp.emit(eng)

            @block.tensor
            def _(eng):
                pe.emit(eng)

            @block.scalar
            def _(eng):
                act.emit(eng)

            @block.vector
            def _(eng):
                dve.emit(eng)

            @block.gpsimd
            def _(eng):
                pool.emit(eng)


def constants():
    f = np.float32

    def rope(n, dim):
        inv = (f(1.0) / f(10000.0) ** (np.arange(0, dim, 2, dtype=f) / f(dim))).astype(f)
        return (np.arange(n, dtype=f)[:, None] * inv[None, :]).astype(f)

    c = {"ident": np.eye(P, dtype=f)}
    fr = np.repeat(rope(L, DC), 2, axis=1)
    sign = np.where(np.arange(DC) < DC // 2, f(-1), f(1))

    def by_key(t):
        return np.ascontiguousarray(np.stack([t[0:P], t[P:2 * P], np.broadcast_to(t[L - 1:L], (P, DC))], 1)).reshape(P, -1)

    c["kcos"] = by_key(np.cos(fr).astype(f))
    c["ksin"] = by_key((np.sin(fr) * sign).astype(f))
    fq = np.repeat(rope(S, DCQ), 2, axis=1)
    cq, sq = np.cos(fq).astype(f), np.sin(fq).astype(f)
    j = np.arange(DCQ)
    sp = sq[:, (j + DCQ // 2) % DCQ] * np.where(j < DCQ // 2, f(1), f(-1))
    c["cosq"] = np.ascontiguousarray(cq.T.reshape(QC, P, S).transpose(1, 0, 2)).reshape(P, -1).astype(f)
    c["sinq"] = np.ascontiguousarray(sp.T.reshape(QC, P, S).transpose(1, 0, 2)).reshape(P, -1).astype(f)
    fa = rope(S, DH)
    fa = np.concatenate([fa, fa], 1)
    sa = np.where(np.arange(DH) < DH // 2, f(-1), f(1))
    c["acos"] = np.tile(np.cos(fa).astype(f), (BPT, 1))
    c["asin"] = np.tile((np.sin(fa) * sa).astype(f), (BPT, 1))
    c["mask"] = np.tile(np.where(np.arange(S)[:, None] >= np.arange(S)[None, :], f(0), f(NEG)), (BPT, 1)).astype(f)
    h = np.ones((1, 1))
    while h.shape[0] < P:
        h = np.block([[h, h], [h, -h]])
    c["had"] = np.concatenate([h / np.sqrt(D), h / np.sqrt(INTER)], 1).astype(f)
    c["iota"] = np.broadcast_to(np.arange(NE, dtype=f), (P, NE)).copy()
    c["order"] = np.broadcast_to(np.arange(TOPK, 0, -1).astype(f), (P, TOPK)).copy()
    return c


def layout(i):
    f = np.float32
    c = np.ascontiguousarray
    o = {"x": i["x"].reshape(NT, BPT, S, D).transpose(0, 2, 1, 3).reshape(TOK, D), "ctx": i["ctx_512"]}

    def padded(a, rows=P):
        out = np.zeros((*a.shape[:-2], rows, a.shape[-1]), f)
        out[..., :a.shape[-2], :] = a
        return out

    def by_partition(a):
        n = a.shape[-1]
        return c(a.reshape(-1, P, n).transpose(1, 0, 2)).reshape(P, -1)

    for name, g in (("L0x", "L0_xattn_"), ("L1x", "L1_xattn_")):
        wq = i[g + "Wq"].reshape(XH, XK, D)
        kcq, qr, kr = i[g + "w_kc_q"], i[g + "W_qr"], i[g + "W_kr"]
        kr_t = padded(kr.transpose(0, 2, 1))
        wo_t = i[g + "Wo"].T.reshape(XH, XK, D)
        if name == "L0x":
            parts = [wq, kcq.transpose(0, 2, 1).reshape(XH, QC, P, XK).transpose(0, 2, 1, 3).reshape(XH, P, -1),
                     qr.reshape(XH, QC, P, RR).transpose(0, 2, 1, 3).reshape(XH, P, -1)]
        else:
            qr_t = qr.transpose(0, 2, 1)
            parts = [wq.transpose(0, 2, 1).reshape(XH, KD, P, XK).transpose(0, 2, 1, 3).reshape(XH, P, -1), kcq,
                     padded(np.concatenate([qr_t, qr_t[:, :, :DCQ // 2]], 2))]
        o[f"{name}_heads"] = c(np.concatenate([*parts, kr_t, i[g + "w_kc_kv"], wo_t], 2))

    a = "L0_attn_"
    rep = lambda w: np.repeat(w.reshape(-1, KVH, 1, DH), HPT, axis=2).reshape(w.shape[0], -1)
    o["L0a_wq"] = by_partition(i[a + "Wq"])
    o["L0a_wk"] = by_partition(rep(i[a + "Wk"]))
    o["L0a_wv"] = by_partition(i[a + "Wv"])
    o["L0a_wo"] = by_partition(i[a + "Wo"])
    o["L0a_bq"] = i[a + "bq"].reshape(1, -1)
    o["L0a_bk"] = rep(i[a + "bk"].reshape(1, -1))
    o["L0a_bv"] = i[a + "bv"].reshape(1, -1)
    o["L0a_bo"] = i[a + "bo"].reshape(1, -1)

    a = "L0_ffn_"
    o["su_ug"] = c(i[a + "SU_ug"].reshape(KD, P).T)
    o["su_dp"] = c(i[a + "SU_dp"].reshape(FC, P).T)
    o["ws_up"] = c(i[a + "Wscale_ug"][:INTER].reshape(FC, P).T)
    o["ws_gate"] = c(i[a + "Wscale_ug"][INTER:].reshape(FC, P).T)
    o["ws_down"] = i[a + "Wscale_dp"].reshape(1, -1)
    o["wdT"] = c(i[a + "W_down"].T.reshape(FC // 4, 4, P, D).transpose(0, 2, 1, 3)).reshape(FC // 4, P, -1)
    ug = np.stack([i[a + "W_up"], i[a + "W_gate"]])
    ug = ug.reshape(2, FC // 2, 2, P, KD, P).transpose(1, 5, 2, 0, 4, 3)
    o["wug"] = c(ug).reshape(FC // 2, P, -1)

    a = "L1_attn_"
    qkv = i[a + "w_qkv"]
    for n, key in enumerate(("wq", "wk", "wv")):
        o[f"L1a_{key}"] = by_partition(qkv[:, n * D:(n + 1) * D])
    o["L1a_wo"] = by_partition(i[a + "w_out"])
    for key, g in (("gq", "q_gamma"), ("gk", "k_gamma")):
        v = i[a + g].reshape(1, DH)
        o[key] = v
        o[f"{key}_roll"] = c(np.concatenate([v[:, DH // 2:], v[:, :DH // 2]], 1))

    a = "L1_ffn_"
    o["gate"] = by_partition(c(i[a + "gate_weight"].T))
    o["alpha"] = i[a + "layer_alpha"].reshape(1, 1)
    gu = i[a + "gate_up_proj"].transpose(0, 2, 1)
    gu = np.concatenate([gu[..., 0:P], gu[..., P:EI], gu[..., EI + P:2 * EI], gu[..., EI:EI + P]], 2)
    gu = gu.reshape(NE, KD, P, 2 * EI).transpose(0, 2, 1, 3).reshape(NE, P, -1)
    dn = i[a + "down_proj"].transpose(0, 2, 1)
    lo = np.zeros((NE, P, D), f)
    lo[:, E2:, :] = dn[:, P:EI, :]
    o["experts"] = c(np.concatenate([gu, dn[:, 0:P, :], lo], 2))
    o.update(constants())
    return {k: np.ascontiguousarray(v) for k, v in o.items()}


def unlayout(out):
    return np.asarray(out).reshape(NT, S, BPT, D).transpose(0, 2, 1, 3).reshape(B, S, D)


def kernel(**inputs):
    import concourse.bacc as bacc
    from concourse.bass_utils import run_bass_kernel_spmd

    arrays = layout({k: np.asarray(v) for k, v in inputs.items()})
    nc = bacc.Bacc("TRN2", target_bir_lowering=False, num_devices=1)
    d = {k: nc.dram_tensor(f"in_{k}", a.shape, mybir.dt.from_np(a.dtype), kind="ExternalInput").ap()
         for k, a in arrays.items()}
    out = nc.dram_tensor("out", (TOK, D), F32, kind="ExternalOutput").ap()
    build_kernel(nc, d, out)
    result = run_bass_kernel_spmd(nc, [{f"in_{k}": a for k, a in arrays.items()}], core_ids=[0])
    return unlayout(result.results[0]["out"])
```

```python
from contextlib import ExitStack

import numpy as np

import concourse.bass as bass
from concourse import mybir

ALU = mybir.AluOpType
ACT = mybir.ActivationFunctionType
F32 = mybir.dt.float32
F32R = mybir.dt.float32r
U32 = mybir.dt.uint32
AX_X = mybir.AxisListType.X

P = 128
BANK = 512
B, S, D = 32, 32, 512
TOK = B * S
NT = TOK // P
BPT = P // S
KD = D // P
L, DC = 257, 128
LC = (L - 1) // P
XH, XK, DCQ, RR = 16, 128, 384, 64
QC = DCQ // P
AH, DH = 16, 32
HPT = P // DH
AT = AH // HPT
KVH = 2
INTER = 2048
FC = INTER // P
NE, EI, TOPK, TAU = 32, 192, 8, 0.05
E2 = EI - P
NEG = -1e30

L0_PACK = {"wq": D, "kcq": QC * XK, "qr": QC * RR, "kr": DC}
L1_PACK = {"wq": KD * XK, "kcq": DCQ, "qr": DCQ + DCQ // 2, "kr": DC}
OUT_PACK = DC + D
OUT_HEADS = 4
SLOT = 2560
NSLOT = 3


def columns(pack):
    at, out = 0, {}
    for name, n in pack.items():
        out[name] = (at, at + n)
        at += n
    return out, at


class Engine:

    def __init__(self, sem):
        self.sem, self.count, self.steps = sem, 0, []

    def __call__(self, step, *after):
        self.count += 1
        self.steps.append((step, after, True))
        return (self.sem, self.count)

    def quiet(self, step, *after):
        self.steps.append((step, after, False))

    def now(self):
        return (self.sem, self.count)

    def emit(self, eng):
        reached = {}

        def wait(mark):
            if mark is None:
                return
            if isinstance(mark, list):
                for m in mark:
                    wait(m)
                return
            sem, value = mark
            if reached.get(id(sem), 0) < value:
                eng.wait_ge(sem, value)
                reached[id(sem)] = value

        for step, after, counted in self.steps:
            for mark in after:
                wait(mark)
            ins = step(eng) if step else None
            if counted:
                ins.then_inc(self.sem, 1)


class Slot:

    def __init__(self, ap, sem=None):
        self.ap, self.sem, self.landed = ap, sem, 0
        self.marks, self.taken = [], False

    @property
    def free(self):
        return self.marks

    @free.setter
    def free(self, marks):
        self.marks, self.taken = marks, False


class Ring:
    def __init__(self, slots):
        self.slots, self.n = slots, 0

    def take(self):
        slot = self.slots[self.n % len(self.slots)]
        self.n += 1
        assert not slot.taken, "taken again before its readers are known"
        slot.taken = True
        return slot


def build_kernel(nc, d, out, last_phase=6):
    with ExitStack() as ctx:
        def sem(name):
            return ctx.enter_context(nc.semaphore(name))

        def keep(name, shape, dt=F32):
            return ctx.enter_context(nc.sbuf_tensor(name, shape, dt))

        pe, act, dve, pool, sp = (Engine(sem(f"s_{n}")) for n in ("pe", "act", "dve", "pool", "sp"))
        compute = (pe, act, dve, pool)

        def dma(slot, dst, src, *after, queue=None):
            slot.landed += 16
            (queue or sp).quiet(lambda e: e.dma_start(dst, src).then_inc(slot.sem, 16), *after)
            return (slot.sem, slot.landed)

        def barrier():
            marks = [q.now() for q in compute]
            for q in compute:
                q.quiet(None, marks)
            return marks

        banks = ctx.enter_context(nc.psum_tensor("banks", [P, 8, BANK], F32))

        def psum(first, n=1):
            return banks[:, first:first + n, :].rearrange("p a n -> p (a n)")

        x = keep("x", [P, NT, D])
        xn = Ring([Slot(keep(f"xn{i}", [P, D])) for i in range(3)])
        stats = keep("stats", [P, NT, 6])
        moments = keep("moments", [P, NT, 2])
        rstd = keep("rstd", [P, NT])
        wring = Ring([Slot(keep(f"w{i}", [P, SLOT]), sem(f"s_w{i}")) for i in range(NSLOT)])
        ident = keep("ident", [P, P])
        kcos = keep("kcos", [P, 3, DC])
        ksin = keep("ksin", [P, 3, DC])

        power = keep("power", [P, AH])
        power_set = pool(lambda e: e.memset(power[:], -0.5))
        combine_rows = nc.dram_tensor("combine_rows", (NE, TOK), F32, kind="Internal").ap()
        const = Slot(None, sem("s_const"))
        xin = [Slot(None, sem(f"s_x{i}")) for i in range(NT)]
        x_ready, rstd_ready = [], [None] * NT
        for i in range(NT):
            x_ready.append([dma(xin[i], x[:, i, :], d["x"][i * P:(i + 1) * P, :])])
            if i == 1:
                dma(const, ident[:], d["ident"])
        dma(const, kcos[:].rearrange("p a n -> p (a n)"), d["kcos"])
        const_ready = dma(const, ksin[:].rearrange("p a n -> p (a n)"), d["ksin"])

        def load_weights(src, n):
            slot = wring.take()
            ready = dma(slot, slot.ap[:, 0:n], src[:, 0:n], list(slot.free))
            return slot, ready

        def x_written(i, mark, more=True):
            x_ready[i] = mark if isinstance(mark, list) else [mark]
            if more:
                m1 = dve(lambda e: e.bn_stats(stats[:, i, :], x[:, i, :]), x_ready[i])
                m2 = dve(lambda e: e.bn_aggr(moments[:, i, :], stats[:, i, :]), m1)
                m3 = dve(lambda e: e.tensor_scalar(rstd[:, i:i + 1], moments[:, i, 1:2], 1e-5, None, ALU.add), m2)
                rstd_ready[i] = pool(lambda e: e.tensor_tensor(rstd[:, i:i + 1], rstd[:, i:i + 1], power[:, 0:1], ALU.pow),
                                     m3, power_set)

        def normalise_tile(i):
            buf = xn.take()
            return buf, dve(lambda e: e.tensor_scalar(buf.ap[:], x[:, i, :], moments[:, i, 0:1], rstd[:, i:i + 1],
                                                      ALU.subtract, ALU.mult), rstd_ready[i], list(buf.free))

        def turn_tile(i, normalised, sink):
            buf, ready = normalised
            bank = ln_banks.take()
            for k in range(KD):
                step = lambda e, k=k: e.transpose(bank.ap[:, k * P:(k + 1) * P], buf.ap[:, k * P:(k + 1) * P], ident[:])
                if k < KD - 1:
                    pe.quiet(step, ready, const_ready, list(bank.free))
                else:
                    turned = pe(step)
            buf.free = [turned]
            done = sink(i, bank.ap.rearrange("p (k n) -> p k n", k=KD), turned)
            bank.free = done
            return done

        def layernorm(sink):
            ready, ahead = [], [normalise_tile(0)]
            for i in range(NT):
                if i + 1 < NT:
                    ahead.append(normalise_tile(i + 1))
                ready.append(turn_tile(i, ahead[i], sink))
            return ready

        def split(dst, src, after, hi_engine=None, lo_engine=None):
            hi_engine, lo_engine = hi_engine or act, lo_engine or dve
            copy = (lambda e: e.copy(dst[0], src)) if hi_engine is act else (lambda e: e.tensor_copy(dst[0], src))
            hi = hi_engine(copy, after)
            lo = lo_engine(lambda e: e.tensor_tensor(dst[1], src, dst[0], ALU.subtract), hi, after)
            return [hi, lo]

        def split_sink(dst):
            return lambda i, src, after: split(tuple(v[:, :, i * P:(i + 1) * P] for v in dst), src, after)

        def parts(w, m):
            return [(w[0], m[0]), (w[0], m[1]), (w[1], m[0])]

        def cut(pair, *index):
            return tuple(v[index] for v in pair)

        def mm_group(out_ap, pairs, after=()):
            for n, (w, m) in enumerate(pairs):
                step = lambda e, n=n, w=w, m=m: e.matmul(out_ap, w, m, start=n == 0, stop=n == len(pairs) - 1)
                if n < len(pairs) - 1:
                    pe.quiet(step, *(after if n == 0 else ()))
                else:
                    return pe(step, *(after if n == 0 else ()))

        def cross_attention(name, rope_q):
            nonlocal ln_banks
            barrier()
            cols, width = columns(L1_PACK if rope_q else L0_PACK)
            with ExitStack() as arena:
                def sb(n, shape, dt=F32):
                    return arena.enter_context(nc.sbuf_tensor(f"{name}_{n}", shape, dt))

                qT = sb("qT", [P, NT, XH, P])
                q_done = [[None, None] for _ in range(XH)]

                with ExitStack() as part:
                    def sbp(n, shape, dt=F32):
                        return part.enter_context(nc.sbuf_tensor(f"{name}_{n}", shape, dt))

                    hT = tuple(sbp(f"hT_{v}", [P, KD, TOK], F32R) for v in ("hi", "lo"))
                    ln_banks = Ring([Slot(psum(6)), Slot(psum(7))])
                    h_ready = layernorm(split_sink(hT))
                    small = Ring([Slot(psum(4)), Slot(psum(5))])
                    wide = Ring([Slot(psum(i)) for i in range(4)])

                    def tokens(k, t):
                        return cut(hT, slice(None), k, slice(t * BANK, (t + 1) * BANK))

                    def q_cols(h, t):
                        return qT[:, t * (NT // 2):(t + 1) * (NT // 2), h, :]

                    def tiles(ap):
                        return ap.rearrange("p (i n) -> p i n", n=P)

                    weights = {}

                    def fetch(h):
                        weights[h] = load_weights(d[f"{name}_heads"][h], width)

                    def w(h, key, rows=P):
                        a, b = cols[key]
                        return weights[h][0].ap[0:rows, a:b]

                    if not rope_q:
                        t1 = Ring([Slot(sbp(f"t1_{i}", [RR, XK])) for i in range(2)])
                        t2 = Ring([Slot(sbp(f"t2_{i}", [P, DC])) for i in range(2)])
                        mq = Ring([Slot(tuple(sbp(f"mq_{v}{i}", [P, KD * DC], F32R) for v in ("hi", "lo"))) for i in range(2)])
                        T1, T2, MQ = {}, {}, {}

                        def fold_1(h):
                            bank, dst = small.take(), t1.take()
                            kcq = w(h, "kcq").rearrange("p (c k) -> p c k", c=QC)
                            qr = w(h, "qr").rearrange("p (c r) -> p c r", c=QC)
                            m = mm_group(bank.ap[0:RR, 0:XK], [(qr[:, c, :], kcq[:, c, :]) for c in range(QC)],
                                         (list(bank.free), weights[h][1]))
                            T1[h] = (dst, act(lambda e: e.copy(dst.ap[:], bank.ap[0:RR, 0:XK]), m, list(dst.free)))
                            bank.free = [T1[h][1]]

                        def fold_2(h):
                            bank, dst = small.take(), t2.take()
                            src, ready = T1[h]
                            m = mm_group(bank.ap[:, 0:DC], [(src.ap[:], w(h, "kr", RR))], (list(bank.free), ready))
                            src.free = [m]
                            T2[h] = (dst, dve(lambda e: e.tensor_copy(dst.ap[:], bank.ap[:, 0:DC]), m, list(dst.free)))
                            bank.free = [T2[h][1]]

                        def fold_3(h):
                            bank, dst = small.take(), mq.take()
                            src, ready = T2[h]
                            for k in range(KD):
                                m = mm_group(bank.ap[:, k * P:(k + 1) * P], [(w(h, "wq")[:, k * P:(k + 1) * P], src.ap[:])],
                                             (list(bank.free), ready))
                            src.free = [m]
                            MQ[h] = (dst, split(cut(dst.ap, slice(None)), bank.ap, [m, list(dst.free)]))
                            bank.free = MQ[h][1]

                        def project(h):
                            src, ready = MQ[h]
                            for t in range(TOK // BANK):
                                bank = wide.take()
                                m = mm_group(bank.ap, [p for k in range(KD) for p in parts(
                                    cut(src.ap, slice(None), slice(k * DC, (k + 1) * DC)), tokens(k, t))],
                                             (list(bank.free), ready, h_ready))
                                q = (act if t else dve)
                                copy = (lambda e, t=t, bank=bank: e.copy(q_cols(h, t), tiles(bank.ap))) if t else \
                                    (lambda e, t=t, bank=bank: e.tensor_copy(q_cols(h, t), tiles(bank.ap)))
                                q_done[h][t] = q(copy, m)
                                bank.free = [q_done[h][t]]
                            src.free = [m]

                        for h in range(XH + 3):
                            if h < XH:
                                fetch(h)
                                fold_1(h)
                            if 0 <= h - 1 < XH:
                                fold_2(h - 1)
                            if 0 <= h - 2 < XH:
                                fold_3(h - 2)
                                weights[h - 2][0].free = [pe.now()]
                            if 0 <= h - 3 < XH:
                                project(h - 3)
                    else:
                        cosq = sbp("cosq", [P, QC, S])
                        sinq = sbp("sinq", [P, QC, S])
                        tabs = Slot(None, sem(f"s_{name}_tabs"))
                        dma(tabs, cosq[:].rearrange("p a n -> p (a n)"), d["cosq"], queue=act)
                        tabs_ready = dma(tabs, sinq[:].rearrange("p a n -> p (a n)"), d["sinq"], queue=act)
                        ubuf = Ring([Slot(sbp(f"u_{i}", [P, 2, QC, DC])) for i in range(2)])
                        qh = Ring([Slot(tuple(sbp(f"qh_{v}{i}", [P, BANK], F32R) for v in ("hi", "lo"))) for i in range(2)])
                        wsplit = Ring([Slot(tuple(sbp(f"ws_{v}{i}", [P, KD * XK + DCQ], F32R) for v in ("hi", "lo")))
                                       for i in range(2)])
                        WS = {}

                        def split_weights(h):
                            dst = wsplit.take()
                            WS[h] = (dst, split(cut(dst.ap, slice(None)), weights[h][0].ap[:, 0:KD * XK + DCQ],
                                                [weights[h][1], list(dst.free)], act, pool))

                        ybuf = Ring([Slot(sbp(f"y_{i}", [P, 2, BANK])) for i in range(4)])
                        U, QH, Y = {}, {}, {}

                        def fold_u(h):
                            dst = ubuf.take()
                            marks = []
                            for v in range(2):
                                bank = small.take()
                                for c in range(QC):
                                    at = c * P + v * (DCQ // 2)
                                    m = mm_group(bank.ap[:, c * P:(c + 1) * P],
                                                 [(w(h, "qr", RR)[:, at:at + P], w(h, "kr", RR))],
                                                 (list(bank.free), weights[h][1]))
                                marks.append(act(lambda e, v=v, bank=bank: e.copy(
                                    dst.ap[:, v, :, :].rearrange("p c n -> p (c n)"), bank.ap[:, 0:QC * P]), m, list(dst.free)))
                                bank.free = [marks[-1]]
                            U[h] = (dst, marks)

                        def query(h, t):
                            bank, dst = wide.take(), qh.take()
                            src, ready = WS[h]
                            m = mm_group(bank.ap, [p for k in range(KD) for p in parts(
                                cut(src.ap, slice(None), slice(k * XK, (k + 1) * XK)), tokens(k, t))],
                                         (list(bank.free), ready, h_ready))
                            QH[h, t] = (dst, split(cut(dst.ap, slice(None)), bank.ap, [m, list(dst.free)]))
                            bank.free = QH[h, t][1]

                        def widen(h, t, c):
                            bank, dst = wide.take(), ybuf.take()
                            src, ready = QH[h, t]
                            at = KD * XK + c * P
                            m = mm_group(bank.ap, parts(cut(WS[h][0].ap, slice(None), slice(at, at + P)),
                                                        cut(src.ap, slice(None))), (list(bank.free), ready))
                            src.free = [m]
                            if t == 1 and c == QC - 1:
                                WS[h][0].free = [m]
                            marks = []
                            for v, tab in enumerate((cosq, sinq)):
                                table = tab[:, c, :].rearrange("p (i s b) -> p i s b", i=1, b=1).to_broadcast([P, BANK // P, S, BPT])
                                marks.append(dve(lambda e, v=v, table=table: e.tensor_tensor(
                                    dst.ap[:, v, :].rearrange("p (i s b) -> p i s b", s=S, b=BPT),
                                    bank.ap.rearrange("p (i s b) -> p i s b", s=S, b=BPT), table, ALU.mult),
                                    m, tabs_ready, list(dst.free)))
                            bank.free = marks
                            Y[h, t, c] = (dst, marks)

                        acc = {}

                        def narrow(h, t, c):
                            if c == 0:
                                acc[h, t] = wide2.take()
                            bank = acc[h, t]
                            src, ready = Y[h, t, c]
                            for v in range(2):
                                step = lambda e, v=v: e.matmul(bank.ap, U[h][0].ap[:, v, c, :], src.ap[:, v, :],
                                                               start=c == 0 and v == 0, stop=c == QC - 1 and v == 1)
                                if v == 0:
                                    pe.quiet(step, ready, U[h][1], list(bank.free) if c == 0 else None)
                                else:
                                    m = pe(step)
                            src.free = [m]
                            if c == QC - 1:
                                q_done[h][t] = act(lambda e: e.copy(q_cols(h, t), tiles(bank.ap)), m)
                                bank.free = [q_done[h][t]]
                                if t == 1:
                                    U[h][0].free = [m]
                                    weights[h][0].free = [m, WS[h][1]]

                        wide = Ring([Slot(psum(i)) for i in range(4)])
                        wide2 = Ring([Slot(psum(6)), Slot(psum(7))])
                        for s_, slot in zip(wide2.slots, ln_banks.slots):
                            s_.free = list(slot.free)
                        items = [(h, t, c) for h in range(XH) for t in range(2) for c in range(QC)]
                        LAG = 2
                        fetch(0)
                        split_weights(0)
                        query(0, 0)
                        for n in range(len(items) + LAG):
                            if n < len(items):
                                h, t, c = items[n]
                                if c == 0 and t == 0:
                                    fold_u(h)
                                    if h + 1 < XH:
                                        fetch(h + 1)
                                        split_weights(h + 1)
                                if c == 1:
                                    nxt = (h, 1) if t == 0 else (h + 1, 0)
                                    if nxt[0] < XH:
                                        query(*nxt)
                                widen(h, t, c)
                            if n >= LAG:
                                narrow(*items[n - LAG])
                last = barrier()

                wn = sb("wn", [P, XH, D])
                wn_done = []
                fold_banks = Ring([Slot(psum(4)), Slot(psum(5))])
                for h in range(XH):
                    if h % OUT_HEADS == 0:
                        slot, ready = load_weights(d[f"{name}_out"][h // OUT_HEADS], OUT_HEADS * OUT_PACK)
                    at = (h % OUT_HEADS) * OUT_PACK
                    bank = fold_banks.take()
                    m = mm_group(bank.ap, [(slot.ap[:, at:at + DC], slot.ap[:, at + DC:at + OUT_PACK])], (list(bank.free), ready))
                    wn_done.append(act(lambda e, h=h, bank=bank: e.copy(wn[:, h, :], bank.ap), m))
                    bank.free = [wn_done[-1]]
                    slot.free = [m]
                craw = Ring([Slot(sb(f"craw{i}", [P, 3, DC]), sem(f"s_{name}_c{i}")) for i in range(2)])
                rot = sb("rot", [P, 3, DC])
                kv = Ring([Slot(sb(f"kv{i}", [P, 3, DC])) for i in range(5)])
                kvT = Ring([Slot(sb(f"kvT{i}", [P, LC * P + S])) for i in range(4)])
                prob = Ring([Slot(sb(f"prob{i}", [P, 4, LC * P])) for i in range(3)])
                pT = Ring([Slot(sb(f"pT{i}", [P, LC, BANK])) for i in range(2)])
                small4 = Ring([Slot(sb(f"small4_{i}", [P, 5, 4])) for i in range(4)])
                s_banks = Ring([Slot(psum(i)) for i in range(3)])
                t_banks = Ring([Slot(psum(4, 2))])
                t_banks.slots[0].free = wn_done[-2:]
                c_bank = Slot(psum(6))
                k_bank = Slot(psum(7))
                o_bank = Slot(psum(3))
                KV, KT, PR, PT = {}, {}, {}, {}

                def of_batch(b, head=0, n=XH):
                    cols = qT[:, b // BPT, :, :].rearrange("p h n -> p (h n)")
                    return cols[:, head * P + b % BPT:(head + n) * P:BPT]
                rot_free = [None]

                def keys(b):
                    raw, dst = craw.take(), kv.take()
                    for c in range(LC):
                        dma(raw, raw.ap[:, c, :], d["ctx"][b, c * P:(c + 1) * P, :], list(raw.free), last)
                    ready = dma(raw, raw.ap[:, LC, :], d["ctx"][b, L - 1:L, :].to_broadcast([P, DC]))
                    hw = DC // 2
                    m1 = pool(lambda e: e.tensor_tensor(dst.ap[:], raw.ap[:], kcos[:], ALU.mult), ready, list(dst.free), const_ready)
                    m2 = pool(lambda e: e.tensor_tensor(rot[:, :, 0:hw], raw.ap[:, :, hw:DC], ksin[:, :, 0:hw], ALU.mult), rot_free[0])
                    m3 = pool(lambda e: e.tensor_tensor(rot[:, :, hw:DC], raw.ap[:, :, 0:hw], ksin[:, :, hw:DC], ALU.mult))
                    m4 = pool(lambda e: e.tensor_tensor(dst.ap[:], dst.ap[:], rot[:], ALU.add), m1, m2, m3)
                    raw.free = [m3]
                    rot_free[0] = m4
                    m5 = pool(lambda e: e.tensor_tensor(dst.ap[:, 0:LC, :], dst.ap[:, 0:LC, :],
                                                        dst.ap[:, LC:LC + 1, :].to_broadcast([P, LC, DC]), ALU.subtract), m4)
                    KV[b] = (dst, m5)

                def keys_T(b):
                    src, ready = KV[b]
                    dst = kvT.take()
                    for c in range(LC):
                        pe.quiet(lambda e, c=c: e.transpose(k_bank.ap[:, c * P:(c + 1) * P], src.ap[:, c, :], ident[:]),
                                 ready, list(k_bank.free))
                    m = pe(lambda e: e.transpose(k_bank.ap[:, LC * P:LC * P + S], src.ap[0:S, LC, :], ident[0:S, 0:S]))
                    done = act(lambda e: e.copy(dst.ap[:], k_bank.ap[:, 0:LC * P + S]), m, list(dst.free))
                    k_bank.free = [done]
                    KT[b] = (dst, done)

                def scores(b):
                    kt, ready = KT[b]
                    dst, small = prob.take(), small4.take()
                    mx, neg, sums, tail, rec = (small.ap[:, n, :] for n in range(5))
                    got = []
                    for g in range(2):
                        bank = s_banks.take()
                        for r in range(2):
                            m = mm_group(bank.ap[:, r * 256:(r + 1) * 256],
                                         [(of_batch(b, 8 * g + 4 * r, 4), kt.ap[:, 0:LC * P])], (list(bank.free), ready))
                        got.append((bank, dve(lambda e, g=g, bank=bank: e.tensor_reduce(
                            mx[:, 2 * g:2 * g + 2], bank.ap.rearrange("p (r n) -> p r n", r=2), AX_X, ALU.max),
                            m, list(small.free))))
                    m2 = dve(lambda e: e.tensor_scalar(neg, mx, -1.0, 0.0, ALU.mult, ALU.min), [m for _, m in got])
                    for r in range(4):
                        bank = got[r // 2][0]
                        m3 = act(lambda e, r=r, bank=bank: e.activation(
                            dst.ap[:, r, :], bank.ap[:, (r % 2) * 256:(r % 2 + 1) * 256], ACT.Exp, bias=neg[:, r:r + 1],
                            accum_out=sums[:, r:r + 1]), m2, list(dst.free))
                        if r % 2:
                            bank.free = [m3]
                    m4 = act(lambda e: e.activation(tail, neg, ACT.Exp))
                    m5 = dve(lambda e: e.tensor_tensor(sums, sums, tail, ALU.add), m4)
                    m6 = dve(lambda e: e.reciprocal(rec, sums), m5)
                    for r in range(4):
                        m7 = dve(lambda e, r=r: e.tensor_scalar(dst.ap[:, r, :], dst.ap[:, r, :], rec[:, r:r + 1], None, ALU.mult), m6)
                    small.free = [m7]
                    PR[b] = (dst, m7)

                def turn(b):
                    src, ready = PR[b]
                    bank, dst = t_banks.take(), pT.take()
                    for c in range(LC):
                        for r in range(4):
                            step = lambda e, c=c, r=r: e.transpose(bank.ap[:, c * BANK + r * P:c * BANK + (r + 1) * P],
                                                                   src.ap[:, r, c * P:(c + 1) * P], ident[:])
                            if r < 3:
                                pe.quiet(step, ready, list(bank.free))
                            else:
                                m = pe(step)
                        if c == 0:
                            d0 = act(lambda e: e.copy(dst.ap[:, 0, :], bank.ap[:, 0:BANK]), m, list(dst.free))
                        else:
                            d1 = dve(lambda e: e.tensor_copy(dst.ap[:, 1, :], bank.ap[:, BANK:2 * BANK]), m, list(dst.free))
                    src.free = [m]
                    bank.free = [d0, d1]
                    PT[b] = (dst, [d0, d1])

                ctx_done = {}

                def values(b):
                    src, ready = PT[b]
                    v, _ = KV[b]
                    kt, _ = KT[b]
                    m = mm_group(c_bank.ap, [(v.ap[:, c, :], src.ap[:, c, :]) for c in range(LC)], (list(c_bank.free), ready))
                    src.free = [m]
                    v.free = [m]
                    ctx_done[b] = dve(lambda e: e.tensor_scalar(
                        of_batch(b), c_bank.ap,
                        kt.ap[:, LC * P:LC * P + 1], None, ALU.add), m)
                    c_bank.free = [ctx_done[b]]
                    kt.free = [ctx_done[b]]

                def output(i, part):
                    for h in range(4 * part, 4 * part + 4):
                        step = lambda e, h=h: e.matmul(o_bank.ap, qT[:, i, h, :], wn[:, h, :], start=h == 0, stop=h == XH - 1)
                        waits = (list(o_bank.free) if h == 0 else None, ctx_done[i * BPT + BPT - 1], wn_done)
                        if h < XH - 1:
                            pe.quiet(step, *waits)
                        else:
                            m = pe(step, *waits)
                            done = dve(lambda e: e.tensor_tensor(x[:, i, :], x[:, i, :], o_bank.ap, ALU.add), m)
                            o_bank.free = [done]
                            x_written(i, done)

                LAG_TURN, LAG_VALUES = 2, 3
                keys(0)
                keys(1)
                keys_T(0)
                for b in range(B + LAG_VALUES + BPT):
                    if b < B:
                        scores(b)
                    if 0 <= b - LAG_VALUES < B:
                        values(b - LAG_VALUES)
                    if b + 2 < B:
                        keys(b + 2)
                    if b + 1 < B:
                        keys_T(b + 1)
                    if 0 <= b - LAG_TURN < B:
                        turn(b - LAG_TURN)
                    if b >= LAG_VALUES + BPT:
                        output((b - LAG_VALUES) // BPT - 1, (b - LAG_VALUES) % BPT)

        def self_attention(name, groups, normed):
            nonlocal ln_banks
            start = barrier()
            tpg = AT // groups
            kw = groups * P
            vw = groups * P if normed else groups * DH
            with ExitStack() as arena:
                def sb(n, shape, dt=F32):
                    return arena.enter_context(nc.sbuf_tensor(f"{name}_{n}", shape, dt))

                mask = sb("mask", [P, S])
                tabs = Slot(None, sem(f"s_{name}_tabs"))
                dma(tabs, mask[:], d["mask"], queue=act)
                if normed:
                    cosg, sing = sb("cosg", [P, 2, DH]), sb("sing", [P, 2, DH])
                    gam = sb("gam", [P, 4, DH])
                    for n, g in enumerate(("gq", "gq_roll", "gk", "gk_roll")):
                        dma(tabs, gam[:, n, :], d[g].to_broadcast([P, DH]), queue=act)
                    for n in range(2):
                        dma(tabs, cosg[:, n, :], d["acos"], queue=act)
                        tabs_ready = dma(tabs, sing[:, n, :], d["asin"], queue=act)
                    g1 = dve(lambda e: e.tensor_tensor(cosg[:], cosg[:], gam[:, 0::2, :], ALU.mult), tabs_ready)
                    g2 = dve(lambda e: e.tensor_tensor(sing[:], sing[:], gam[:, 1::2, :], ALU.mult), tabs_ready)
                    table_done = [g1, g2]
                else:
                    bias = {}
                    for key, n in (("bq", D), ("bk", kw), ("bv", vw), ("bo", D)):
                        bias[key] = sb(key, [P, n])
                        tabs_ready = dma(tabs, bias[key][:], d[f"{name}_{key}"].to_broadcast([P, n]), queue=act)
                    table_done = [tabs_ready]

                wq, wq_ready = load_weights(d[f"{name}_wq"], KD * D)
                wk, wk_ready = load_weights(d[f"{name}_wk"], KD * kw)
                wv, wv_ready = load_weights(d[f"{name}_wv"], KD * vw)
                w_q, w_k, w_v = (tuple(sb(f"{key}_{v}", [P, KD, n], F32R) for v in ("hi", "lo"))
                                 for key, n in (("wq", D), ("wk", kw), ("wv", vw)))
                w_ready = []
                for dst, slot, ready, n in ((w_q, wq, wq_ready, D), (w_k, wk, wk_ready, kw), (w_v, wv, wv_ready, vw)):
                    w_ready.append(split(cut(dst, slice(None)), slot.ap[:, 0:KD * n].rearrange("p (k n) -> p k n", k=KD),
                                         [ready], act, pool if slot is wk else dve))
                    slot.free = w_ready[-1]
                wo, wo_ready = load_weights(d[f"{name}_wo"], KD * D)
                w_o = wo.ap[:, 0:KD * D].rearrange("p (k n) -> p k n", k=KD)

                banks_o = ln_banks = Ring([Slot(psum(7))])
                hT = Ring([Slot(tuple(sb(f"hT_{v}{i}", [P, KD, P], F32R) for v in ("hi", "lo"))) for i in range(3)])
                H = {}

                NORM = {}

                def turn_input(i):
                    dst = hT.take()

                    def sink(i, src, after):
                        b_major = tuple(v[:, :, :].rearrange("p k (b s) -> p k b s", s=S) for v in dst.ap)
                        return split(b_major, src.rearrange("p k (s b) -> p k b s", s=S), [after, list(dst.free)])

                    H[i] = (dst, turn_tile(i, NORM[i], sink))

                kbd = Ring([Slot(sb(f"kbd{i}", [P, groups, BPT, P])) for i in range(2)])
                vbd = Ring([Slot(sb(f"vbd{i}", [P, BPT, groups, P])) for i in range(3)])
                for r in (kbd, vbd):
                    for s_ in r.slots:
                        s_.free = [pool(lambda e, s_=s_: e.memset(s_.ap[:], 0.0))]
                qn = Ring([Slot(sb(f"qn{i}", [P, D])) for i in range(3)])
                kn = Ring([Slot(sb(f"kn{i}", [P, kw])) for i in range(3)])
                vn = Ring([Slot(sb(f"vn{i}", [P, vw])) for i in range(3)])
                qTb = Ring([Slot(sb(f"qTb{i}", [P, AT, P])) for i in range(2)])
                pr = Ring([Slot(sb(f"pr{i}", [P, AH, S])) for i in range(2)])
                pTb = Ring([Slot(sb(f"pTb{i}", [P, AT, P])) for i in range(2)])
                oTb = Ring([Slot(sb(f"oTb{i}", [P, AT, P])) for i in range(2)])
                if normed:
                    sq, part_c, part_s = ([sb(f"{key}{w}", [P, *shape]) for w in range(2)]
                                          for key, shape in (("sq", (D,)), ("part_c", (AH, DH)), ("part_s", (AH, DH))))
                tiny = sb("tiny", [P, NT, 8, AH])
                banks_qkv = Ring([Slot(psum(i)) for i in range(3)])
                banks_t = Ring([Slot(psum(3)), Slot(psum(4))])
                banks_a = Ring([Slot(psum(5)), Slot(psum(6))])
                Q, K, V, QT, KB, VB, PB, OB, EX, PTB, PJ = ({} for _ in range(11))

                heads = lambda ap: ap.rearrange("p (h d) -> p h d", d=DH)

                def head_norms(i, todo):
                    ss, rs = ([tiny[:, i, 2 * w + n, :] for w in range(2)] for n in range(2))
                    m = {}
                    for w, (src, dst, ready) in enumerate(todo):
                        m[w] = act(lambda e, w=w, src=src: e.activation(sq[w][:], src, ACT.Square), ready, sq_free[w])
                    for w in range(2):
                        m[w] = dve(lambda e, w=w: e.tensor_reduce(ss[w], heads(sq[w][:]), AX_X, ALU.add), m[w])
                        sq_free[w] = m[w]
                    for w in range(2):
                        m[w] = dve(lambda e, w=w: e.tensor_scalar(ss[w], ss[w], 1.0 / DH, 1e-6, ALU.mult, ALU.add), m[w])
                        m[w] = pool(lambda e, w=w: e.tensor_tensor(rs[w], ss[w], power[:], ALU.pow), m[w])
                    return m

                def normalise(i, todo, m):
                    across = lambda ap: ap.rearrange("p (o d) -> p o d", o=1).to_broadcast([P, AH, ap.shape[-1]])
                    hd = DH // 2
                    rs = [tiny[:, i, 2 * w + 1, :] for w in range(2)]
                    read, cosd, sind, out_ = {}, {}, {}, {}
                    for w, (src, dst, _) in enumerate(todo):
                        read[w] = dve(lambda e, w=w, src=src, dst=dst: e.tensor_tensor(
                            heads(dst.ap[:]), heads(src), rs[w].rearrange("p (h o) -> p h o", o=1).to_broadcast([P, AH, DH]),
                            ALU.mult), m[w], list(dst.free))
                    for w, (src, dst, _) in enumerate(todo):
                        cosd[w] = dve(lambda e, w=w, dst=dst: e.tensor_tensor(
                            part_c[w][:], heads(dst.ap[:]), across(cosg[:, w, :]), ALU.mult), read[w], table_done, part_free[w])
                        for lo, hi in ((0, hd), (hd, 0)):
                            sind[w] = pool(lambda e, w=w, dst=dst, lo=lo, hi=hi: e.tensor_tensor(
                                part_s[w][:, :, lo:lo + hd], heads(dst.ap[:])[:, :, hi:hi + hd],
                                across(sing[:, w, lo:lo + hd]), ALU.mult), read[w], table_done, part_free[w])
                    for w, (src, dst, _) in enumerate(todo):
                        out_[w] = dve(lambda e, w=w, dst=dst: e.tensor_tensor(heads(dst.ap[:]), part_c[w][:], part_s[w][:], ALU.add),
                                      cosd[w], sind[w])
                        part_free[w] = out_[w]
                    return read, out_

                sq_free, part_free = [None, None], [None, None]

                def project(i):
                    src, h_ready = H[i]
                    got = []
                    for which, (w_, n, ring, ready) in enumerate(
                            ((w_q, D, qn, w_ready[0]), (w_k, kw, kn, w_ready[1]), (w_v, vw, vn, w_ready[2]))):
                        bank, dst = banks_qkv.take(), ring.take()
                        m = mm_group(bank.ap[:, 0:n], [p for k in range(KD) for p in parts(
                            cut(src.ap, slice(None), k, slice(None)), cut(w_, slice(None), k, slice(None)))],
                                     (list(bank.free), ready, h_ready))
                        if not normed:
                            bv = bias[("bq", "bk", "bv")[which]]
                            done = dve(lambda e, bank=bank, dst=dst, n=n, bv=bv: e.tensor_tensor(
                                dst.ap[:], bank.ap[:, 0:n], bv[:], ALU.add), m, list(dst.free), table_done)
                        if not normed:
                            bank.free = [done]
                            (Q, K, V)[which][i] = (dst, done)
                        got.append((bank, dst, m))
                    src.free = [m]
                    if normed:
                        todo = [(bank.ap, dst, m) for bank, dst, m in got[:2]]
                        PJ[i] = (got, todo, head_norms(i, todo))
                        bank, dst, m = got[2]
                        done = act(lambda e: e.copy(dst.ap[:], bank.ap), m, list(dst.free))
                        bank.free = [done]
                        V[i] = (dst, done)

                def finish_projection(i):
                    if normed:
                        got, todo, norms = PJ[i]
                        read, done = normalise(i, todo, norms)
                        for w in range(2):
                            got[w][0].free = [read[w]]
                            (Q, K)[w][i] = (got[w][1], done[w])

                def spread(i):
                    qsrc, ready = Q[i]
                    bank, dst = banks_t.take(), qTb.take()
                    for t in range(AT):
                        step = lambda e, t=t: e.transpose(bank.ap[:, t * P:(t + 1) * P], qsrc.ap[:, t * P:(t + 1) * P], ident[:])
                        m = pe(step, ready, list(bank.free))
                    qsrc.free = [m]
                    done = act(lambda e: e.copy(dst.ap[:].rearrange("p t n -> p (t n)"), bank.ap), m, list(dst.free))
                    bank.free = [done]
                    QT[i] = (dst, done)
                    ksrc, ready = K[i]
                    kbank, kdst = banks_t.take(), kbd.take()
                    for t in range(groups):
                        step = lambda e, t=t: e.transpose(kbank.ap[:, t * P:(t + 1) * P], ksrc.ap[:, t * P:(t + 1) * P], ident[:])
                        m = pe(step, ready, list(kbank.free))
                    ksrc.free = [m]
                    marks = []
                    for j in range(HPT):
                        rows = slice(j * DH, (j + 1) * DH)
                        o = kdst.ap[rows, :, :, j * S:(j + 1) * S]
                        s_ = kbank.ap[rows, 0:groups * P].rearrange("p (t b s) -> p t b s", t=groups, s=S)
                        if j % 2:
                            marks.append(act(lambda e, o=o, s_=s_: e.copy(o, s_), m, list(kdst.free)))
                        else:
                            marks.append(dve(lambda e, o=o, s_=s_: e.tensor_copy(o, s_), m, list(kdst.free)))
                    kbank.free = marks
                    KB[i] = (kdst, marks)
                    vsrc, ready = V[i]
                    vdst = vbd.take()
                    marks = []
                    for b in range(BPT):
                        for j in range(HPT):
                            o = vdst.ap[j * S:(j + 1) * S, b, :, j * DH:(j + 1) * DH]
                            s_ = vsrc.ap[b * S:(b + 1) * S, :].rearrange("p (t j d) -> p t j d", t=groups, d=DH)
                            s_ = s_[:, :, j if normed else 0, :]
                            if j % 2:
                                marks.append(act(lambda e, o=o, s_=s_: e.copy(o, s_), ready, list(vdst.free)))
                            else:
                                marks.append(dve(lambda e, o=o, s_=s_: e.tensor_copy(o, s_), ready, list(vdst.free)))
                    vsrc.free = marks
                    VB[i] = (vdst, marks)

                def attend(i):
                    qt, q_ready = QT[i]
                    kb, k_ready = KB[i]
                    bank, dst = banks_a.take(), pr.take()
                    for b in range(BPT):
                        for t in range(AT):
                            m = mm_group(bank.ap[b * S:(b + 1) * S, t * P:(t + 1) * P],
                                         [(qt.ap[:, t, b * S:(b + 1) * S], kb.ap[:, t // tpg, b, :])],
                                         (list(bank.free), q_ready, k_ready))
                    qt.free = [m]
                    kb.free = [m]
                    mx = tiny[:, i, 4, :]
                    bc = lambda ap: ap.rearrange("p (h o) -> p h o", o=1).to_broadcast([P, AH, S])
                    sc = bank.ap.rearrange("p (h s) -> p h s", s=S)
                    c1 = dve(lambda e: e.tensor_tensor(dst.ap[:], sc, mask[:].rearrange("p (o s) -> p o s", o=1).to_broadcast([P, AH, S]),
                                                       ALU.add), m, table_done, list(dst.free))
                    bank.free = [c1]
                    c2 = dve(lambda e: e.tensor_reduce(mx, dst.ap[:], AX_X, ALU.max), c1)
                    c3 = pool(lambda e: e.tensor_tensor(dst.ap[:], dst.ap[:], bc(mx), ALU.subtract), c2)
                    c4 = act(lambda e: e.activation(dst.ap[:], dst.ap[:], ACT.Exp, scale=float(DH) ** -0.5), c3)
                    EX[i] = (dst, c4)

                def weigh(i):
                    dst, c4 = EX[i]
                    sm, rc = tiny[:, i, 5, :], tiny[:, i, 6, :]
                    bc = lambda ap: ap.rearrange("p (h o) -> p h o", o=1).to_broadcast([P, AH, S])
                    c5 = dve(lambda e: e.tensor_reduce(sm, dst.ap[:], AX_X, ALU.add), c4)
                    c6 = dve(lambda e: e.reciprocal(rc, sm), c5)
                    c7 = pool(lambda e: e.tensor_tensor(dst.ap[:], dst.ap[:], bc(rc), ALU.mult), c6)
                    PB[i] = (dst, c7)

                def turn_weights(i):
                    src, ready = PB[i]
                    bank, dst = banks_t.take(), pTb.take()
                    for t in range(AT):
                        m = pe(lambda e, t=t: e.transpose(bank.ap[:, t * P:(t + 1) * P],
                                                          src.ap[:, t * HPT:(t + 1) * HPT, :], ident[:]),
                               ready, list(bank.free))
                    src.free = [m]
                    done = act(lambda e: e.copy(dst.ap[:].rearrange("p t n -> p (t n)"), bank.ap), m, list(dst.free))
                    bank.free = [done]
                    PTB[i] = (dst, done)

                def mix(i):
                    dst, done = PTB[i]
                    vb, v_ready = VB[i]
                    obank, odst = banks_a.take(), oTb.take()
                    for t in range(AT):
                        for b in range(BPT):
                            at = t * P + b * S
                            m = mm_group(obank.ap[:, at:at + S], [(vb.ap[:, b, t // tpg, :], dst.ap[:, t, b * S:(b + 1) * S])],
                                         (list(obank.free), v_ready, done))
                    vb.free = [m]
                    dst.free = [m]
                    odone = dve(lambda e: e.tensor_copy(
                        odst.ap[:].rearrange("p t (s b) -> p t b s", s=S),
                        obank.ap.rearrange("p (t b s) -> p t b s", t=AT, s=S)), m, list(odst.free))
                    obank.free = [odone]
                    OB[i] = (odst, odone)

                def output(i):
                    src, ready = OB[i]
                    bank = banks_o.take()
                    m = mm_group(bank.ap, [(src.ap[:, t, :], w_o[:, t, :]) for t in range(AT)],
                                 (list(bank.free), ready, wo_ready))
                    src.free = [m]
                    done = dve(lambda e: e.tensor_tensor(x[:, i, :], x[:, i, :], bank.ap, ALU.add), m)
                    bank.free = [done]
                    if not normed:
                        done = pool(lambda e: e.tensor_tensor(x[:, i, :], x[:, i, :], bias["bo"][:], ALU.add), done)
                    x_written(i, done)

                def run(stage, i):
                    if 0 <= i < NT:
                        stage(i)

                def normalise_input(i):
                    NORM[i] = normalise_tile(i)

                normalise_input(0)
                turn_input(0)
                normalise_input(1)
                for i in range(NT + 5):
                    run(project, i)
                    run(attend, i - 3)
                    run(mix, i - 5)
                    run(spread, i - 2)
                    run(turn_weights, i - 4)
                    run(turn_input, i + 1)
                    run(normalise_input, i + 2)
                    run(weigh, i - 3)
                    run(output, i - 5)
                    run(finish_projection, i)
                wo.free = [pe.now()]

        def hadamard_ffn(name):
            nonlocal ln_banks
            barrier()
            with ExitStack() as arena:
                def sb(n, shape, dt=F32):
                    return arena.enter_context(nc.sbuf_tensor(f"{name}_{n}", shape, dt))

                down = sb("down", [P, FC, D])
                z = sb("z", [P, FC, TOK])
                other = z[:, FC // 2:FC, :].rearrange("p a n -> p (a n)").rearrange("p (a n) -> p a n", a=FC)
                had = sb("had", [P, 2, P])
                su_ug = sb("su_ug", [P, KD])
                su_dp = sb("su_dp", [P, FC])
                ws_up = sb("ws_up", [P, FC])
                ws_gate = sb("ws_gate", [P, FC])
                ws_down = sb("ws_down", [P, D])
                su = sb("su", [P, FC])
                ugs = Ring([Slot(tuple(sb(f"ug_{v}{i}", [P, KD * P], F32R) for v in ("hi", "lo"))) for i in range(3)])
                sg = Ring([Slot(sb(f"sg{i}", [P, TOK])) for i in range(2)])
                tabs = Slot(None, sem(f"s_{name}_tabs"))
                for dst, key in ((su_ug[:], "su_ug"), (had[:].rearrange("p a n -> p (a n)"), "had"), (su_dp[:], "su_dp"),
                                 (ws_up[:], "ws_up"), (ws_gate[:], "ws_gate")):
                    dma(tabs, dst, d[key], queue=act)
                tabs_ready = dma(tabs, ws_down[:], d["ws_down"].to_broadcast([P, D]), queue=act)
                scaled = dve(lambda e: e.tensor_tensor(su[:], ws_up[:], su_dp[:], ALU.mult), tabs_ready)

                hT = tuple(sb(f"hT_{v}", [P, KD, TOK], F32R) for v in ("hi", "lo"))
                hs = z[:, 4:8, :]

                def scale_sink(i, src, after):
                    scale = su_ug[:].rearrange("p (k o) -> p k o", o=1).to_broadcast([P, KD, P])
                    return [dve(lambda e: e.tensor_tensor(hs[:, :, i * P:(i + 1) * P], src, scale, ALU.mult), after, tabs_ready)]

                got = []
                banks_d = Ring([Slot(psum(4)), Slot(psum(5))])
                for q in range(FC // 4):
                    slot, ready = load_weights(d["wdT"][q], 4 * D)
                    for a in range(4):
                        bank = banks_d.take()
                        m = mm_group(bank.ap, [(had[:, 1, :], slot.ap[:, a * D:(a + 1) * D])], (list(bank.free), ready, tabs_ready))
                        got.append(act(lambda e, n=4 * q + a, bank=bank: e.copy(down[:, n, :], bank.ap), m))
                        bank.free = [got[-1]]
                    slot.free = [m]
                ln_banks = Ring([Slot(psum(6)), Slot(psum(7))])
                h_ready = layernorm(scale_sink)

                def butterfly_ops(src, dst, stride):
                    n = src.shape[1]
                    return [(dst[:, at + (stride if op == ALU.subtract else 0), :], src[:, at, :], src[:, at + stride, :], op)
                            for at in range(n) if not at & stride for op in (ALU.add, ALU.subtract)]

                def butterfly(eng, src, dst, stride, after):
                    return [eng(lambda e, o=o: e.tensor_tensor(*o), after) for o in butterfly_ops(src, dst, stride)]

                tmp = z[:, 0:2, :].rearrange("p a n -> p (a n)").rearrange("p (k n) -> p k n", k=KD)
                tmp2 = z[:, 2:4, :].rearrange("p a n -> p (a n)").rearrange("p (k n) -> p k n", k=KD)
                hx_ready = []
                banks_h = Ring([Slot(psum(i)) for i in range(4)])
                free = None
                for t in range(TOK // BANK):
                    cols_ = slice(t * BANK, (t + 1) * BANK)
                    got = []
                    for k in range(KD):
                        bank = banks_h.take()
                        m = mm_group(bank.ap, [(had[:, 0, :], hs[:, k, cols_])], (list(bank.free), h_ready, tabs_ready))
                        got.append(act(lambda e, k=k, bank=bank: e.copy(tmp[:, k, :], bank.ap), m, free))
                        bank.free = [got[-1]]
                    one = butterfly(dve, tmp, tmp2, 1, [got, free])
                    two = butterfly(dve, tmp2, tmp, 2, one)
                    done = split(tuple(v[:, :, cols_] for v in hT), tmp, two)
                    free = done
                    hx_ready += done
                pairs = Ring([Slot(psum(2 * i, 2)) for i in range(4)])
                for n, s_ in enumerate(pairs.slots):
                    s_.free = [[banks_h, banks_h, banks_d, ln_banks][n].slots[j + (2 if n == 1 else 0)].free for j in range(2)]
                    s_.free = [m for f in s_.free for m in f]
                stages = [(down[:], other, 1), (other, down[:], 2), (down[:], other, 4), (other, down[:], 8)]
                stage_marks = [got]

                def butterfly_steps():
                    for src, dst, stride in stages:
                        marks = []
                        before = stage_marks[-1]
                        for n, o in enumerate(butterfly_ops(src, dst, stride)):
                            marks.append((dve if n % 2 else pool)(lambda e, o=o: e.tensor_tensor(*o), before))
                            yield
                        stage_marks.append(marks)

                steps = butterfly_steps()
                uw = {}

                def split_up(n):
                    a, u = n // 2, 1 - n % 2
                    if n % 4 == 0:
                        uw["slot"] = load_weights(d["wug"][a // 2], 2 * 2 * KD * P)
                    slot, landed = uw["slot"]
                    at = ((a % 2) * 2 + u) * KD * P
                    w_ = ugs.take()
                    uw[n] = (w_, split(cut(w_.ap, slice(None)), slot.ap[:, at:at + KD * P], [landed, list(w_.free)], act, pool))
                    if n % 4 == 3:
                        slot.free = uw[n][1]

                split_up(0)
                z_ready = []
                for a in range(FC):
                    gate, up = pairs.take(), pairs.take()
                    for u, unit in ((1, gate), (0, up)):
                        n = 2 * a + 1 - u
                        if n + 1 < 2 * FC:
                            split_up(n + 1)
                        w_, ready = uw[n]
                        for t in range(2):
                            m = mm_group(unit.ap[:, t * BANK:(t + 1) * BANK],
                                         [p for k in range(KD) for p in parts(
                                             cut(w_.ap, slice(None), slice(k * P, (k + 1) * P)),
                                             cut(hT, slice(None), k, slice(t * BANK, (t + 1) * BANK)))],
                                         (list(unit.free), ready, hx_ready))
                        w_.free = [m]
                        if u == 1:
                            sgb = sg.take()
                            g1 = act(lambda e, a=a, sgb=sgb, unit=unit: e.activation(sgb.ap[:], unit.ap, ACT.Silu,
                                                                                     scale=ws_gate[:, a:a + 1]),
                                     m, list(sgb.free), tabs_ready)
                            unit.free = [g1]
                    z1 = dve(lambda e, a=a, sgb=sgb, up=up: e.scalar_tensor_tensor(
                        out=z[:, a, :], in0=up.ap, scalar=su[:, a:a + 1], in1=sgb.ap[:], op0=ALU.mult, op1=ALU.mult),
                        m, g1, scaled, stage_marks[4] if a >= FC // 2 else hx_ready)
                    up.free = [z1]
                    sgb.free = [z1]
                    for _ in range(9):
                        next(steps, None)
                    z_ready.append(z1)

                tail_banks = Ring([Slot(psum(i)) for i in range(8)])
                for n, s_ in enumerate(tail_banks.slots):
                    s_.free = list(pairs.slots[n // 2].free)
                for i in range(NT):
                    bank = tail_banks.take()
                    m = mm_group(bank.ap, [(z[:, a, i * P:(i + 1) * P], down[:, a, :]) for a in range(FC)],
                                 (list(bank.free), z_ready, stage_marks[4]))
                    buf = xn.take()
                    f1 = dve(lambda e, bank=bank, buf=buf: e.tensor_tensor(buf.ap[:], bank.ap, ws_down[:], ALU.mult), m, list(buf.free))
                    f2 = dve(lambda e, i=i, buf=buf: e.tensor_tensor(x[:, i, :], x[:, i, :], buf.ap[:], ALU.add), f1)
                    bank.free = [f1]
                    buf.free = [f2]
                    x_written(i, f2)

        def experts(name):
            nonlocal ln_banks
            barrier()
            with ExitStack() as arena:
                def sb(n, shape, dt=F32):
                    return arena.enter_context(nc.sbuf_tensor(f"{name}_{n}", shape, dt))

                gate = sb("gate", [P, KD, NE])
                alpha = sb("alpha", [P, 1])
                iota = sb("iota", [P, NE])
                order = sb("order", [P, TOPK])
                tabs = Slot(None, sem(f"s_{name}_tabs"))
                dma(tabs, gate[:].rearrange("p k n -> p (k n)"), d["gate"], queue=act)
                dma(tabs, iota[:], d["iota"], queue=act)
                dma(tabs, order[:], d["order"], queue=act)
                tabs_ready = dma(tabs, alpha[:], d["alpha"].to_broadcast([P, 1]), queue=act)
                hT = tuple(sb(f"hT_{v}", [P, KD, TOK], F32R) for v in ("hi", "lo"))

                combine = sb("combine", [P, NT, NE])
                pb = sb("pb", [P, NT, NE])
                top = sb("top", [P, NT, TOPK])
                at = sb("at", [P, NT, TOPK], U32)
                atf = sb("atf", [P, NT, TOPK])
                rw = sb("rw", [P, NT, TOPK])
                act_ = sb("act_", [P, NT, TOPK])
                fb = sb("fb", [P, NT, TOPK])
                one = sb("one", [P, 10, NT])

                def chain(step, *after):
                    return dve(step, dve.now(), *after)

                def lone(step, *after):
                    return pool(step, pool.now(), *after)

                def per_tile(ap, n):
                    return ap.rearrange("p (i o) -> p i o", o=1).to_broadcast([P, NT, n])

                gates = tuple(sb(f"gate_{v}", [P, KD, NE], F32R) for v in ("hi", "lo"))
                gate_ready = split(cut(gates, slice(None)), gate[:], [tabs_ready])
                ln_banks = Ring([Slot(psum(0)), Slot(psum(1))])
                bank = Slot(psum(6))
                wgu = Ring([Slot(tuple(sb(f"wgu_{v}{i}", [P, KD * 2 * EI], F32R) for v in ("hi", "lo"))) for i in range(2)])
                wdn = Ring([Slot(tuple(sb(f"wdn_{v}{i}", [P, 3 * D], F32R) for v in ("hi", "lo"))) for i in range(2)])
                z1b = Ring([Slot(tuple(sb(f"z1_{v}{i}", [P, TOK], F32R) for v in ("hi", "lo"))) for i in range(3)])
                z2b = Ring([Slot(tuple(sb(f"z2_{v}{i}", [P, TOK], F32R) for v in ("hi", "lo"))) for i in range(2)])
                work = Ring([Slot(sb(f"work{i}", [P, TOK])) for i in range(3)])
                crow = Ring([Slot(sb(f"crow{i}", [P, TOK]), sem(f"s_{name}_c{i}")) for i in range(2)])
                W, WD, WG, C, Z1, Z2 = ({} for _ in range(6))
                rows_stored = [None]
                GU = KD * 2 * EI

                def fetch(e_):
                    W[e_] = load_weights(d["experts"][e_], SLOT if e_ % 2 == 0 else SLOT - D)

                def fetch_row(e_):
                    row = crow.take()
                    C[e_] = (row, dma(row, row.ap[:], combine_rows[e_:e_ + 1, :].to_broadcast([P, TOK]),
                                      list(row.free), rows_stored[0]))

                def split_weights(e_):
                    slot, ready = W[e_]
                    dst = wgu.take()
                    WG[e_] = (dst, split(cut(dst.ap, slice(None)), slot.ap[:, 0:GU], [ready, list(dst.free)], act, lone))
                    if e_ % 2 == 0:
                        WD[e_ // 2] = (wdn.take(), [])
                    down, marks = WD[e_ // 2]
                    at, n = (0, 2 * D) if e_ % 2 == 0 else (2 * D, D)
                    marks += split(cut(down.ap, slice(None), slice(at, at + n)), slot.ap[:, GU:GU + n],
                                   [ready, list(down.free)], act, lone)
                    slot.free = WG[e_][1] + marks[-2:]

                fetch(0)
                fetch(1)
                split_weights(0)
                h_ready = layernorm(split_sink(hT))
                for i in range(NT):
                    m = mm_group(bank.ap[:, i * NE:(i + 1) * NE],
                                 [p for k in range(KD) for p in parts(cut(hT, slice(None), k, slice(i * P, (i + 1) * P)),
                                                                      tuple(v[:, k, :] for v in gates))],
                                 (h_ready, gate_ready))
                lg = bank.ap[:, 0:NT * NE].rearrange("p (i n) -> p i n", i=NT)
                chain(lambda e: e.tensor_reduce(one[:, 0, :], lg, AX_X, ALU.max), m)
                c1 = chain(lambda e: e.tensor_tensor(pb[:], lg, per_tile(one[:, 0, :], NE), ALU.subtract))
                c2 = act(lambda e: e.activation(pb[:], pb[:], ACT.Exp), c1)
                chain(lambda e: e.tensor_reduce(one[:, 1, :], pb[:], AX_X, ALU.add), c2)
                chain(lambda e: e.reciprocal(one[:, 2, :], one[:, 1, :]))
                chain(lambda e: e.tensor_tensor(pb[:], pb[:], per_tile(one[:, 2, :], NE), ALU.mult))
                for i in range(NT):
                    chain(lambda e, i=i: e.max(top[:, i, :], pb[:, i, :]))
                    chain(lambda e, i=i: e.max_index(at[:, i, :], top[:, i, :], pb[:, i, :]))
                chain(lambda e: e.tensor_copy(atf[:], at[:]))
                chain(lambda e: e.tensor_reduce(one[:, 3, :], top[:], AX_X, ALU.add))
                chain(lambda e: e.tensor_scalar(one[:, 3, :], one[:, 3, :], 1e-12, None, ALU.max))
                chain(lambda e: e.reciprocal(one[:, 3, :], one[:, 3, :]))
                chain(lambda e: e.tensor_tensor(rw[:], top[:], per_tile(one[:, 3, :], TOPK), ALU.mult))
                chain(lambda e: e.tensor_scalar(top[:], rw[:], alpha[:, 0:1], None, ALU.mult))
                chain(lambda e: e.tensor_scalar(act_[:], top[:], TAU, None, ALU.is_ge))
                chain(lambda e: e.tensor_reduce(one[:, 4, :], act_[:], AX_X, ALU.max))
                chain(lambda e: e.tensor_scalar(one[:, 4, :], one[:, 4, :], -1.0, 1.0, ALU.mult, ALU.add))
                chain(lambda e: e.tensor_reduce(one[:, 5, :], top[:], AX_X, ALU.max))
                chain(lambda e: e.tensor_tensor(fb[:], top[:], per_tile(one[:, 5, :], TOPK), ALU.is_equal))
                orders = order[:].rearrange("p (o n) -> p o n", o=1).to_broadcast([P, NT, TOPK])
                chain(lambda e: e.tensor_tensor(fb[:], fb[:], orders, ALU.mult))
                chain(lambda e: e.tensor_reduce(one[:, 6, :], fb[:], AX_X, ALU.max))
                chain(lambda e: e.tensor_tensor(fb[:], orders, per_tile(one[:, 6, :], TOPK), ALU.is_equal))
                chain(lambda e: e.tensor_tensor(fb[:], fb[:], per_tile(one[:, 4, :], TOPK), ALU.mult))
                chain(lambda e: e.tensor_tensor(act_[:], act_[:], fb[:], ALU.max))
                chain(lambda e: e.tensor_tensor(rw[:], rw[:], act_[:], ALU.mult))
                chain(lambda e: e.tensor_reduce(one[:, 7, :], rw[:], AX_X, ALU.add))
                chain(lambda e: e.tensor_scalar(one[:, 7, :], one[:, 7, :], 1e-12, None, ALU.max))
                chain(lambda e: e.reciprocal(one[:, 7, :], one[:, 7, :]))
                chain(lambda e: e.tensor_tensor(rw[:], rw[:], per_tile(one[:, 7, :], TOPK), ALU.mult))
                pick = sb("pick", [P, NT, NE])
                over_tiles = iota[:].rearrange("p (o n) -> p o n", o=1).to_broadcast([P, NT, NE])
                over_experts = lambda ap: ap.to_broadcast([P, NT, NE])
                for k in range(TOPK):
                    dst = pick if k else combine
                    chain(lambda e, k=k, dst=dst: e.tensor_tensor(dst[:], over_tiles, over_experts(atf[:, :, k:k + 1]), ALU.is_equal))
                    chain(lambda e, k=k, dst=dst: e.tensor_tensor(dst[:], dst[:], over_experts(rw[:, :, k:k + 1]), ALU.mult))
                    if k:
                        chain(lambda e: e.tensor_tensor(combine[:], combine[:], pick[:], ALU.add))
                routed = dve.now()

                units = Ring([Slot(psum(0, 2)), Slot(psum(2, 2)), Slot(psum(4, 2))])
                units.slots[0].free = ln_banks.slots[0].free + ln_banks.slots[1].free
                def hidden(e_):
                    w_, ready = WG[e_]

                    def product(col):
                        unit = units.take()
                        for t in range(2):
                            m = mm_group(unit.ap[:, t * BANK:(t + 1) * BANK],
                                         [p for k in range(KD) for p in parts(
                                             cut(w_.ap, slice(None), slice(k * 2 * EI + col, k * 2 * EI + col + P)),
                                             cut(hT, slice(None), k, slice(t * BANK, (t + 1) * BANK)))],
                                         (list(unit.free), ready, h_ready))
                        return unit, m

                    def begin(gate_ap, g_done, rows):
                        buf = work.take()
                        return buf, act(lambda e: e.activation(buf.ap[rows, :], gate_ap, ACT.Silu), g_done, list(buf.free))

                    def weigh(buf, a1, rows):
                        row, row_ready = C[e_]
                        return lone(lambda e: e.tensor_tensor(buf.ap[rows, :], buf.ap[rows, :], row.ap[rows, :], ALU.mult),
                                    a1, row_ready)

                    def finish(buf, a2, up_ap, u_done, rows, dst, dst_free):
                        b_ = buf.ap[rows, :]
                        a3 = dve(lambda e: e.tensor_tensor(b_, up_ap, b_, ALU.mult), a2, u_done)
                        buf.free = split(tuple(v[rows, :] for v in dst.ap), b_, [a3, dst_free], lo_engine=lone)
                        return a3

                    everything = slice(0, P)
                    mine, other = (slice(0, E2), slice(E2, P)) if e_ % 2 == 0 else (slice(E2, P), slice(0, E2))
                    g, g_done = product(0)
                    u, u_done = product(2 * P)
                    buf1, a1 = begin(g.ap, g_done, everything)
                    g.free = [a1]
                    gu, gu_done = product(P)
                    buf2, b1 = begin(gu.ap[other, :], gu_done, mine)
                    w_.free = [gu_done]

                    def finish_first():
                        a2 = weigh(buf1, a1, everything)
                        z1 = z1b.take()
                        u.free = [finish(buf1, a2, u.ap, u_done, everything, z1, list(z1.free))]
                        Z1[e_] = (z1, buf1.free)

                    def finish_rest():
                        if e_ % 2 == 0:
                            Z2[e_ // 2] = (z2b.take(), [])
                        z2, marks = Z2[e_ // 2]
                        a2 = weigh(buf2, b1, mine)
                        b3 = finish(buf2, a2, gu.ap[mine, :], gu_done, mine, z2, list(z2.free))
                        gu.free = [b1, b3]
                        marks += buf2.free
                        C[e_][0].free = [b3]

                    return finish_first, finish_rest

                first = hidden(0)

                cT = sb("cT", [NE, TOK])
                unit = Slot(psum(6, 2))
                for i in range(NT):
                    m = pe(lambda e, i=i: e.transpose(unit.ap[0:NE, i * P:(i + 1) * P], combine[:, i, :], ident[:]), routed)
                c3 = act(lambda e: e.copy(cT[:], unit.ap[0:NE, :]), m)
                rows = Slot(None, sem(f"s_{name}_rows"))
                rows_stored[0] = dma(rows, combine_rows, cT[:], c3)

                outs = Ring([Slot(psum(6)), Slot(psum(7))])
                for s_ in outs.slots:
                    s_.free = [c3]

                def contribute(pair, tiles):
                    z1a, z1c, (z2, z2_ready) = Z1[2 * pair], Z1[2 * pair + 1], Z2[pair]
                    down, ready = WD[pair]
                    for i in tiles:
                        bank = outs.take()
                        tok = slice(i * P, (i + 1) * P)
                        products = [p for n, z_ in enumerate((z1a[0], z2, z1c[0])) for p in parts(
                            cut(z_.ap, slice(None), tok), cut(down.ap, slice(None), slice(n * D, (n + 1) * D)))]
                        m = mm_group(bank.ap, products, (list(bank.free), z1a[1], z1c[1], z2_ready, ready))
                        done = dve(lambda e, i=i, bank=bank: e.tensor_tensor(x[:, i, :], x[:, i, :], bank.ap, ALU.add),
                                   m, x_ready[i])
                        bank.free = [done]
                        x_ready[i] = [done]
                    if NT - 1 in tiles:
                        for s_ in (z1a[0], z1c[0], z2, down):
                            s_.free = [m]

                fetch_row(0)
                fetch_row(1)
                AHEAD = 3
                for e_ in range(NE + 2):
                    if e_ + 1 < NE:
                        split_weights(e_ + 1)
                    if e_ < NE:
                        finish_first, finish_rest = hidden(e_) if e_ else first
                        finish_first()
                    if e_ + 2 < NE:
                        fetch(e_ + 2)
                    if e_ >= 2 and e_ % 2 == 0:
                        contribute(e_ // 2 - 1, range(AHEAD))
                    if e_ < NE:
                        finish_rest()
                    if e_ + 2 < NE:
                        fetch_row(e_ + 2)
                    if e_ >= 2 and e_ % 2 == 0:
                        contribute(e_ // 2 - 1, range(AHEAD, NT))

        ln_banks = None
        for i in range(NT):
            x_written(i, x_ready[i])
        phases = [lambda: cross_attention("L0x", False), lambda: self_attention("L0a", KVH, False),
                  lambda: hadamard_ffn("L0f"), lambda: cross_attention("L1x", True),
                  lambda: self_attention("L1a", AT, True), lambda: experts("L1f")]
        for phase in phases[:last_phase]:
            prior = [q.now() for q in compute]
            phase()

        stored = Slot(None, sem("s_stored"))
        for i in range(NT):
            end = dma(stored, out[i * P:(i + 1) * P, :], x[:, i, :], x_ready[i])
        sp.quiet(None, end)

        with nc.Block() as block:
            @block.sync
            def _(eng):
                sp.emit(eng)

            @block.tensor
            def _(eng):
                pe.emit(eng)

            @block.scalar
            def _(eng):
                act.emit(eng)

            @block.vector
            def _(eng):
                dve.emit(eng)

            @block.gpsimd
            def _(eng):
                pool.emit(eng)


def constants():
    f = np.float32

    def rope(n, dim):
        inv = (f(1.0) / f(10000.0) ** (np.arange(0, dim, 2, dtype=f) / f(dim))).astype(f)
        return (np.arange(n, dtype=f)[:, None] * inv[None, :]).astype(f)

    c = {"ident": np.eye(P, dtype=f)}
    fr = np.repeat(rope(L, DC), 2, axis=1)
    sign = np.where(np.arange(DC) < DC // 2, f(-1), f(1))

    def by_key(t):
        return np.ascontiguousarray(np.stack([t[0:P], t[P:2 * P], np.broadcast_to(t[L - 1:L], (P, DC))], 1)).reshape(P, -1)

    c["kcos"] = by_key(np.cos(fr).astype(f))
    c["ksin"] = by_key((np.sin(fr) * sign).astype(f))
    fq = np.repeat(rope(S, DCQ), 2, axis=1)
    cq, sq = np.cos(fq).astype(f), np.sin(fq).astype(f)
    j = np.arange(DCQ)
    sp = sq[:, (j + DCQ // 2) % DCQ] * np.where(j < DCQ // 2, f(1), f(-1))
    c["cosq"] = np.ascontiguousarray(cq.T.reshape(QC, P, S).transpose(1, 0, 2)).reshape(P, -1).astype(f)
    c["sinq"] = np.ascontiguousarray(sp.T.reshape(QC, P, S).transpose(1, 0, 2)).reshape(P, -1).astype(f)
    fa = rope(S, DH)
    fa = np.concatenate([fa, fa], 1)
    sa = np.where(np.arange(DH) < DH // 2, f(-1), f(1))
    c["acos"] = np.tile(np.cos(fa).astype(f), (BPT, 1))
    c["asin"] = np.tile((np.sin(fa) * sa).astype(f), (BPT, 1))
    c["mask"] = np.tile(np.where(np.arange(S)[:, None] >= np.arange(S)[None, :], f(0), f(NEG)), (BPT, 1)).astype(f)
    h = np.ones((1, 1))
    while h.shape[0] < P:
        h = np.block([[h, h], [h, -h]])
    c["had"] = np.concatenate([h / np.sqrt(D), h / np.sqrt(INTER)], 1).astype(f)
    c["iota"] = np.broadcast_to(np.arange(NE, dtype=f), (P, NE)).copy()
    c["order"] = np.broadcast_to(np.arange(TOPK, 0, -1).astype(f), (P, TOPK)).copy()
    return c


def layout(i):
    f = np.float32
    c = np.ascontiguousarray
    o = {"x": i["x"].reshape(NT, BPT, S, D).transpose(0, 2, 1, 3).reshape(TOK, D), "ctx": i["ctx_512"]}

    def padded(a, rows=P):
        out = np.zeros((*a.shape[:-2], rows, a.shape[-1]), f)
        out[..., :a.shape[-2], :] = a
        return out

    def by_partition(a):
        n = a.shape[-1]
        return c(a.reshape(-1, P, n).transpose(1, 0, 2)).reshape(P, -1)

    for name, g in (("L0x", "L0_xattn_"), ("L1x", "L1_xattn_")):
        wq = i[g + "Wq"].reshape(XH, XK, D)
        kcq, qr, kr = i[g + "w_kc_q"], i[g + "W_qr"], i[g + "W_kr"]
        kr_t = padded(kr.transpose(0, 2, 1))
        wo_t = i[g + "Wo"].T.reshape(XH, XK, D)
        both = np.concatenate([i[g + "w_kc_kv"], wo_t], 2).reshape(XH // OUT_HEADS, OUT_HEADS, P, OUT_PACK)
        o[f"{name}_out"] = c(both.transpose(0, 2, 1, 3)).reshape(XH // OUT_HEADS, P, -1)
        if name == "L0x":
            parts = [wq, kcq.transpose(0, 2, 1).reshape(XH, QC, P, XK).transpose(0, 2, 1, 3).reshape(XH, P, -1),
                     qr.reshape(XH, QC, P, RR).transpose(0, 2, 1, 3).reshape(XH, P, -1)]
        else:
            qr_t = qr.transpose(0, 2, 1)
            parts = [wq.transpose(0, 2, 1).reshape(XH, KD, P, XK).transpose(0, 2, 1, 3).reshape(XH, P, -1), kcq,
                     padded(np.concatenate([qr_t, qr_t[:, :, :DCQ // 2]], 2))]
        o[f"{name}_heads"] = c(np.concatenate([*parts, kr_t], 2))

    a = "L0_attn_"
    rep = lambda w: np.repeat(w.reshape(-1, KVH, 1, DH), HPT, axis=2).reshape(w.shape[0], -1)
    o["L0a_wq"] = by_partition(i[a + "Wq"])
    o["L0a_wk"] = by_partition(rep(i[a + "Wk"]))
    o["L0a_wv"] = by_partition(i[a + "Wv"])
    o["L0a_wo"] = by_partition(i[a + "Wo"])
    o["L0a_bq"] = i[a + "bq"].reshape(1, -1)
    o["L0a_bk"] = rep(i[a + "bk"].reshape(1, -1))
    o["L0a_bv"] = i[a + "bv"].reshape(1, -1)
    o["L0a_bo"] = i[a + "bo"].reshape(1, -1)

    a = "L0_ffn_"
    o["su_ug"] = c(i[a + "SU_ug"].reshape(KD, P).T)
    o["su_dp"] = c(i[a + "SU_dp"].reshape(FC, P).T)
    o["ws_up"] = c(i[a + "Wscale_ug"][:INTER].reshape(FC, P).T)
    o["ws_gate"] = c(i[a + "Wscale_ug"][INTER:].reshape(FC, P).T)
    o["ws_down"] = i[a + "Wscale_dp"].reshape(1, -1)
    o["wdT"] = c(i[a + "W_down"].T.reshape(FC // 4, 4, P, D).transpose(0, 2, 1, 3)).reshape(FC // 4, P, -1)
    ug = np.stack([i[a + "W_up"], i[a + "W_gate"]])
    ug = ug.reshape(2, FC // 2, 2, P, KD, P).transpose(1, 5, 2, 0, 4, 3)
    o["wug"] = c(ug).reshape(FC // 2, P, -1)

    a = "L1_attn_"
    qkv = i[a + "w_qkv"]
    for n, key in enumerate(("wq", "wk", "wv")):
        o[f"L1a_{key}"] = by_partition(qkv[:, n * D:(n + 1) * D])
    o["L1a_wo"] = by_partition(i[a + "w_out"])
    for key, g in (("gq", "q_gamma"), ("gk", "k_gamma")):
        v = i[a + g].reshape(1, DH)
        o[key] = v
        o[f"{key}_roll"] = c(np.concatenate([v[:, DH // 2:], v[:, :DH // 2]], 1))

    a = "L1_ffn_"
    o["gate"] = by_partition(c(i[a + "gate_weight"].T))
    o["alpha"] = i[a + "layer_alpha"].reshape(1, 1)
    gu = i[a + "gate_up_proj"].transpose(0, 2, 1)
    dn = i[a + "down_proj"].transpose(0, 2, 1)
    experts = np.zeros((NE, P, SLOT), f)
    for e in range(NE):
        rest = [gu[e, :, P:EI], gu[e, :, EI + P:2 * EI]]
        if e % 2 == 0:
            rest = rest[::-1]
        w = np.concatenate([gu[e, :, 0:P], *rest, gu[e, :, EI:EI + P]], 1)
        experts[e, :, 0:KD * 2 * EI] = by_partition(w)
        at = KD * 2 * EI
        experts[e, :, at:at + D] = dn[e, 0:P, :]
        if e % 2 == 0:
            experts[e, :E2, at + D:] = dn[e, P:EI, :]
            experts[e, E2:, at + D:] = dn[e + 1, P:EI, :]
    o["experts"] = experts
    o.update(constants())
    return {k: np.ascontiguousarray(v) for k, v in o.items()}


def unlayout(out):
    return np.asarray(out).reshape(NT, S, BPT, D).transpose(0, 2, 1, 3).reshape(B, S, D)


def kernel(**inputs):
    import concourse.bacc as bacc
    from concourse.bass_utils import run_bass_kernel_spmd

    arrays = layout({k: np.asarray(v) for k, v in inputs.items()})
    nc = bacc.Bacc("TRN2", target_bir_lowering=False, num_devices=1)
    d = {k: nc.dram_tensor(f"in_{k}", a.shape, mybir.dt.from_np(a.dtype), kind="ExternalInput").ap()
         for k, a in arrays.items()}
    out = nc.dram_tensor("out", (TOK, D), F32, kind="ExternalOutput").ap()
    build_kernel(nc, d, out)
    result = run_bass_kernel_spmd(nc, [{f"in_{k}": a for k, a in arrays.items()}], core_ids=[0])
    return unlayout(result.results[0]["out"])
```

```python
from contextlib import ExitStack

import numpy as np

import concourse.bass as bass
from concourse import mybir

ALU = mybir.AluOpType
ACT = mybir.ActivationFunctionType
F32 = mybir.dt.float32
F32R = mybir.dt.float32r
U32 = mybir.dt.uint32
AX_X = mybir.AxisListType.X

P = 128
BANK = 512
B, S, D = 32, 32, 512
TOK = B * S
NT = TOK // P
BPT = P // S
KD = D // P
L, DC = 257, 128
LC = (L - 1) // P
XH, XK, DCQ, RR = 16, 128, 384, 64
QC = DCQ // P
AH, DH = 16, 32
HPT = P // DH
AT = AH // HPT
KVH = 2
INTER = 2048
FC = INTER // P
NE, EI, TOPK, TAU = 32, 192, 8, 0.05
E2 = EI - P
NEG = -1e30

L0_PACK = {"wq": D, "kcq": QC * XK, "qr": QC * RR, "kr": DC}
L1_PACK = {"wq": KD * XK, "kcq": DCQ, "qr": DCQ + DCQ // 2, "kr": DC}
OUT_PACK = DC + D
OUT_HEADS = 4
SLOT = 2560
NSLOT = 3


def columns(pack):
    at, out = 0, {}
    for name, n in pack.items():
        out[name] = (at, at + n)
        at += n
    return out, at


class Engine:

    def __init__(self, sem):
        self.sem, self.count, self.steps = sem, 0, []

    def __call__(self, step, *after):
        self.count += 1
        self.steps.append((step, after, True))
        return (self.sem, self.count)

    def quiet(self, step, *after):
        self.steps.append((step, after, False))

    def now(self):
        return (self.sem, self.count)

    def emit(self, eng):
        reached = {}

        def wait(mark):
            if mark is None:
                return
            if isinstance(mark, list):
                for m in mark:
                    wait(m)
                return
            sem, value = mark
            if reached.get(id(sem), 0) < value:
                eng.wait_ge(sem, value)
                reached[id(sem)] = value

        for step, after, counted in self.steps:
            for mark in after:
                wait(mark)
            ins = step(eng) if step else None
            if counted:
                ins.then_inc(self.sem, 1)


class Slot:

    def __init__(self, ap, sem=None):
        self.ap, self.sem, self.landed = ap, sem, 0
        self.marks, self.taken = [], False

    @property
    def free(self):
        return self.marks

    @free.setter
    def free(self, marks):
        self.marks, self.taken = marks, False


class Ring:
    def __init__(self, slots):
        self.slots, self.n = slots, 0

    def take(self):
        slot = self.slots[self.n % len(self.slots)]
        self.n += 1
        assert not slot.taken, "taken again before its readers are known"
        slot.taken = True
        return slot


def build_kernel(nc, d, out, last_phase=6):
    with ExitStack() as ctx:
        def sem(name):
            return ctx.enter_context(nc.semaphore(name))

        def keep(name, shape, dt=F32):
            return ctx.enter_context(nc.sbuf_tensor(name, shape, dt))

        pe, act, dve, pool, sp = (Engine(sem(f"s_{n}")) for n in ("pe", "act", "dve", "pool", "sp"))
        compute = (pe, act, dve, pool)

        def dma(slot, dst, src, *after, queue=None):
            slot.landed += 16
            (queue or sp).quiet(lambda e: e.dma_start(dst, src).then_inc(slot.sem, 16), *after)
            return (slot.sem, slot.landed)

        def barrier():
            marks = [q.now() for q in compute]
            for q in compute:
                q.quiet(None, marks)
            return marks

        def phase_start():
            marks = list(arena_left)
            ahead[:] = [normalise_tile(i) for i in range(2)]
            for q in compute:
                q.quiet(None, marks)
            return marks

        banks = ctx.enter_context(nc.psum_tensor("banks", [P, 8, BANK], F32))

        def psum(first, n=1):
            return banks[:, first:first + n, :].rearrange("p a n -> p (a n)")

        x = keep("x", [P, NT, D])
        xn = Ring([Slot(keep(f"xn{i}", [P, D])) for i in range(3)])
        stats = keep("stats", [P, NT, 6])
        moments = keep("moments", [P, NT, 2])
        rstd = keep("rstd", [P, NT])
        wring = Ring([Slot(keep(f"w{i}", [P, SLOT]), sem(f"s_w{i}")) for i in range(NSLOT)])
        ident = keep("ident", [P, P])

        power = keep("power", [P, AH])
        power_set = pool(lambda e: e.memset(power[:], -0.5))
        combine_rows = nc.dram_tensor("combine_rows", (NE, TOK), F32, kind="Internal").ap()
        const = Slot(None, sem("s_const"))
        def load_weights(src, n):
            slot = wring.take()
            ready = dma(slot, slot.ap[:, 0:n], src[:, 0:n], list(slot.free))
            return slot, ready

        xin = [Slot(None, sem(f"s_x{i}")) for i in range(NT)]
        x_ready, rstd_ready = [], [None] * NT
        first_heads = []
        for i in range(NT):
            if i in (0, 3, 6):
                first_heads.append(load_weights(d["L0x_heads"][len(first_heads)], columns(L0_PACK)[1]))
            x_ready.append([dma(xin[i], x[:, i, :], d["x"][i * P:(i + 1) * P, :])])
            if i == 1:
                const_ready = dma(const, ident[:], d["ident"])

        arena_left, ahead = [], []

        def x_written(i, mark):
            x_ready[i] = mark if isinstance(mark, list) else [mark]
            if i == NT - 1:
                arena_left[:] = [q.now() for q in compute]
            m1 = dve(lambda e: e.bn_stats(stats[:, i, :], x[:, i, :]), x_ready[i])
            m2 = dve(lambda e: e.bn_aggr(moments[:, i, :], stats[:, i, :]), m1)
            m3 = dve(lambda e: e.tensor_scalar(rstd[:, i:i + 1], moments[:, i, 1:2], 1e-5, None, ALU.add), m2)
            rstd_ready[i] = pool(lambda e: e.tensor_tensor(rstd[:, i:i + 1], rstd[:, i:i + 1], power[:, 0:1], ALU.pow),
                                 m3, power_set)

        def normalise_tile(i):
            buf = xn.take()
            return buf, dve(lambda e: e.tensor_scalar(buf.ap[:], x[:, i, :], moments[:, i, 0:1], rstd[:, i:i + 1],
                                                      ALU.subtract, ALU.mult), rstd_ready[i], list(buf.free))

        def turn_tile(i, normalised, sink):
            buf, ready = normalised
            bank = ln_banks.take()
            for k in range(KD):
                step = lambda e, k=k: e.transpose(bank.ap[:, k * P:(k + 1) * P], buf.ap[:, k * P:(k + 1) * P], ident[:])
                if k < KD - 1:
                    pe.quiet(step, ready, const_ready, list(bank.free))
                else:
                    turned = pe(step)
            buf.free = [turned]
            done = sink(i, bank.ap.rearrange("p (k n) -> p k n", k=KD), turned)
            bank.free = done
            return done

        def layernorm(sink):
            ready = []
            for i in range(NT):
                if i + 4 < NT and rstd_ready[i + 4] is None:
                    x_written(i + 4, x_ready[i + 4])
                if i + 2 < NT:
                    ahead.append(normalise_tile(i + 2))
                ready.append(turn_tile(i, ahead[i], sink))
            return ready

        def split(dst, src, after, hi_engine=None, lo_engine=None):
            hi_engine, lo_engine = hi_engine or act, lo_engine or dve
            copy = (lambda e: e.copy(dst[0], src)) if hi_engine is act else (lambda e: e.tensor_copy(dst[0], src))
            hi = hi_engine(copy, after)
            lo = lo_engine(lambda e: e.tensor_tensor(dst[1], src, dst[0], ALU.subtract), hi, after)
            return [hi, lo]

        def split_sink(dst):
            return lambda i, src, after: split(tuple(v[:, :, i * P:(i + 1) * P] for v in dst), src, after)

        def parts(w, m):
            return [(w[0], m[0]), (w[0], m[1]), (w[1], m[0])]

        def cut(pair, *index):
            return tuple(v[index] for v in pair)

        def mm_group(out_ap, pairs, after=()):
            for n, (w, m) in enumerate(pairs):
                step = lambda e, n=n, w=w, m=m: e.matmul(out_ap, w, m, start=n == 0, stop=n == len(pairs) - 1)
                if n < len(pairs) - 1:
                    pe.quiet(step, *(after if n == 0 else ()))
                else:
                    return pe(step, *(after if n == 0 else ()))

        def cross_attention(name, rope_q):
            nonlocal ln_banks
            phase_start()
            cols, width = columns(L1_PACK if rope_q else L0_PACK)
            with ExitStack() as arena:
                def sb(n, shape, dt=F32):
                    return arena.enter_context(nc.sbuf_tensor(f"{name}_{n}", shape, dt))

                qT = sb("qT", [P, NT, XH, P])
                q_done = [[None, None] for _ in range(XH)]

                with ExitStack() as part:
                    def sbp(n, shape, dt=F32):
                        return part.enter_context(nc.sbuf_tensor(f"{name}_{n}", shape, dt))

                    hT = tuple(sbp(f"hT_{v}", [P, KD, TOK], F32R) for v in ("hi", "lo"))
                    ln_banks = Ring([Slot(psum(6)), Slot(psum(7))])
                    small = Ring([Slot(psum(4)), Slot(psum(5))])
                    wide = Ring([Slot(psum(i)) for i in range(4)])

                    def tokens(k, t):
                        return cut(hT, slice(None), k, slice(t * BANK, (t + 1) * BANK))

                    def q_cols(h, t):
                        return qT[:, t * (NT // 2):(t + 1) * (NT // 2), h, :]

                    def tiles(ap):
                        return ap.rearrange("p (i n) -> p i n", n=P)

                    weights = {}

                    def fetch(h):
                        weights[h] = first_heads.pop(0) if first_heads else load_weights(d[f"{name}_heads"][h], width)

                    def w(h, key, rows=P):
                        a, b = cols[key]
                        return weights[h][0].ap[0:rows, a:b]

                    if not rope_q:
                        t1 = Ring([Slot(sbp(f"t1_{i}", [RR, XK])) for i in range(2)])
                        t2 = Ring([Slot(sbp(f"t2_{i}", [P, DC])) for i in range(2)])
                        mq = Ring([Slot(tuple(sbp(f"mq_{v}{i}", [P, KD * DC], F32R) for v in ("hi", "lo"))) for i in range(2)])
                        T1, T2, MQ = {}, {}, {}

                        def fold_1(h):
                            bank, dst = small.take(), t1.take()
                            kcq = w(h, "kcq").rearrange("p (c k) -> p c k", c=QC)
                            qr = w(h, "qr").rearrange("p (c r) -> p c r", c=QC)
                            m = mm_group(bank.ap[0:RR, 0:XK], [(qr[:, c, :], kcq[:, c, :]) for c in range(QC)],
                                         (list(bank.free), weights[h][1]))
                            T1[h] = (dst, act(lambda e: e.copy(dst.ap[:], bank.ap[0:RR, 0:XK]), m, list(dst.free)))
                            bank.free = [T1[h][1]]

                        def fold_2(h):
                            bank, dst = small.take(), t2.take()
                            src, ready = T1[h]
                            m = mm_group(bank.ap[:, 0:DC], [(src.ap[:], w(h, "kr", RR))], (list(bank.free), ready))
                            src.free = [m]
                            T2[h] = (dst, dve(lambda e: e.tensor_copy(dst.ap[:], bank.ap[:, 0:DC]), m, list(dst.free)))
                            bank.free = [T2[h][1]]

                        def fold_3(h):
                            bank, dst = small.take(), mq.take()
                            src, ready = T2[h]
                            for k in range(KD):
                                m = mm_group(bank.ap[:, k * P:(k + 1) * P], [(w(h, "wq")[:, k * P:(k + 1) * P], src.ap[:])],
                                             (list(bank.free), ready))
                            src.free = [m]
                            MQ[h] = (dst, split(cut(dst.ap, slice(None)), bank.ap, [m, list(dst.free)]))
                            bank.free = MQ[h][1]

                        def project(h):
                            src, ready = MQ[h]
                            for t in range(TOK // BANK):
                                bank = wide.take()
                                m = mm_group(bank.ap, [p for k in range(KD) for p in parts(
                                    cut(src.ap, slice(None), slice(k * DC, (k + 1) * DC)), tokens(k, t))],
                                             (list(bank.free), ready, h_ready))
                                q = (act if t else dve)
                                copy = (lambda e, t=t, bank=bank: e.copy(q_cols(h, t), tiles(bank.ap))) if t else \
                                    (lambda e, t=t, bank=bank: e.tensor_copy(q_cols(h, t), tiles(bank.ap)))
                                q_done[h][t] = q(copy, m)
                                bank.free = [q_done[h][t]]
                            src.free = [m]

                        for h in range(XH + 3):
                            if h == 3:
                                h_ready = layernorm(split_sink(hT))
                            if h < XH:
                                fetch(h)
                                fold_1(h)
                            if 0 <= h - 1 < XH:
                                fold_2(h - 1)
                            if 0 <= h - 2 < XH:
                                fold_3(h - 2)
                                weights[h - 2][0].free = [pe.now()]
                            if 0 <= h - 3 < XH:
                                project(h - 3)
                    else:
                        cosq = sbp("cosq", [P, QC, S])
                        sinq = sbp("sinq", [P, QC, S])
                        tabs = Slot(None, sem(f"s_{name}_tabs"))
                        dma(tabs, cosq[:].rearrange("p a n -> p (a n)"), d["cosq"], queue=act)
                        tabs_ready = dma(tabs, sinq[:].rearrange("p a n -> p (a n)"), d["sinq"], queue=act)
                        ubuf = Ring([Slot(tuple(sbp(f"u_{v}{i}", [P, QC, DC], F32R) for v in ("hi", "lo"))) for i in range(4)])
                        qh = Ring([Slot(tuple(sbp(f"qh_{v}{i}", [P, BANK], F32R) for v in ("hi", "lo"))) for i in range(2)])
                        wsplit = Ring([Slot(tuple(sbp(f"ws_{v}{i}", [P, KD * XK + DCQ], F32R) for v in ("hi", "lo")))
                                       for i in range(2)])
                        WS = {}

                        def split_weights(h):
                            dst = wsplit.take()
                            WS[h] = (dst, split(cut(dst.ap, slice(None)), weights[h][0].ap[:, 0:KD * XK + DCQ],
                                                [weights[h][1], list(dst.free)], act, pool))

                        ybuf = Ring([Slot(tuple(sbp(f"y_{v}{i}", [P, 2, BANK], F32R) for v in ("hi", "lo"))) for i in range(3)])
                        U, QH, Y = {}, {}, {}

                        def fold_u(h, v):
                            dst, bank = ubuf.take(), small.take()
                            for c in range(QC):
                                at = c * P + v * (DCQ // 2)
                                m = mm_group(bank.ap[:, c * P:(c + 1) * P],
                                             [(w(h, "qr", RR)[:, at:at + P], w(h, "kr", RR))],
                                             (list(bank.free), weights[h][1]))
                            bank.free = split(tuple(u[:].rearrange("p c n -> p (c n)") for u in dst.ap),
                                              bank.ap[:, 0:QC * P], [m, list(dst.free)])
                            U[h, v] = (dst, bank.free)

                        def query(h, t):
                            bank, dst = wide.take(), qh.take()
                            src, ready = WS[h]
                            m = mm_group(bank.ap, [p for k in range(KD) for p in parts(
                                cut(src.ap, slice(None), slice(k * XK, (k + 1) * XK)), tokens(k, t))],
                                         (list(bank.free), ready, h_ready))
                            QH[h, t] = (dst, split(cut(dst.ap, slice(None)), bank.ap, [m, list(dst.free)]))
                            bank.free = QH[h, t][1]

                        def widen(h, t, c):
                            bank, dst = wide.take(), ybuf.take()
                            src, ready = QH[h, t]
                            at = KD * XK + c * P
                            m = mm_group(bank.ap, parts(cut(WS[h][0].ap, slice(None), slice(at, at + P)),
                                                        cut(src.ap, slice(None))), (list(bank.free), ready))
                            src.free = [m]
                            if t == 1 and c == QC - 1:
                                WS[h][0].free = [m]
                            read, wholes, ready = [], [], []
                            for v, tab in enumerate((cosq, sinq)):
                                table = tab[:, c, :].rearrange("p (i s b) -> p i s b", i=1, b=1).to_broadcast([P, BANK // P, S, BPT])
                                whole = xn.take()
                                read.append(dve(lambda e, table=table, whole=whole: e.tensor_tensor(
                                    whole.ap[:].rearrange("p (i s b) -> p i s b", s=S, b=BPT),
                                    bank.ap.rearrange("p (i s b) -> p i s b", s=S, b=BPT), table, ALU.mult),
                                    m, tabs_ready, list(whole.free)))
                                wholes.append(whole)
                            bank.free = read
                            for v, (whole, done) in enumerate(zip(wholes, read)):
                                whole.free = split(cut(dst.ap, slice(None), v), whole.ap[:], [done, list(dst.free)],
                                                   act, pool if v else dve)
                                ready += whole.free
                            Y[h, t, c] = (dst, ready)

                        acc = {}

                        def narrow(h, t, c):
                            if c == 0:
                                acc[h, t] = wide2.take()
                            bank = acc[h, t]
                            src, ready = Y[h, t, c]
                            products = [p for v in range(2) for p in parts(
                                cut(U[h, v][0].ap, slice(None), c), cut(src.ap, slice(None), v))]
                            for n, (u, y) in enumerate(products):
                                step = lambda e, n=n, u=u, y=y: e.matmul(
                                    bank.ap, u, y, start=c == 0 and n == 0, stop=c == QC - 1 and n == len(products) - 1)
                                if n < len(products) - 1:
                                    pe.quiet(step, ready, U[h, 0][1], U[h, 1][1], list(bank.free) if c == 0 else None)
                                else:
                                    m = pe(step)
                            src.free = [m]
                            if c == QC - 1:
                                q_done[h][t] = act(lambda e: e.copy(q_cols(h, t), tiles(bank.ap)), m)
                                bank.free = [q_done[h][t]]
                                if t == 1:
                                    for v in range(2):
                                        U[h, v][0].free = [m]
                                    weights[h][0].free = [m, WS[h][1]]

                        wide = Ring([Slot(psum(i)) for i in range(4)])
                        wide2 = Ring([Slot(psum(6)), Slot(psum(7))])
                        items = [(h, t, c) for h in range(XH) for t in range(2) for c in range(QC)]
                        LAG = 2
                        fetch(0)
                        split_weights(0)
                        h_ready = layernorm(split_sink(hT))
                        for s_, slot in zip(wide2.slots, ln_banks.slots):
                            s_.free = list(slot.free)
                        query(0, 0)
                        for n in range(len(items) + LAG):
                            if n < len(items):
                                h, t, c = items[n]
                                if c == 0 and t == 0:
                                    fold_u(h, 0)
                                    fold_u(h, 1)
                                    if h + 1 < XH:
                                        fetch(h + 1)
                                        split_weights(h + 1)
                                if c == 1:
                                    nxt = (h, 1) if t == 0 else (h + 1, 0)
                                    if nxt[0] < XH:
                                        query(*nxt)
                                widen(h, t, c)
                            if n >= LAG:
                                narrow(*items[n - LAG])
                out_weights = [load_weights(d[f"{name}_out"][n], OUT_HEADS * OUT_PACK) for n in range(NSLOT)]
                last = barrier()

                wn = sb("wn", [P, XH, D])
                wn_done = []

                def fold_out(h, bank):
                    n = h // OUT_HEADS
                    if n == len(out_weights):
                        out_weights.append(load_weights(d[f"{name}_out"][n], OUT_HEADS * OUT_PACK))
                    slot, ready = out_weights[n]
                    at = (h % OUT_HEADS) * OUT_PACK
                    m = mm_group(bank.ap, [(slot.ap[:, at:at + DC], slot.ap[:, at + DC:at + OUT_PACK])],
                                 (list(bank.free), ready))
                    wn_done.append(act(lambda e: e.copy(wn[:, h, :], bank.ap), m))
                    bank.free = [wn_done[-1]]
                    slot.free = [m]

                craw = Ring([Slot(sb(f"craw{i}", [P, 3, DC]), sem(f"s_{name}_c{i}")) for i in range(2)])
                rot = sb("rot", [P, 3, DC])
                kcos, ksin = sb("kcos", [P, 3, DC]), sb("ksin", [P, 3, DC])
                rope = Slot(None, sem(f"s_{name}_rope"))
                dma(rope, kcos[:].rearrange("p a n -> p (a n)"), d["kcos"], last)
                rope_ready = dma(rope, ksin[:].rearrange("p a n -> p (a n)"), d["ksin"])
                kv = Ring([Slot(sb(f"kv{i}", [P, 3, DC])) for i in range(5)])
                kvT = Ring([Slot(sb(f"kvT{i}", [P, LC * P + S])) for i in range(4)])
                prob = Ring([Slot(sb(f"prob{i}", [P, 4, LC * P])) for i in range(3)])
                pT = Ring([Slot(tuple(sb(f"pT_{v}{i}", [P, LC, BANK], F32R) for v in ("hi", "lo"))) for i in range(2)])
                kvs = Ring([Slot(tuple(sb(f"kvs_{v}{i}", [P, LC, DC], F32R) for v in ("hi", "lo"))) for i in range(2)])
                small4 = Ring([Slot(sb(f"small4_{i}", [P, 5, 4])) for i in range(4)])
                s_banks = Ring([Slot(psum(i)) for i in range(3)])
                t_banks = Ring([Slot(psum(4, 2))])
                c_bank = Slot(psum(6))
                k_bank = Slot(psum(7))
                o_bank = Slot(psum(3))
                EX = {}
                KV, KT, PR, PT, VS, VS_ready = {}, {}, {}, {}, {}, {}

                def of_batch(b, head=0, n=XH):
                    cols = qT[:, b // BPT, :, :].rearrange("p h n -> p (h n)")
                    return cols[:, head * P + b % BPT:(head + n) * P:BPT]
                rot_free = [None]

                def keys(b):
                    raw, dst = craw.take(), kv.take()
                    for c in range(LC):
                        dma(raw, raw.ap[:, c, :], d["ctx"][b, c * P:(c + 1) * P, :], list(raw.free), last)
                    ready = dma(raw, raw.ap[:, LC, :], d["ctx"][b, L - 1:L, :].to_broadcast([P, DC]))
                    hw = DC // 2
                    m1 = pool(lambda e: e.tensor_tensor(dst.ap[:], raw.ap[:], kcos[:], ALU.mult), ready, list(dst.free), rope_ready)
                    m2 = pool(lambda e: e.tensor_tensor(rot[:, :, 0:hw], raw.ap[:, :, hw:DC], ksin[:, :, 0:hw], ALU.mult), rot_free[0])
                    m3 = pool(lambda e: e.tensor_tensor(rot[:, :, hw:DC], raw.ap[:, :, 0:hw], ksin[:, :, hw:DC], ALU.mult))
                    m4 = pool(lambda e: e.tensor_tensor(dst.ap[:], dst.ap[:], rot[:], ALU.add), m1, m2, m3)
                    raw.free = [m3]
                    rot_free[0] = m4
                    m5 = pool(lambda e: e.tensor_tensor(dst.ap[:, 0:LC, :], dst.ap[:, 0:LC, :],
                                                        dst.ap[:, LC:LC + 1, :].to_broadcast([P, LC, DC]), ALU.subtract), m4)
                    KV[b] = (dst, m5)

                def keys_T(b):
                    src, ready = KV[b]
                    dst = kvT.take()
                    for c in range(LC):
                        pe.quiet(lambda e, c=c: e.transpose(k_bank.ap[:, c * P:(c + 1) * P], src.ap[:, c, :], ident[:]),
                                 ready, list(k_bank.free))
                    m = pe(lambda e: e.transpose(k_bank.ap[:, LC * P:LC * P + S], src.ap[0:S, LC, :], ident[0:S, 0:S]))
                    done = act(lambda e: e.copy(dst.ap[:], k_bank.ap[:, 0:LC * P + S]), m, list(dst.free))
                    k_bank.free = [done]
                    KT[b] = (dst, done)

                def scores(b):
                    kt, ready = KT[b]
                    dst, small = prob.take(), small4.take()
                    mx, neg, sums, tail = (small.ap[:, n, :] for n in range(4))
                    got = []
                    for g in range(2):
                        bank = s_banks.take()
                        for r in range(2):
                            m = mm_group(bank.ap[:, r * 256:(r + 1) * 256],
                                         [(of_batch(b, 8 * g + 4 * r, 4), kt.ap[:, 0:LC * P])], (list(bank.free), ready))
                        got.append((bank, dve(lambda e, g=g, bank=bank: e.tensor_reduce(
                            mx[:, 2 * g:2 * g + 2], bank.ap.rearrange("p (r n) -> p r n", r=2), AX_X, ALU.max),
                            m, list(small.free))))
                    m2 = dve(lambda e: e.tensor_scalar(neg, mx, -1.0, 0.0, ALU.mult, ALU.min), [m for _, m in got])
                    for r in range(4):
                        bank = got[r // 2][0]
                        m3 = act(lambda e, r=r, bank=bank: e.activation(
                            dst.ap[:, r, :], bank.ap[:, (r % 2) * 256:(r % 2 + 1) * 256], ACT.Exp, bias=neg[:, r:r + 1],
                            accum_out=sums[:, r:r + 1]), m2, list(dst.free))
                        if r % 2:
                            bank.free = [m3]
                    m4 = act(lambda e: e.activation(tail, neg, ACT.Exp))
                    EX[b] = (dst, small, m4)

                def weigh(b):
                    dst, small, m4 = EX[b]
                    sums, tail, rec = (small.ap[:, n, :] for n in range(2, 5))
                    m5 = dve(lambda e: e.tensor_tensor(sums, sums, tail, ALU.add), m4)
                    m6 = dve(lambda e: e.reciprocal(rec, sums), m5)
                    for r in range(4):
                        m7 = dve(lambda e, r=r: e.tensor_scalar(dst.ap[:, r, :], dst.ap[:, r, :], rec[:, r:r + 1], None, ALU.mult), m6)
                    small.free = [m7]
                    PR[b] = (dst, m7)

                def turn(b):
                    src, ready = PR[b]
                    bank, dst = t_banks.take(), pT.take()
                    done = []
                    for c in range(LC):
                        for r in range(4):
                            step = lambda e, c=c, r=r: e.transpose(bank.ap[:, c * BANK + r * P:c * BANK + (r + 1) * P],
                                                                   src.ap[:, r, c * P:(c + 1) * P], ident[:])
                            if r < 3:
                                pe.quiet(step, ready, list(bank.free))
                            else:
                                m = pe(step)
                        done += split(cut(dst.ap, slice(None), c), bank.ap[:, c * BANK:(c + 1) * BANK], [m, list(dst.free)])
                    src.free = [m]
                    bank.free = done
                    PT[b] = (dst, done)
                    kv_, _ = KV[b]
                    VS[b] = kvs.take()
                    VS_ready[b] = split(cut(VS[b].ap, slice(None)), kv_.ap[:, 0:LC, :], [list(VS[b].free)], pool, pool)
                    kv_.free = [*VS_ready[b], KT[b][1]]

                ctx_done = {}

                def values(b):
                    src, ready = PT[b]
                    v = VS[b]
                    kt, _ = KT[b]
                    m = mm_group(c_bank.ap, [p for c in range(LC) for p in parts(
                        cut(v.ap, slice(None), c), cut(src.ap, slice(None), c))], (list(c_bank.free), ready, VS_ready[b]))
                    src.free = [m]
                    v.free = [m]
                    ctx_done[b] = dve(lambda e: e.tensor_scalar(
                        of_batch(b), c_bank.ap,
                        kt.ap[:, LC * P:LC * P + 1], None, ALU.add), m)
                    c_bank.free = [ctx_done[b]]
                    kt.free = [ctx_done[b]]

                def output(i, part):
                    for h in range(4 * part, 4 * part + 4):
                        step = lambda e, h=h: e.matmul(o_bank.ap, qT[:, i, h, :], wn[:, h, :], start=h == 0, stop=h == XH - 1)
                        waits = (list(o_bank.free) if h == 0 else None, ctx_done[i * BPT + BPT - 1], wn_done)
                        if h < XH - 1:
                            pe.quiet(step, *waits)
                        else:
                            m = pe(step, *waits)
                            done = dve(lambda e: e.tensor_tensor(x[:, i, :], x[:, i, :], o_bank.ap, ALU.add), m)
                            o_bank.free = [done]
                            x_written(i, done)

                LAG_TURN, LAG_VALUES = 2, 3
                FIRST = XH - (LAG_VALUES + BPT)
                keys(0)
                keys(1)
                for h in range(FIRST):
                    fold_out(h, (o_bank, c_bank)[h % 2])
                keys_T(0)
                for b in range(B + LAG_VALUES + BPT):
                    if b < B:
                        scores(b)
                    if 0 <= b - LAG_VALUES < B:
                        values(b - LAG_VALUES)
                    if FIRST + b < XH:
                        fold_out(FIRST + b, o_bank)
                    if b + 2 < B:
                        keys(b + 2)
                    if b + 1 < B:
                        keys_T(b + 1)
                    if 0 <= b - LAG_TURN < B:
                        turn(b - LAG_TURN)
                    if b < B:
                        weigh(b)
                    if b >= LAG_VALUES + BPT:
                        output((b - LAG_VALUES) // BPT - 1, (b - LAG_VALUES) % BPT)

        def self_attention(name, groups, normed):
            nonlocal ln_banks
            start = phase_start()
            tpg = AT // groups
            kw = groups * P
            vw = groups * P if normed else groups * DH
            with ExitStack() as arena:
                def sb(n, shape, dt=F32):
                    return arena.enter_context(nc.sbuf_tensor(f"{name}_{n}", shape, dt))

                wq, wq_ready = load_weights(d[f"{name}_wq"], KD * D)
                wk, wk_ready = load_weights(d[f"{name}_wk"], KD * kw)
                wv, wv_ready = load_weights(d[f"{name}_wv"], KD * vw)
                banks_o = ln_banks = Ring([Slot(psum(7))])
                hT = Ring([Slot(tuple(sb(f"hT_{v}{i}", [P, KD, P], F32R) for v in ("hi", "lo"))) for i in range(3)])
                H = {}
                NORM = dict(enumerate(ahead))

                def turn_input(i):
                    dst = hT.take()

                    def sink(i, src, after):
                        b_major = tuple(v[:, :, :].rearrange("p k (b s) -> p k b s", s=S) for v in dst.ap)
                        return split(b_major, src.rearrange("p k (s b) -> p k b s", s=S), [after, list(dst.free)])

                    H[i] = (dst, turn_tile(i, NORM[i], sink))

                turn_input(0)
                mask = sb("mask", [P, S])
                tabs = Slot(None, sem(f"s_{name}_tabs"))
                dma(tabs, mask[:], d["mask"], start)
                if normed:
                    cosg, sing = sb("cosg", [P, 2, DH]), sb("sing", [P, 2, DH])
                    gam = sb("gam", [P, 4, DH])
                    for n, g in enumerate(("gq", "gq_roll", "gk", "gk_roll")):
                        dma(tabs, gam[:, n, :], d[g].to_broadcast([P, DH]))
                    for n in range(2):
                        dma(tabs, cosg[:, n, :], d["acos"])
                        tabs_ready = dma(tabs, sing[:, n, :], d["asin"])
                else:
                    bias = {}
                    for key, n in (("bq", D), ("bk", kw), ("bv", vw), ("bo", D)):
                        bias[key] = sb(key, [P, n])
                        tabs_ready = dma(tabs, bias[key][:], d[f"{name}_{key}"].to_broadcast([P, n]))

                w_q, w_k, w_v = (tuple(sb(f"{key}_{v}", [P, KD, n], F32R) for v in ("hi", "lo"))
                                 for key, n in (("wq", D), ("wk", kw), ("wv", vw)))
                w_ready = []
                for dst, slot, ready, n in ((w_q, wq, wq_ready, D), (w_k, wk, wk_ready, kw), (w_v, wv, wv_ready, vw)):
                    w_ready.append(split(cut(dst, slice(None)), slot.ap[:, 0:KD * n].rearrange("p (k n) -> p k n", k=KD),
                                         [ready], act, pool if slot is wk else dve))
                    slot.free = w_ready[-1]
                if normed:
                    g1 = dve(lambda e: e.tensor_tensor(cosg[:], cosg[:], gam[:, 0::2, :], ALU.mult), tabs_ready)
                    g2 = dve(lambda e: e.tensor_tensor(sing[:], sing[:], gam[:, 1::2, :], ALU.mult), tabs_ready)
                    table_done = [g1, g2]
                else:
                    table_done = [tabs_ready]
                wo, wo_ready = load_weights(d[f"{name}_wo"], KD * D)
                w_o = wo.ap[:, 0:KD * D].rearrange("p (k n) -> p k n", k=KD)

                kbd = Ring([Slot(sb(f"kbd{i}", [P, groups, BPT, P])) for i in range(2)])
                vbd = Ring([Slot(sb(f"vbd{i}", [P, BPT, groups, P])) for i in range(3)])
                for r in (kbd, vbd):
                    for s_ in r.slots:
                        s_.free = [pool(lambda e, s_=s_: e.memset(s_.ap[:], 0.0))]
                qn = Ring([Slot(sb(f"qn{i}", [P, D])) for i in range(3)])
                kn = Ring([Slot(sb(f"kn{i}", [P, kw])) for i in range(3)])
                vn = Ring([Slot(sb(f"vn{i}", [P, vw])) for i in range(3)])
                qTb = Ring([Slot(sb(f"qTb{i}", [P, AT, P])) for i in range(2)])
                pr = Ring([Slot(sb(f"pr{i}", [P, AH, S])) for i in range(2)])
                pTb = Ring([Slot(sb(f"pTb{i}", [P, AT, P])) for i in range(2)])
                oTb = Ring([Slot(sb(f"oTb{i}", [P, AT, P])) for i in range(2)])
                if normed:
                    sq, part_c, part_s = ([sb(f"{key}{w}", [P, *shape]) for w in range(2)]
                                          for key, shape in (("sq", (D,)), ("part_c", (AH, DH)), ("part_s", (AH, DH))))
                tiny = sb("tiny", [P, NT, 8, AH])
                banks_qkv = Ring([Slot(psum(i)) for i in range(3)])
                banks_t = Ring([Slot(psum(3)), Slot(psum(4))])
                banks_a = Ring([Slot(psum(5)), Slot(psum(6))])
                Q, K, V, QT, KB, VB, PB, OB, EX, PTB, PJ = ({} for _ in range(11))

                heads = lambda ap: ap.rearrange("p (h d) -> p h d", d=DH)

                def head_norms(i, todo):
                    ss, rs = ([tiny[:, i, 2 * w + n, :] for w in range(2)] for n in range(2))
                    m, copied = {}, {}
                    for w, (src, dst, ready) in enumerate(todo):
                        m[w] = act(lambda e, w=w, src=src: e.activation(sq[w][:], src, ACT.Square), ready, sq_free[w])
                        copied[w] = act(lambda e, src=src, dst=dst: e.copy(dst.ap[:], src), ready, list(dst.free))
                    for w in range(2):
                        m[w] = dve(lambda e, w=w: e.tensor_reduce(ss[w], heads(sq[w][:]), AX_X, ALU.add), m[w])
                        sq_free[w] = m[w]
                    for w in range(2):
                        m[w] = dve(lambda e, w=w: e.tensor_scalar(ss[w], ss[w], 1.0 / DH, 1e-6, ALU.mult, ALU.add), m[w])
                        m[w] = pool(lambda e, w=w: e.tensor_tensor(rs[w], ss[w], power[:], ALU.pow), m[w])
                    return m, copied

                def normalise(i, todo, m, copied):
                    across = lambda ap: ap.rearrange("p (o d) -> p o d", o=1).to_broadcast([P, AH, ap.shape[-1]])
                    hd = DH // 2
                    rs = [tiny[:, i, 2 * w + 1, :] for w in range(2)]
                    scaled, cosd, sind, out_ = {}, {}, {}, {}
                    for w, (_, dst, _) in enumerate(todo):
                        scaled[w] = dve(lambda e, w=w, dst=dst: e.tensor_tensor(
                            heads(dst.ap[:]), heads(dst.ap[:]), rs[w].rearrange("p (h o) -> p h o", o=1).to_broadcast([P, AH, DH]),
                            ALU.mult), m[w], copied[w])
                    for w, (src, dst, _) in enumerate(todo):
                        cosd[w] = dve(lambda e, w=w, dst=dst: e.tensor_tensor(
                            part_c[w][:], heads(dst.ap[:]), across(cosg[:, w, :]), ALU.mult), scaled[w], table_done, part_free[w])
                        for lo, hi in ((0, hd), (hd, 0)):
                            sind[w] = pool(lambda e, w=w, dst=dst, lo=lo, hi=hi: e.tensor_tensor(
                                part_s[w][:, :, lo:lo + hd], heads(dst.ap[:])[:, :, hi:hi + hd],
                                across(sing[:, w, lo:lo + hd]), ALU.mult), scaled[w], table_done, part_free[w])
                    for w, (src, dst, _) in enumerate(todo):
                        out_[w] = dve(lambda e, w=w, dst=dst: e.tensor_tensor(heads(dst.ap[:]), part_c[w][:], part_s[w][:], ALU.add),
                                      cosd[w], sind[w])
                        part_free[w] = out_[w]
                    return out_

                sq_free, part_free = [None, None], [None, None]

                def project(i):
                    src, h_ready = H[i]
                    got = []
                    for which, (w_, n, ring, ready) in enumerate(
                            ((w_q, D, qn, w_ready[0]), (w_k, kw, kn, w_ready[1]), (w_v, vw, vn, w_ready[2]))):
                        bank, dst = banks_qkv.take(), ring.take()
                        m = mm_group(bank.ap[:, 0:n], [p for k in range(KD) for p in parts(
                            cut(src.ap, slice(None), k, slice(None)), cut(w_, slice(None), k, slice(None)))],
                                     (list(bank.free), ready, h_ready))
                        if not normed:
                            bv = bias[("bq", "bk", "bv")[which]]
                            done = dve(lambda e, bank=bank, dst=dst, n=n, bv=bv: e.tensor_tensor(
                                dst.ap[:], bank.ap[:, 0:n], bv[:], ALU.add), m, list(dst.free), table_done)
                        if not normed:
                            bank.free = [done]
                            (Q, K, V)[which][i] = (dst, done)
                        got.append((bank, dst, m))
                    src.free = [m]
                    if normed:
                        todo = [(bank.ap, dst, m) for bank, dst, m in got[:2]]
                        norms, copied = head_norms(i, todo)
                        for w in range(2):
                            got[w][0].free = [copied[w]]
                        PJ[i] = (todo, norms, copied)
                        bank, dst, m = got[2]
                        done = act(lambda e: e.copy(dst.ap[:], bank.ap), m, list(dst.free))
                        bank.free = [done]
                        V[i] = (dst, done)

                def finish_projection(i):
                    if normed:
                        todo, norms, copied = PJ[i]
                        done = normalise(i, todo, norms, copied)
                        for w in range(2):
                            (Q, K)[w][i] = (todo[w][1], done[w])

                def spread(i):
                    qsrc, ready = Q[i]
                    bank, dst = banks_t.take(), qTb.take()
                    for t in range(AT):
                        step = lambda e, t=t: e.transpose(bank.ap[:, t * P:(t + 1) * P], qsrc.ap[:, t * P:(t + 1) * P], ident[:])
                        m = pe(step, ready, list(bank.free))
                    qsrc.free = [m]
                    done = act(lambda e: e.copy(dst.ap[:].rearrange("p t n -> p (t n)"), bank.ap), m, list(dst.free))
                    bank.free = [done]
                    QT[i] = (dst, done)
                    ksrc, ready = K[i]
                    kbank, kdst = banks_t.take(), kbd.take()
                    for t in range(groups):
                        step = lambda e, t=t: e.transpose(kbank.ap[:, t * P:(t + 1) * P], ksrc.ap[:, t * P:(t + 1) * P], ident[:])
                        m = pe(step, ready, list(kbank.free))
                    ksrc.free = [m]
                    marks = []
                    for j in range(HPT):
                        rows = slice(j * DH, (j + 1) * DH)
                        o = kdst.ap[rows, :, :, j * S:(j + 1) * S]
                        s_ = kbank.ap[rows, 0:groups * P].rearrange("p (t b s) -> p t b s", t=groups, s=S)
                        if j % 2:
                            marks.append(act(lambda e, o=o, s_=s_: e.copy(o, s_), m, list(kdst.free)))
                        else:
                            marks.append(dve(lambda e, o=o, s_=s_: e.tensor_copy(o, s_), m, list(kdst.free)))
                    kbank.free = marks
                    KB[i] = (kdst, marks)
                    vsrc, ready = V[i]
                    vdst = vbd.take()
                    marks = []
                    for b in range(BPT):
                        for j in range(HPT):
                            o = vdst.ap[j * S:(j + 1) * S, b, :, j * DH:(j + 1) * DH]
                            s_ = vsrc.ap[b * S:(b + 1) * S, :].rearrange("p (t j d) -> p t j d", t=groups, d=DH)
                            s_ = s_[:, :, j if normed else 0, :]
                            if j % 2:
                                marks.append(act(lambda e, o=o, s_=s_: e.copy(o, s_), ready, list(vdst.free)))
                            else:
                                marks.append(dve(lambda e, o=o, s_=s_: e.tensor_copy(o, s_), ready, list(vdst.free)))
                    vsrc.free = marks
                    VB[i] = (vdst, marks)

                def attend(i):
                    qt, q_ready = QT[i]
                    kb, k_ready = KB[i]
                    bank, dst = banks_a.take(), pr.take()
                    for b in range(BPT):
                        for t in range(AT):
                            m = mm_group(bank.ap[b * S:(b + 1) * S, t * P:(t + 1) * P],
                                         [(qt.ap[:, t, b * S:(b + 1) * S], kb.ap[:, t // tpg, b, :])],
                                         (list(bank.free), q_ready, k_ready))
                    qt.free = [m]
                    kb.free = [m]
                    mx = tiny[:, i, 4, :]
                    bc = lambda ap: ap.rearrange("p (h o) -> p h o", o=1).to_broadcast([P, AH, S])
                    sc = bank.ap.rearrange("p (h s) -> p h s", s=S)
                    c1 = dve(lambda e: e.tensor_tensor(dst.ap[:], sc, mask[:].rearrange("p (o s) -> p o s", o=1).to_broadcast([P, AH, S]),
                                                       ALU.add), m, table_done, list(dst.free))
                    bank.free = [c1]
                    c2 = dve(lambda e: e.tensor_reduce(mx, dst.ap[:], AX_X, ALU.max), c1)
                    c3 = (dve if normed else pool)(lambda e: e.tensor_tensor(dst.ap[:], dst.ap[:], bc(mx), ALU.subtract), c2)
                    c4 = act(lambda e: e.activation(dst.ap[:], dst.ap[:], ACT.Exp, scale=float(DH) ** -0.5), c3)
                    EX[i] = (dst, c4)

                def weigh(i):
                    dst, c4 = EX[i]
                    sm, rc = tiny[:, i, 5, :], tiny[:, i, 6, :]
                    bc = lambda ap: ap.rearrange("p (h o) -> p h o", o=1).to_broadcast([P, AH, S])
                    c5 = dve(lambda e: e.tensor_reduce(sm, dst.ap[:], AX_X, ALU.add), c4)
                    c6 = dve(lambda e: e.reciprocal(rc, sm), c5)
                    c7 = pool(lambda e: e.tensor_tensor(dst.ap[:], dst.ap[:], bc(rc), ALU.mult), c6)
                    PB[i] = (dst, c7)

                def turn_weights(i):
                    src, ready = PB[i]
                    bank, dst = banks_t.take(), pTb.take()
                    for t in range(AT):
                        m = pe(lambda e, t=t: e.transpose(bank.ap[:, t * P:(t + 1) * P],
                                                          src.ap[:, t * HPT:(t + 1) * HPT, :], ident[:]),
                               ready, list(bank.free))
                    src.free = [m]
                    done = act(lambda e: e.copy(dst.ap[:].rearrange("p t n -> p (t n)"), bank.ap), m, list(dst.free))
                    bank.free = [done]
                    PTB[i] = (dst, done)

                def mix(i):
                    dst, done = PTB[i]
                    vb, v_ready = VB[i]
                    obank, odst = banks_a.take(), oTb.take()
                    for t in range(AT):
                        for b in range(BPT):
                            at = t * P + b * S
                            m = mm_group(obank.ap[:, at:at + S], [(vb.ap[:, b, t // tpg, :], dst.ap[:, t, b * S:(b + 1) * S])],
                                         (list(obank.free), v_ready, done))
                    vb.free = [m]
                    dst.free = [m]
                    odone = dve(lambda e: e.tensor_copy(
                        odst.ap[:].rearrange("p t (s b) -> p t b s", s=S),
                        obank.ap.rearrange("p (t b s) -> p t b s", t=AT, s=S)), m, list(odst.free))
                    obank.free = [odone]
                    OB[i] = (odst, odone)

                def output(i):
                    src, ready = OB[i]
                    bank = banks_o.take()
                    m = mm_group(bank.ap, [(src.ap[:, t, :], w_o[:, t, :]) for t in range(AT)],
                                 (list(bank.free), ready, wo_ready))
                    src.free = [m]
                    done = dve(lambda e: e.tensor_tensor(x[:, i, :], x[:, i, :], bank.ap, ALU.add), m)
                    bank.free = [done]
                    if not normed:
                        done = pool(lambda e: e.tensor_tensor(x[:, i, :], x[:, i, :], bias["bo"][:], ALU.add), done)
                    x_written(i, done)

                def run(stage, i):
                    if 0 <= i < NT:
                        stage(i)

                def normalise_input(i):
                    NORM[i] = normalise_tile(i)

                for i in range(NT + 5):
                    run(project, i)
                    run(turn_input, i + 1)
                    run(attend, i - 3)
                    run(mix, i - 5)
                    run(spread, i - 2)
                    run(turn_weights, i - 4)
                    run(normalise_input, i + 2)
                    run(weigh, i - 3)
                    run(output, i - 5)
                    run(finish_projection, i)
                wo.free = [pe.now()]

        def hadamard_ffn(name):
            nonlocal ln_banks
            start = phase_start()
            with ExitStack() as arena:
                def sb(n, shape, dt=F32):
                    return arena.enter_context(nc.sbuf_tensor(f"{name}_{n}", shape, dt))

                WDT = [load_weights(d["wdT"][q], 4 * D) for q in range(2)]
                down = sb("down", [P, FC, D])
                z = sb("z", [P, FC, TOK])
                other = z[:, FC // 2:FC, :].rearrange("p a n -> p (a n)").rearrange("p (a n) -> p a n", a=FC)
                had = sb("had", [P, 2, P])
                su_ug = sb("su_ug", [P, KD])
                su_dp = sb("su_dp", [P, FC])
                ws_up = sb("ws_up", [P, FC])
                ws_gate = sb("ws_gate", [P, FC])
                ws_down = sb("ws_down", [P, D])
                su = sb("su", [P, FC])
                ugs = Ring([Slot(tuple(sb(f"ug_{v}{i}", [P, KD * P], F32R) for v in ("hi", "lo"))) for i in range(3)])
                sg = Ring([Slot(sb(f"sg{i}", [P, TOK])) for i in range(2)])
                tabs = Slot(None, sem(f"s_{name}_tabs"))
                for dst, key in ((su_ug[:], "su_ug"), (had[:].rearrange("p a n -> p (a n)"), "had"), (su_dp[:], "su_dp"),
                                 (ws_up[:], "ws_up"), (ws_gate[:], "ws_gate")):
                    dma(tabs, dst, d[key], start)
                tabs_ready = dma(tabs, ws_down[:], d["ws_down"].to_broadcast([P, D]), start)
                scaled = dve(lambda e: e.tensor_tensor(su[:], ws_up[:], su_dp[:], ALU.mult), tabs_ready)

                hT = tuple(sb(f"hT_{v}", [P, KD, TOK], F32R) for v in ("hi", "lo"))
                hs = z[:, 4:8, :]

                def scale_sink(i, src, after):
                    scale = su_ug[:].rearrange("p (k o) -> p k o", o=1).to_broadcast([P, KD, P])
                    return [dve(lambda e: e.tensor_tensor(hs[:, :, i * P:(i + 1) * P], src, scale, ALU.mult), after, tabs_ready)]

                ln_banks = Ring([Slot(psum(6)), Slot(psum(7))])
                h_ready = layernorm(scale_sink)

                def butterfly_ops(src, dst, stride):
                    n = src.shape[1]
                    return [(dst[:, at + (stride if op == ALU.subtract else 0), :], src[:, at, :], src[:, at + stride, :], op)
                            for at in range(n) if not at & stride for op in (ALU.add, ALU.subtract)]

                def butterfly(eng, src, dst, stride, after):
                    return [eng(lambda e, o=o: e.tensor_tensor(*o), after) for o in butterfly_ops(src, dst, stride)]

                room = {(t, v): z[:, 8 * t + 2 * v:8 * t + 2 * v + 2, :].rearrange("p a n -> p (a n)")
                        .rearrange("p (k n) -> p k n", k=KD) for t in range(2) for v in range(2)}
                hx_ready = []
                banks_h = Ring([Slot(psum(i)) for i in range(4)])
                mixed = []
                for t in range(TOK // BANK):
                    cols_ = slice(t * BANK, (t + 1) * BANK)
                    got = []
                    for k in range(KD):
                        bank = banks_h.take()
                        m = mm_group(bank.ap, [(had[:, 0, :], hs[:, k, cols_])],
                                     (list(bank.free), h_ready[4 * t:4 * t + 4], tabs_ready))
                        got.append(act(lambda e, t=t, k=k, bank=bank: e.copy(room[t, 0][:, k, :], bank.ap), m))
                        bank.free = [got[-1]]
                    one = butterfly(dve, room[t, 0], room[t, 1], 1, got)
                    mixed.append(butterfly(dve, room[t, 1], room[t, 0], 2, one))

                got = []
                banks_d = Ring([Slot(psum(4)), Slot(psum(5))])
                for q in range(FC // 4):
                    slot, ready = WDT[q] if q < 2 else load_weights(d["wdT"][q], 4 * D)
                    for a in range(4):
                        bank = banks_d.take()
                        m = mm_group(bank.ap, [(had[:, 1, :], slot.ap[:, a * D:(a + 1) * D])], (list(bank.free), ready, tabs_ready))
                        got.append(act(lambda e, n=4 * q + a, bank=bank: e.copy(down[:, n, :], bank.ap), m))
                        bank.free = [got[-1]]
                    slot.free = [m]
                    if q < 2:
                        hx_ready.append(split(tuple(v[:, :, q * BANK:(q + 1) * BANK] for v in hT), room[q, 0], mixed[q],
                                              act, dve if q else pool))
                pairs = Ring([Slot(psum(2 * i, 2)) for i in range(4)])
                for n, s_ in enumerate(pairs.slots):
                    s_.free = [[banks_h, banks_h, banks_d, ln_banks][n].slots[j + (2 if n == 1 else 0)].free for j in range(2)]
                    s_.free = [m for f in s_.free for m in f]
                stages = [(down[:], other, 1), (other, down[:], 2), (down[:], other, 4), (other, down[:], 8)]
                stage_marks = [[got, hx_ready]]

                def butterfly_steps():
                    for src, dst, stride in stages:
                        marks = []
                        before = stage_marks[-1]
                        for n, o in enumerate(butterfly_ops(src, dst, stride)):
                            marks.append((dve if n % 2 else pool)(lambda e, o=o: e.tensor_tensor(*o), before))
                            yield
                        stage_marks.append(marks)

                steps = butterfly_steps()
                uw = {}

                def split_up(n):
                    a, u = n // 2, 1 - n % 2
                    if n % 4 == 0:
                        uw["slot"] = load_weights(d["wug"][a // 2], 2 * 2 * KD * P)
                    slot, landed = uw["slot"]
                    at = ((a % 2) * 2 + u) * KD * P
                    w_ = ugs.take()
                    uw[n] = (w_, split(cut(w_.ap, slice(None)), slot.ap[:, at:at + KD * P], [landed, list(w_.free)], act, pool))
                    if n % 4 == 3:
                        slot.free = uw[n][1]

                split_up(0)
                z_ready = []
                for a in range(FC):
                    gate, up = pairs.take(), pairs.take()
                    for u, unit in ((1, gate), (0, up)):
                        n = 2 * a + 1 - u
                        if n + 1 < 2 * FC:
                            split_up(n + 1)
                        w_, ready = uw[n]
                        for t in range(2):
                            m = mm_group(unit.ap[:, t * BANK:(t + 1) * BANK],
                                         [p for k in range(KD) for p in parts(
                                             cut(w_.ap, slice(None), slice(k * P, (k + 1) * P)),
                                             cut(hT, slice(None), k, slice(t * BANK, (t + 1) * BANK)))],
                                         (list(unit.free), ready, hx_ready[t]))
                        w_.free = [m]
                        if u == 1:
                            sgb = sg.take()
                            g1 = act(lambda e, a=a, sgb=sgb, unit=unit: e.activation(sgb.ap[:], unit.ap, ACT.Silu,
                                                                                     scale=ws_gate[:, a:a + 1]),
                                     m, list(sgb.free), tabs_ready)
                            unit.free = [g1]
                    z1 = dve(lambda e, a=a, sgb=sgb, up=up: e.scalar_tensor_tensor(
                        out=z[:, a, :], in0=up.ap, scalar=su[:, a:a + 1], in1=sgb.ap[:], op0=ALU.mult, op1=ALU.mult),
                        m, g1, scaled, stage_marks[4] if a >= FC // 2 else hx_ready)
                    up.free = [z1]
                    sgb.free = [z1]
                    for _ in range(9):
                        next(steps, None)
                    z_ready.append(z1)

                tail_banks = Ring([Slot(psum(i)) for i in range(8)])
                for n, s_ in enumerate(tail_banks.slots):
                    s_.free = list(pairs.slots[n // 2].free)
                for i in range(NT):
                    bank = tail_banks.take()
                    m = mm_group(bank.ap, [(z[:, a, i * P:(i + 1) * P], down[:, a, :]) for a in range(FC)],
                                 (list(bank.free), z_ready, stage_marks[4]))
                    buf = xn.take()
                    f1 = dve(lambda e, bank=bank, buf=buf: e.tensor_tensor(buf.ap[:], bank.ap, ws_down[:], ALU.mult), m, list(buf.free))
                    f2 = dve(lambda e, i=i, buf=buf: e.tensor_tensor(x[:, i, :], x[:, i, :], buf.ap[:], ALU.add), f1)
                    bank.free = [f1]
                    buf.free = [f2]
                    x_written(i, f2)

        def experts(name):
            nonlocal ln_banks
            phase_start()
            with ExitStack() as arena:
                def sb(n, shape, dt=F32):
                    return arena.enter_context(nc.sbuf_tensor(f"{name}_{n}", shape, dt))

                gate = sb("gate", [P, KD, NE])
                alpha = sb("alpha", [P, 1])
                iota = sb("iota", [P, NE])
                order = sb("order", [P, TOPK])
                tabs = Slot(None, sem(f"s_{name}_tabs"))
                dma(tabs, gate[:].rearrange("p k n -> p (k n)"), d["gate"], queue=act)
                dma(tabs, iota[:], d["iota"], queue=act)
                dma(tabs, order[:], d["order"], queue=act)
                tabs_ready = dma(tabs, alpha[:], d["alpha"].to_broadcast([P, 1]), queue=act)
                hT = tuple(sb(f"hT_{v}", [P, KD, TOK], F32R) for v in ("hi", "lo"))

                cT = sb("cT", [NE, TOK])
                combine = sb("combine", [P, NT, NE])
                pb = sb("pb", [P, NT, NE])
                top = sb("top", [P, NT, TOPK])
                at = sb("at", [P, NT, TOPK], U32)
                atf = sb("atf", [P, NT, TOPK])
                rw = sb("rw", [P, NT, TOPK])
                act_ = sb("act_", [P, NT, TOPK])
                fb = sb("fb", [P, NT, TOPK])
                one = sb("one", [P, 10, NT])

                def chain(step, *after):
                    return dve(step, dve.now(), *after)

                def lone(step, *after):
                    return pool(step, pool.now(), *after)

                def per_tile(ap, n):
                    return ap.rearrange("p (i o) -> p i o", o=1).to_broadcast([P, NT, n])

                gates = tuple(sb(f"gate_{v}", [P, KD, NE], F32R) for v in ("hi", "lo"))
                gate_ready = split(cut(gates, slice(None)), gate[:], [tabs_ready])
                ln_banks = Ring([Slot(psum(0)), Slot(psum(1))])
                wgu = Ring([Slot(tuple(sb(f"wgu_{v}{i}", [P, KD * 2 * EI], F32R) for v in ("hi", "lo"))) for i in range(2)])
                wdn = Ring([Slot(tuple(sb(f"wdn_{v}{i}", [P, 3 * D], F32R) for v in ("hi", "lo"))) for i in range(2)])
                z1b = Ring([Slot(tuple(sb(f"z1_{v}{i}", [P, TOK], F32R) for v in ("hi", "lo"))) for i in range(3)])
                z2b = Ring([Slot(tuple(sb(f"z2_{v}{i}", [P, TOK], F32R) for v in ("hi", "lo"))) for i in range(2)])
                work = Ring([Slot(sb(f"work{i}", [P, TOK])) for i in range(3)])
                crow = Ring([Slot(sb(f"crow{i}", [P, TOK]), sem(f"s_{name}_c{i}")) for i in range(2)])
                W, WD, WG, C, Z1, Z2 = ({} for _ in range(6))
                rows_stored = [None]
                GU = KD * 2 * EI

                def fetch(e_):
                    W[e_] = load_weights(d["experts"][e_], SLOT if e_ % 2 == 0 else SLOT - D)

                def fetch_row(e_):
                    row = crow.take()
                    C[e_] = (row, dma(row, row.ap[:], combine_rows[e_:e_ + 1, :].to_broadcast([P, TOK]),
                                      list(row.free), rows_stored[0]))

                def split_weights(e_):
                    slot, ready = W[e_]
                    dst = wgu.take()
                    WG[e_] = (dst, split(cut(dst.ap, slice(None)), slot.ap[:, 0:GU], [ready, list(dst.free)], act, lone))
                    if e_ % 2 == 0:
                        WD[e_ // 2] = (wdn.take(), [])
                    down, marks = WD[e_ // 2]
                    at, n = (0, 2 * D) if e_ % 2 == 0 else (2 * D, D)
                    marks += split(cut(down.ap, slice(None), slice(at, at + n)), slot.ap[:, GU:GU + n],
                                   [ready, list(down.free)], act, lone)
                    slot.free = WG[e_][1] + marks[-2:]

                fetch(0)
                fetch(1)
                split_weights(0)
                h_ready = layernorm(split_sink(hT))
                wide_rows, tall_rows = psum(6, 2), psum(4)
                for t in range(TOK // BANK):
                    m = mm_group(wide_rows[0:NE, t * BANK:(t + 1) * BANK],
                                 [p for k in range(KD) for p in parts(tuple(v[:, k, :] for v in gates),
                                                                      cut(hT, slice(None), k, slice(t * BANK, (t + 1) * BANK)))],
                                 (h_ready[4 * t:4 * t + 4], gate_ready))
                copied = act(lambda e: e.copy(cT[:], wide_rows[0:NE, :]), m)
                for i in range(NT):
                    m = pe(lambda e, i=i: e.transpose(tall_rows[:, i * NE:(i + 1) * NE], cT[:, i * P:(i + 1) * P],
                                                      ident[0:NE, 0:NE]), copied)
                lg = tall_rows[:, 0:NT * NE].rearrange("p (i n) -> p i n", i=NT)
                chain(lambda e: e.tensor_reduce(one[:, 0, :], lg, AX_X, ALU.max), m)
                c1 = chain(lambda e: e.tensor_tensor(pb[:], lg, per_tile(one[:, 0, :], NE), ALU.subtract))
                c2 = act(lambda e: e.activation(pb[:], pb[:], ACT.Exp), c1)
                chain(lambda e: e.tensor_reduce(one[:, 1, :], pb[:], AX_X, ALU.add), c2)
                chain(lambda e: e.reciprocal(one[:, 2, :], one[:, 1, :]))
                chain(lambda e: e.tensor_tensor(pb[:], pb[:], per_tile(one[:, 2, :], NE), ALU.mult))
                for i in range(NT):
                    chain(lambda e, i=i: e.max(top[:, i, :], pb[:, i, :]))
                    chain(lambda e, i=i: e.max_index(at[:, i, :], top[:, i, :], pb[:, i, :]))
                chain(lambda e: e.tensor_copy(atf[:], at[:]))
                chain(lambda e: e.tensor_reduce(one[:, 3, :], top[:], AX_X, ALU.add))
                chain(lambda e: e.tensor_scalar(one[:, 3, :], one[:, 3, :], 1e-12, None, ALU.max))
                chain(lambda e: e.reciprocal(one[:, 3, :], one[:, 3, :]))
                chain(lambda e: e.tensor_tensor(rw[:], top[:], per_tile(one[:, 3, :], TOPK), ALU.mult))
                chain(lambda e: e.tensor_scalar(top[:], rw[:], alpha[:, 0:1], None, ALU.mult))
                chain(lambda e: e.tensor_scalar(act_[:], top[:], TAU, None, ALU.is_ge))
                chain(lambda e: e.tensor_reduce(one[:, 4, :], act_[:], AX_X, ALU.max))
                chain(lambda e: e.tensor_scalar(one[:, 4, :], one[:, 4, :], -1.0, 1.0, ALU.mult, ALU.add))
                chain(lambda e: e.tensor_reduce(one[:, 5, :], top[:], AX_X, ALU.max))
                chain(lambda e: e.tensor_tensor(fb[:], top[:], per_tile(one[:, 5, :], TOPK), ALU.is_equal))
                orders = order[:].rearrange("p (o n) -> p o n", o=1).to_broadcast([P, NT, TOPK])
                chain(lambda e: e.tensor_tensor(fb[:], fb[:], orders, ALU.mult))
                chain(lambda e: e.tensor_reduce(one[:, 6, :], fb[:], AX_X, ALU.max))
                chain(lambda e: e.tensor_tensor(fb[:], orders, per_tile(one[:, 6, :], TOPK), ALU.is_equal))
                chain(lambda e: e.tensor_tensor(fb[:], fb[:], per_tile(one[:, 4, :], TOPK), ALU.mult))
                chain(lambda e: e.tensor_tensor(act_[:], act_[:], fb[:], ALU.max))
                chain(lambda e: e.tensor_tensor(rw[:], rw[:], act_[:], ALU.mult))
                chain(lambda e: e.tensor_reduce(one[:, 7, :], rw[:], AX_X, ALU.add))
                chain(lambda e: e.tensor_scalar(one[:, 7, :], one[:, 7, :], 1e-12, None, ALU.max))
                chain(lambda e: e.reciprocal(one[:, 7, :], one[:, 7, :]))
                chain(lambda e: e.tensor_tensor(rw[:], rw[:], per_tile(one[:, 7, :], TOPK), ALU.mult))
                pick = sb("pick", [P, NT, NE])
                over_tiles = iota[:].rearrange("p (o n) -> p o n", o=1).to_broadcast([P, NT, NE])
                over_experts = lambda ap: ap.to_broadcast([P, NT, NE])
                for k in range(TOPK):
                    dst = pick if k else combine
                    chain(lambda e, k=k, dst=dst: e.tensor_tensor(dst[:], over_tiles, over_experts(atf[:, :, k:k + 1]), ALU.is_equal))
                    chain(lambda e, k=k, dst=dst: e.tensor_tensor(dst[:], dst[:], over_experts(rw[:, :, k:k + 1]), ALU.mult))
                    if k:
                        chain(lambda e: e.tensor_tensor(combine[:], combine[:], pick[:], ALU.add))
                routed = dve.now()

                units = Ring([Slot(psum(0, 2)), Slot(psum(2, 2)), Slot(psum(4, 2))])
                units.slots[0].free = ln_banks.slots[0].free + ln_banks.slots[1].free
                units.slots[2].free = [c1]

                def hidden(e_):
                    w_, ready = WG[e_]

                    def product(col):
                        unit = units.take()
                        for t in range(2):
                            m = mm_group(unit.ap[:, t * BANK:(t + 1) * BANK],
                                         [p for k in range(KD) for p in parts(
                                             cut(w_.ap, slice(None), slice(k * 2 * EI + col, k * 2 * EI + col + P)),
                                             cut(hT, slice(None), k, slice(t * BANK, (t + 1) * BANK)))],
                                         (list(unit.free), ready, h_ready))
                        return unit, m

                    def begin(gate_ap, g_done, rows):
                        buf = work.take()
                        return buf, act(lambda e: e.activation(buf.ap[rows, :], gate_ap, ACT.Silu), g_done, list(buf.free))

                    def weigh(buf, a1, rows):
                        row, row_ready = C[e_]
                        return lone(lambda e: e.tensor_tensor(buf.ap[rows, :], buf.ap[rows, :], row.ap[rows, :], ALU.mult),
                                    a1, row_ready)

                    def finish(buf, a2, up_ap, u_done, rows, dst, dst_free, lo_engine):
                        b_ = buf.ap[rows, :]
                        a3 = dve(lambda e: e.tensor_tensor(b_, up_ap, b_, ALU.mult), a2, u_done)
                        buf.free = split(tuple(v[rows, :] for v in dst.ap), b_, [a3, dst_free], lo_engine=lo_engine)
                        return a3

                    everything = slice(0, P)
                    mine, other = (slice(0, E2), slice(E2, P)) if e_ % 2 == 0 else (slice(E2, P), slice(0, E2))
                    if e_ == NE - 1:
                        gu, gu_done = product(P)
                        buf2, b1 = begin(gu.ap[other, :], gu_done, mine)
                    g, g_done = product(0)
                    buf1, a1 = begin(g.ap, g_done, everything)
                    g.free = [a1]
                    u, u_done = product(2 * P)
                    if e_ < NE - 1:
                        gu, gu_done = product(P)
                        buf2, b1 = begin(gu.ap[other, :], gu_done, mine)
                    w_.free = [gu_done, u_done]

                    def finish_first():
                        a2 = weigh(buf1, a1, everything)
                        z1 = z1b.take()
                        u.free = [finish(buf1, a2, u.ap, u_done, everything, z1, list(z1.free), dve)]
                        Z1[e_] = (z1, buf1.free)

                    def finish_rest():
                        if e_ % 2 == 0:
                            Z2[e_ // 2] = (z2b.take(), [])
                        z2, marks = Z2[e_ // 2]
                        a2 = weigh(buf2, b1, mine)
                        b3 = finish(buf2, a2, gu.ap[mine, :], gu_done, mine, z2, list(z2.free), lone)
                        gu.free = [b1, b3]
                        marks += buf2.free
                        C[e_][0].free = [b3]

                    return finish_first, finish_rest

                first = hidden(0)
                split_weights(1)

                unit = Slot(psum(6, 2))
                for i in range(NT):
                    m = pe(lambda e, i=i: e.transpose(unit.ap[0:NE, i * P:(i + 1) * P], combine[:, i, :], ident[:]), routed)
                c3 = act(lambda e: e.copy(cT[:], unit.ap[0:NE, :]), m)
                rows = Slot(None, sem(f"s_{name}_rows"))
                rows_stored[0] = dma(rows, combine_rows, cT[:], c3)

                outs = Ring([Slot(psum(6)), Slot(psum(7))])
                for s_ in outs.slots:
                    s_.free = [c3]

                def contribute(pair, tiles):
                    z1a, z1c, (z2, z2_ready) = Z1[2 * pair], Z1[2 * pair + 1], Z2[pair]
                    down, ready = WD[pair]
                    for i in tiles:
                        bank = outs.take()
                        tok = slice(i * P, (i + 1) * P)
                        products = [p for n, z_ in enumerate((z1a[0], z2, z1c[0])) for p in parts(
                            cut(z_.ap, slice(None), tok), cut(down.ap, slice(None), slice(n * D, (n + 1) * D)))]
                        m = mm_group(bank.ap, products, (list(bank.free), z1a[1], z1c[1], z2_ready, ready))
                        done = dve(lambda e, i=i, bank=bank: e.tensor_tensor(x[:, i, :], x[:, i, :], bank.ap, ALU.add),
                                   m, x_ready[i])
                        bank.free = [done]
                        x_ready[i] = [done]
                    if NT - 1 in tiles:
                        for s_ in (z1a[0], z1c[0], z2, down):
                            s_.free = [m]

                fetch_row(0)
                fetch_row(1)
                AHEAD = 3
                for e_ in range(NE + 2):
                    if 0 < e_ < NE - 1:
                        split_weights(e_ + 1)
                    if e_ < NE:
                        finish_first, finish_rest = hidden(e_) if e_ else first
                        if e_ == NE - 1:
                            finish_rest()
                        finish_first()
                    if e_ + 2 < NE:
                        fetch(e_ + 2)
                    if e_ >= 2 and e_ % 2 == 0:
                        contribute(e_ // 2 - 1, range(AHEAD))
                    if e_ < NE - 1:
                        finish_rest()
                    if e_ + 2 < NE:
                        fetch_row(e_ + 2)
                    if e_ >= 2 and e_ % 2 == 0:
                        contribute(e_ // 2 - 1, range(AHEAD, NT))

        ln_banks = None
        for i in range(4):
            x_written(i, x_ready[i])
        phases = [lambda: cross_attention("L0x", False), lambda: self_attention("L0a", KVH, False),
                  lambda: hadamard_ffn("L0f"), lambda: cross_attention("L1x", True),
                  lambda: self_attention("L1a", AT, True), lambda: experts("L1f")]
        for phase in phases[:last_phase]:
            phase()

        stored = Slot(None, sem("s_stored"))
        for i in range(NT):
            end = dma(stored, out[i * P:(i + 1) * P, :], x[:, i, :], x_ready[i])
        sp.quiet(None, end)

        with nc.Block() as block:
            @block.sync
            def _(eng):
                sp.emit(eng)

            @block.tensor
            def _(eng):
                pe.emit(eng)

            @block.scalar
            def _(eng):
                act.emit(eng)

            @block.vector
            def _(eng):
                dve.emit(eng)

            @block.gpsimd
            def _(eng):
                pool.emit(eng)


def constants():
    f = np.float32

    def rope(n, dim):
        inv = (f(1.0) / f(10000.0) ** (np.arange(0, dim, 2, dtype=f) / f(dim))).astype(f)
        return (np.arange(n, dtype=f)[:, None] * inv[None, :]).astype(f)

    c = {"ident": np.eye(P, dtype=f)}
    fr = np.repeat(rope(L, DC), 2, axis=1)
    sign = np.where(np.arange(DC) < DC // 2, f(-1), f(1))

    def by_key(t):
        return np.ascontiguousarray(np.stack([t[0:P], t[P:2 * P], np.broadcast_to(t[L - 1:L], (P, DC))], 1)).reshape(P, -1)

    c["kcos"] = by_key(np.cos(fr).astype(f))
    c["ksin"] = by_key((np.sin(fr) * sign).astype(f))
    fq = np.repeat(rope(S, DCQ), 2, axis=1)
    cq, sq = np.cos(fq).astype(f), np.sin(fq).astype(f)
    j = np.arange(DCQ)
    sp = sq[:, (j + DCQ // 2) % DCQ] * np.where(j < DCQ // 2, f(1), f(-1))
    c["cosq"] = np.ascontiguousarray(cq.T.reshape(QC, P, S).transpose(1, 0, 2)).reshape(P, -1).astype(f)
    c["sinq"] = np.ascontiguousarray(sp.T.reshape(QC, P, S).transpose(1, 0, 2)).reshape(P, -1).astype(f)
    fa = rope(S, DH)
    fa = np.concatenate([fa, fa], 1)
    sa = np.where(np.arange(DH) < DH // 2, f(-1), f(1))
    c["acos"] = np.tile(np.cos(fa).astype(f), (BPT, 1))
    c["asin"] = np.tile((np.sin(fa) * sa).astype(f), (BPT, 1))
    c["mask"] = np.tile(np.where(np.arange(S)[:, None] >= np.arange(S)[None, :], f(0), f(NEG)), (BPT, 1)).astype(f)
    h = np.ones((1, 1))
    while h.shape[0] < P:
        h = np.block([[h, h], [h, -h]])
    c["had"] = np.concatenate([h / np.sqrt(D), h / np.sqrt(INTER)], 1).astype(f)
    c["iota"] = np.broadcast_to(np.arange(NE, dtype=f), (P, NE)).copy()
    c["order"] = np.broadcast_to(np.arange(TOPK, 0, -1).astype(f), (P, TOPK)).copy()
    return c


def layout(i):
    f = np.float32
    c = np.ascontiguousarray
    o = {"x": i["x"].reshape(NT, BPT, S, D).transpose(0, 2, 1, 3).reshape(TOK, D), "ctx": i["ctx_512"]}

    def padded(a, rows=P):
        out = np.zeros((*a.shape[:-2], rows, a.shape[-1]), f)
        out[..., :a.shape[-2], :] = a
        return out

    def by_partition(a):
        n = a.shape[-1]
        return c(a.reshape(-1, P, n).transpose(1, 0, 2)).reshape(P, -1)

    for name, g in (("L0x", "L0_xattn_"), ("L1x", "L1_xattn_")):
        wq = i[g + "Wq"].reshape(XH, XK, D)
        kcq, qr, kr = i[g + "w_kc_q"], i[g + "W_qr"], i[g + "W_kr"]
        kr_t = padded(kr.transpose(0, 2, 1))
        wo_t = i[g + "Wo"].T.reshape(XH, XK, D)
        both = np.concatenate([i[g + "w_kc_kv"], wo_t], 2).reshape(XH // OUT_HEADS, OUT_HEADS, P, OUT_PACK)
        o[f"{name}_out"] = c(both.transpose(0, 2, 1, 3)).reshape(XH // OUT_HEADS, P, -1)
        if name == "L0x":
            parts = [wq, kcq.transpose(0, 2, 1).reshape(XH, QC, P, XK).transpose(0, 2, 1, 3).reshape(XH, P, -1),
                     qr.reshape(XH, QC, P, RR).transpose(0, 2, 1, 3).reshape(XH, P, -1)]
        else:
            qr_t = qr.transpose(0, 2, 1)
            parts = [wq.transpose(0, 2, 1).reshape(XH, KD, P, XK).transpose(0, 2, 1, 3).reshape(XH, P, -1), kcq,
                     padded(np.concatenate([qr_t, qr_t[:, :, :DCQ // 2]], 2))]
        o[f"{name}_heads"] = c(np.concatenate([*parts, kr_t], 2))

    a = "L0_attn_"
    rep = lambda w: np.repeat(w.reshape(-1, KVH, 1, DH), HPT, axis=2).reshape(w.shape[0], -1)
    o["L0a_wq"] = by_partition(i[a + "Wq"])
    o["L0a_wk"] = by_partition(rep(i[a + "Wk"]))
    o["L0a_wv"] = by_partition(i[a + "Wv"])
    o["L0a_wo"] = by_partition(i[a + "Wo"])
    o["L0a_bq"] = i[a + "bq"].reshape(1, -1)
    o["L0a_bk"] = rep(i[a + "bk"].reshape(1, -1))
    o["L0a_bv"] = i[a + "bv"].reshape(1, -1)
    o["L0a_bo"] = i[a + "bo"].reshape(1, -1)

    a = "L0_ffn_"
    o["su_ug"] = c(i[a + "SU_ug"].reshape(KD, P).T)
    o["su_dp"] = c(i[a + "SU_dp"].reshape(FC, P).T)
    o["ws_up"] = c(i[a + "Wscale_ug"][:INTER].reshape(FC, P).T)
    o["ws_gate"] = c(i[a + "Wscale_ug"][INTER:].reshape(FC, P).T)
    o["ws_down"] = i[a + "Wscale_dp"].reshape(1, -1)
    o["wdT"] = c(i[a + "W_down"].T.reshape(FC // 4, 4, P, D).transpose(0, 2, 1, 3)).reshape(FC // 4, P, -1)
    ug = np.stack([i[a + "W_up"], i[a + "W_gate"]])
    ug = ug.reshape(2, FC // 2, 2, P, KD, P).transpose(1, 5, 2, 0, 4, 3)
    o["wug"] = c(ug).reshape(FC // 2, P, -1)

    a = "L1_attn_"
    qkv = i[a + "w_qkv"]
    for n, key in enumerate(("wq", "wk", "wv")):
        o[f"L1a_{key}"] = by_partition(qkv[:, n * D:(n + 1) * D])
    o["L1a_wo"] = by_partition(i[a + "w_out"])
    for key, g in (("gq", "q_gamma"), ("gk", "k_gamma")):
        v = i[a + g].reshape(1, DH)
        o[key] = v
        o[f"{key}_roll"] = c(np.concatenate([v[:, DH // 2:], v[:, :DH // 2]], 1))

    a = "L1_ffn_"
    o["gate"] = by_partition(c(i[a + "gate_weight"].T))
    o["alpha"] = i[a + "layer_alpha"].reshape(1, 1)
    gu = i[a + "gate_up_proj"].transpose(0, 2, 1)
    dn = i[a + "down_proj"].transpose(0, 2, 1)
    experts = np.zeros((NE, P, SLOT), f)
    for e in range(NE):
        rest = [gu[e, :, P:EI], gu[e, :, EI + P:2 * EI]]
        if e % 2 == 0:
            rest = rest[::-1]
        w = np.concatenate([gu[e, :, 0:P], *rest, gu[e, :, EI:EI + P]], 1)
        experts[e, :, 0:KD * 2 * EI] = by_partition(w)
        at = KD * 2 * EI
        experts[e, :, at:at + D] = dn[e, 0:P, :]
        if e % 2 == 0:
            experts[e, :E2, at + D:] = dn[e, P:EI, :]
            experts[e, E2:, at + D:] = dn[e + 1, P:EI, :]
    o["experts"] = experts
    o.update(constants())
    return {k: np.ascontiguousarray(v) for k, v in o.items()}


def unlayout(out):
    return np.asarray(out).reshape(NT, S, BPT, D).transpose(0, 2, 1, 3).reshape(B, S, D)


def kernel(**inputs):
    import concourse.bacc as bacc
    from concourse.bass_utils import run_bass_kernel_spmd

    arrays = layout({k: np.asarray(v) for k, v in inputs.items()})
    nc = bacc.Bacc("TRN2", target_bir_lowering=False, num_devices=1)
    d = {k: nc.dram_tensor(f"in_{k}", a.shape, mybir.dt.from_np(a.dtype), kind="ExternalInput").ap()
         for k, a in arrays.items()}
    out = nc.dram_tensor("out", (TOK, D), F32, kind="ExternalOutput").ap()
    build_kernel(nc, d, out)
    result = run_bass_kernel_spmd(nc, [{f"in_{k}": a for k, a in arrays.items()}], core_ids=[0])
    return unlayout(result.results[0]["out"])
```
